# Optimizing a Trainium2 kernel written in Bass

```python
import numpy as np
import jax
import jax.numpy as jnp

def _softmax(x, axis=-1):
    return jax.nn.softmax(x, axis=axis)

def _gelu(x):
    return jax.nn.gelu(x, approximate=True)

def _silu(x):
    return jax.nn.silu(x)

def _sigmoid(x):
    return jax.nn.sigmoid(x)

def _layernorm(x, axis=-1, eps=1e-05):
    m = jnp.mean(x, axis=axis, keepdims=True)
    v = jnp.var(x, axis=axis, keepdims=True)
    return (x - m) / jnp.sqrt(v + eps)

def _scatter_add(tgt, idx, src, axis=0):
    return tgt.at[idx].add(src)

def _segment_sum(src, seg, n):
    return jax.ops.segment_sum(src, seg, n)
kernel_name = 'mk_decoder_postln_d1_seqx_r4_d4b729'

def setup_inputs(seed: int=0):
    np.random.seed(seed)
    _w = jnp.asarray

    def _rec_inputs():
        import jax
        import jax.numpy as jnp
        _rk = jax.random.key(seed)
        x = -1.394e-06 + 0.9999 * jax.random.normal(jax.random.fold_in(_rk, 1), (4, 1024, 256), jnp.float32)
        _lenS = 1024 - jax.random.randint(jax.random.fold_in(_rk, 7), (4,), 0, max(1, 1024 // 4) + 1, jnp.int32)
        _lenS2 = 77 - jax.random.randint(jax.random.fold_in(_rk, 8), (4,), 0, max(1, 77 // 4) + 1, jnp.int32)
        _ctx_1024P = jax.random.normal(jax.random.fold_in(_rk, 11), (4, 16, 256), jnp.float32)
        _ctx_1024c = jax.random.dirichlet(jax.random.fold_in(_rk, 511), 0.3 * jnp.ones((16,), jnp.float32), (4, 77))
        _ctx_1024t = jnp.einsum('bsk,bkd->bsd', _ctx_1024c, _ctx_1024P)
        _ctx_1024t = _ctx_1024t * jax.lax.rsqrt(jnp.mean(jnp.square(_ctx_1024t)) + 1e-12) * 0.953939
        ctx_1024 = 7.22013e-05 + 1.00017 * (_ctx_1024t + 0.3 * jax.random.normal(jax.random.fold_in(_rk, 611), (4, 77, 256), jnp.float32))
        _validS = jnp.arange(1024)[None, :] < _lenS[:, None]
        _validS2 = jnp.arange(77)[None, :] < _lenS2[:, None]
        _causal = jnp.tril(jnp.ones((1024, 1024), dtype=bool))
        mask_Bx1x1xS2_bk0 = jnp.logical_not(jnp.broadcast_to(_validS2[:, None, None, :], (4, 1, 1, 77)))
        return (x, ctx_1024, mask_Bx1x1xS2_bk0)
    x, ctx_1024, mask_Bx1x1xS2_bk0 = _rec_inputs()

    def _L0_attn_setup():
        import jax, jax.numpy as jnp
        import numpy as np
        B, S, D, H = (4, 512, 256, 4)
        HD = D // H

        def _reference_tuple_inner(hidden_states, Wq, Wk, Wv, Wo, bo, betas, mem, z):
            b, s, d = hidden_states.shape
            h = betas.shape[1]
            hd = d // h

            def split(x):
                return x.reshape(b, s, h, hd).transpose(0, 2, 1, 3)
            q = split(hidden_states @ Wq.T)
            k = split(hidden_states @ Wk.T)
            v = split(hidden_states @ Wv.T)
            aw = jnp.einsum('bhqd,bhkd->bhqk', q, k)
            causal = jnp.tril(jnp.ones((s, s), bool))
            aw = jnp.where(causal, aw, jnp.finfo(aw.dtype).min)
            p = jax.nn.softmax(aw, axis=-1)
            attn = jnp.einsum('bhqk,bhkd->bhqd', p, v)
            sq = jax.nn.elu(q) + 1.0
            sk = jax.nn.elu(k) + 1.0
            A_mem = jnp.einsum('bhsd,hde->bhse', sq, mem) / (jnp.einsum('bhsd,hdo->bhso', sq, z) + 1e-06)
            g = jax.nn.sigmoid(betas)
            out = g * A_mem + (1.0 - g) * attn
            delta = jnp.einsum('bhsd,hde->bhse', sk, mem) / (jnp.einsum('bhsd,hdo->bhso', sk, z) + 1e-06)
            mem_new = mem + jnp.einsum('bhsd,bhse->hde', sk, v - delta) / b
            z_new = z + jnp.mean(jnp.sum(sk, axis=2), axis=0)[:, :, None]
            out = out.transpose(0, 2, 1, 3).reshape(b, s, d)
            out = out @ Wo.T + bo
            return (out, mem_new, z_new)
        key = jax.random.key(seed)
        ks = jax.random.split(key, 6)
        s = 0.02
        return {'hidden_states': jax.random.normal(ks[0], (B, S, D), jnp.float32), 'Wq': jax.random.normal(ks[1], (D, D), jnp.float32) * s, 'Wk': jax.random.normal(ks[2], (D, D), jnp.float32) * s, 'Wv': jax.random.normal(ks[3], (D, D), jnp.float32) * s, 'Wo': jax.random.normal(ks[4], (D, D), jnp.float32) * s, 'bo': jnp.zeros((D,), jnp.float32), 'betas': jax.random.normal(ks[5], (1, H, 1, 1), jnp.float32), 'mem': jnp.zeros((H, HD, HD), jnp.float32), 'z': jnp.zeros((H, HD, 1), jnp.float32)}
    _L0_attn_all = _L0_attn_setup()
    _L0_attn_in = {k: v for k, v in _L0_attn_all.items() if k in ('Wq', 'Wk', 'Wv', 'Wo', 'bo', 'betas', 'mem', 'z')}
    del _L0_attn_all

    def _L0_xattn_setup():
        import math
        import jax, jax.numpy as jnp
        import numpy as np
        NUM_BUCKETS = 32
        MAX_DISTANCE = 128
        H = 16
        D_MODEL = 256
        D_K = D_MODEL // H

        def _relative_position_bucket(relative_position):
            nb = NUM_BUCKETS // 2
            buckets = (relative_position > 0).astype(jnp.int32) * nb
            rp = jnp.abs(relative_position)
            max_exact = nb // 2
            is_small = rp < max_exact
            rp_large = max_exact + (jnp.log(jnp.maximum(rp, 1).astype(jnp.float32) / max_exact) / math.log(MAX_DISTANCE / max_exact) * (nb - max_exact)).astype(jnp.int32)
            rp_large = jnp.minimum(rp_large, nb - 1)
            return buckets + jnp.where(is_small, rp, rp_large)
        key = jax.random.key(seed)
        ks = jax.random.split(key, 8)
        B, T_k, T_q = (4, 512, 256)
        std = D_MODEL ** (-0.5)
        inp = {'src': jax.random.normal(ks[0], (B, T_k, D_MODEL), dtype=jnp.float32), 'dst': jax.random.normal(ks[1], (B, T_q, D_MODEL), dtype=jnp.float32), 'mask': jax.random.randint(ks[2], (B, 1, 1, T_k), 0, 2).astype(bool), 'Wq': jax.random.normal(ks[3], (D_MODEL, D_MODEL), dtype=jnp.float32) * std, 'Wk': jax.random.normal(ks[4], (D_MODEL, D_MODEL), dtype=jnp.float32) * std, 'Wv': jax.random.normal(ks[5], (D_MODEL, D_MODEL), dtype=jnp.float32) * std, 'Wo': jax.random.normal(ks[6], (D_MODEL, D_MODEL), dtype=jnp.float32) * std, 'rel_bias': jax.random.normal(ks[7], (H, NUM_BUCKETS), dtype=jnp.float32) * NUM_BUCKETS ** (-0.5)}
        return inp
    _L0_xattn_all = _L0_xattn_setup()
    _L0_xattn_in = {k: v for k, v in _L0_xattn_all.items() if k in ('Wq', 'Wk', 'Wv', 'Wo', 'rel_bias')}
    del _L0_xattn_all

    def _L0_ffn_setup():
        import jax, jax.numpy as jnp
        import numpy as np
        import math
        D_MODEL = 256
        N_EXPERTS = 16
        D_FF = 1024
        CAP_FACTOR = 1.25
        MIN_CAPACITY = 4

        def _capacity(num_tokens, num_experts):
            cap = math.floor(CAP_FACTOR * num_tokens / num_experts)
            cap += cap % 2
            return max(cap, MIN_CAPACITY)

        def _top1_router(gate_logits, capacity):
            s, e = gate_logits.shape
            probs = jax.nn.softmax(gate_logits, axis=-1)
            top1 = jnp.argmax(gate_logits, axis=-1)
            mask = jax.nn.one_hot(top1, e, dtype=jnp.int32)
            ranks = jnp.cumsum(mask, axis=0) - 1
            mask = mask * (ranks < capacity).astype(jnp.int32)
            rank1 = jnp.sum(mask * ranks, axis=-1)
            ranks_oh = jax.nn.one_hot(rank1, capacity, dtype=probs.dtype)
            weight = mask.astype(probs.dtype) * probs
            combine_weights = weight[:, :, None] * ranks_oh[:, None, :]
            sec_mask = combine_weights > 0
            return (combine_weights, sec_mask)
        key = jax.random.key(seed)
        k1, k2, k3, k4 = jax.random.split(key, 4)
        x = jax.random.normal(k1, (4, 512, D_MODEL), dtype=jnp.float32)
        gate_w = jax.random.normal(k2, (N_EXPERTS, D_MODEL), dtype=jnp.float32) * math.sqrt(0.1 / D_MODEL)
        w1 = jax.random.normal(k3, (N_EXPERTS, D_MODEL, D_FF), dtype=jnp.float32) * (1.0 / math.sqrt(D_MODEL))
        w2 = jax.random.normal(k4, (N_EXPERTS, D_FF, D_MODEL), dtype=jnp.float32) * (1.0 / math.sqrt(D_FF))
        return {'x': x, 'gate_w': gate_w, 'w1': w1, 'w2': w2}
    _L0_ffn_all = _L0_ffn_setup()
    _L0_ffn_in = {k: v for k, v in _L0_ffn_all.items() if k in ('gate_w', 'w1', 'w2')}
    del _L0_ffn_all
    return {'x': x, 'ctx_1024': ctx_1024, 'mask_Bx1x1xS2_bk0': mask_Bx1x1xS2_bk0, 'L0_attn_Wq': _L0_attn_in['Wq'], 'L0_attn_Wk': _L0_attn_in['Wk'], 'L0_attn_Wv': _L0_attn_in['Wv'], 'L0_attn_Wo': _L0_attn_in['Wo'], 'L0_attn_bo': _L0_attn_in['bo'], 'L0_attn_betas': _L0_attn_in['betas'], 'L0_attn_mem': _L0_attn_in['mem'], 'L0_attn_z': _L0_attn_in['z'], 'L0_xattn_Wq': _L0_xattn_in['Wq'], 'L0_xattn_Wk': _L0_xattn_in['Wk'], 'L0_xattn_Wv': _L0_xattn_in['Wv'], 'L0_xattn_Wo': _L0_xattn_in['Wo'], 'L0_xattn_rel_bias': _L0_xattn_in['rel_bias'], 'L0_ffn_gate_w': _L0_ffn_in['gate_w'], 'L0_ffn_w1': _L0_ffn_in['w1'], 'L0_ffn_w2': _L0_ffn_in['w2']}

def reference(x, ctx_1024, mask_Bx1x1xS2_bk0, L0_attn_Wq, L0_attn_Wk, L0_attn_Wv, L0_attn_Wo, L0_attn_bo, L0_attn_betas, L0_attn_mem, L0_attn_z, L0_xattn_Wq, L0_xattn_Wk, L0_xattn_Wv, L0_xattn_Wo, L0_xattn_rel_bias, L0_ffn_gate_w, L0_ffn_w1, L0_ffn_w2):
    import jax
    import jax.numpy as jnp

    def _L0_attn_ref(hidden_states, Wq, Wk, Wv, Wo, bo, betas, mem, z):
        import jax, jax.numpy as jnp
        import numpy as np
        B, S, D, H = (4, 512, 256, 4)
        HD = D // H

        def _reference_tuple_inner(hidden_states, Wq, Wk, Wv, Wo, bo, betas, mem, z):
            b, s, d = hidden_states.shape
            h = betas.shape[1]
            hd = d // h

            def split(x):
                return x.reshape(b, s, h, hd).transpose(0, 2, 1, 3)
            q = split(hidden_states @ Wq.T)
            k = split(hidden_states @ Wk.T)
            v = split(hidden_states @ Wv.T)
            aw = jnp.einsum('bhqd,bhkd->bhqk', q, k)
            causal = jnp.tril(jnp.ones((s, s), bool))
            aw = jnp.where(causal, aw, jnp.finfo(aw.dtype).min)
            p = jax.nn.softmax(aw, axis=-1)
            attn = jnp.einsum('bhqk,bhkd->bhqd', p, v)
            sq = jax.nn.elu(q) + 1.0
            sk = jax.nn.elu(k) + 1.0
            A_mem = jnp.einsum('bhsd,hde->bhse', sq, mem) / (jnp.einsum('bhsd,hdo->bhso', sq, z) + 1e-06)
            g = jax.nn.sigmoid(betas)
            out = g * A_mem + (1.0 - g) * attn
            delta = jnp.einsum('bhsd,hde->bhse', sk, mem) / (jnp.einsum('bhsd,hdo->bhso', sk, z) + 1e-06)
            mem_new = mem + jnp.einsum('bhsd,bhse->hde', sk, v - delta) / b
            z_new = z + jnp.mean(jnp.sum(sk, axis=2), axis=0)[:, :, None]
            out = out.transpose(0, 2, 1, 3).reshape(b, s, d)
            out = out @ Wo.T + bo
            return (out, mem_new, z_new)
        return _reference_tuple_inner(hidden_states, Wq, Wk, Wv, Wo, bo, betas, mem, z)[0]

    def _L0_xattn_ref(src, dst, mask, Wq, Wk, Wv, Wo, rel_bias):
        import math
        import jax, jax.numpy as jnp
        import numpy as np
        NUM_BUCKETS = 32
        MAX_DISTANCE = 128
        H = 16
        D_MODEL = 256
        D_K = D_MODEL // H

        def _relative_position_bucket(relative_position):
            nb = NUM_BUCKETS // 2
            buckets = (relative_position > 0).astype(jnp.int32) * nb
            rp = jnp.abs(relative_position)
            max_exact = nb // 2
            is_small = rp < max_exact
            rp_large = max_exact + (jnp.log(jnp.maximum(rp, 1).astype(jnp.float32) / max_exact) / math.log(MAX_DISTANCE / max_exact) * (nb - max_exact)).astype(jnp.int32)
            rp_large = jnp.minimum(rp_large, nb - 1)
            return buckets + jnp.where(is_small, rp, rp_large)
        B, T_k, _ = src.shape
        T_q = dst.shape[1]
        q = (dst @ Wq.T).reshape(B, T_q, H, D_K)
        k = (src @ Wk.T).reshape(B, T_k, H, D_K)
        v = (src @ Wv.T).reshape(B, T_k, H, D_K)
        scores = jnp.einsum('bqhd,bkhd->bhqk', q, k)
        rel_pos = jnp.arange(T_k)[None, :] - jnp.arange(T_q)[:, None]
        rp_bucket = _relative_position_bucket(rel_pos)
        bias = rel_bias[:, rp_bucket]
        scores = scores + bias[None]
        scores = jnp.where(mask, scores, -1000000000.0)
        attn = jax.nn.softmax(scores, axis=-1)
        out = jnp.einsum('bhqk,bkhd->bqhd', attn, v).reshape(B, T_q, H * D_K)
        return out @ Wo.T

    def _L0_ffn_ref(x, gate_w, w1, w2):
        import jax, jax.numpy as jnp
        import numpy as np
        import math
        D_MODEL = 256
        N_EXPERTS = 16
        D_FF = 1024
        CAP_FACTOR = 1.25
        MIN_CAPACITY = 4

        def _capacity(num_tokens, num_experts):
            cap = math.floor(CAP_FACTOR * num_tokens / num_experts)
            cap += cap % 2
            return max(cap, MIN_CAPACITY)

        def _top1_router(gate_logits, capacity):
            s, e = gate_logits.shape
            probs = jax.nn.softmax(gate_logits, axis=-1)
            top1 = jnp.argmax(gate_logits, axis=-1)
            mask = jax.nn.one_hot(top1, e, dtype=jnp.int32)
            ranks = jnp.cumsum(mask, axis=0) - 1
            mask = mask * (ranks < capacity).astype(jnp.int32)
            rank1 = jnp.sum(mask * ranks, axis=-1)
            ranks_oh = jax.nn.one_hot(rank1, capacity, dtype=probs.dtype)
            weight = mask.astype(probs.dtype) * probs
            combine_weights = weight[:, :, None] * ranks_oh[:, None, :]
            sec_mask = combine_weights > 0
            return (combine_weights, sec_mask)
        tokens = x.reshape(-1, D_MODEL)
        s = tokens.shape[0]
        capacity = _capacity(s, N_EXPERTS)
        gate_logits = tokens.astype(jnp.float32) @ gate_w.T
        combine_weights, sec_mask = _top1_router(gate_logits, capacity)
        dispatch = jnp.einsum('sec,sd->ecd', sec_mask.astype(tokens.dtype), tokens)
        h = jax.nn.gelu(jnp.einsum('ecd,edf->ecf', dispatch, w1))
        expert_out = jnp.einsum('ecf,efd->ecd', h, w2)
        out = jnp.einsum('sec,ecd->sd', combine_weights.astype(tokens.dtype), expert_out)
        return out.reshape(x.shape)
    x = _layernorm(x + _L0_attn_ref(x, L0_attn_Wq, L0_attn_Wk, L0_attn_Wv, L0_attn_Wo, L0_attn_bo, L0_attn_betas, L0_attn_mem, L0_attn_z), axis=-1)
    x = _layernorm(x + _L0_xattn_ref(ctx_1024, x, mask_Bx1x1xS2_bk0, L0_xattn_Wq, L0_xattn_Wk, L0_xattn_Wv, L0_xattn_Wo, L0_xattn_rel_bias), axis=-1)
    x = _layernorm(x + _L0_ffn_ref(x, L0_ffn_gate_w, L0_ffn_w1, L0_ffn_w2), axis=-1)
    return x

_drawn_inputs = setup_inputs


def setup_inputs(seed=0):
    import zlib

    import numpy as np

    out = dict(_drawn_inputs(seed))
    spreads = {'L0_attn_bo': (0.0, 0.1), 'L0_attn_mem': (0.0, 0.1), 'L0_attn_z': (0.0, 0.1)}
    factors = {'L0_attn_Wk': 8.0, 'L0_attn_Wv': 8.0, 'L0_xattn_rel_bias': 6.117}
    for name, (base, spread) in spreads.items():
        noise = np.random.default_rng([zlib.crc32(name.encode()), seed]).standard_normal(out[name].shape)
        drawn = base * np.exp(spread * noise) if base else spread * noise
        out[name] = jnp.asarray(drawn.astype(out[name].dtype))
    for name, factor in factors.items():
        out[name] = (out[name] * factor).astype(out[name].dtype)
    return out
```

```python
from contextlib import ExitStack

import concourse.bass as bass
from concourse import mybir

F32 = mybir.dt.float32
F32R = mybir.dt.float32r
BF16 = mybir.dt.bfloat16
I32 = mybir.dt.int32
U8 = mybir.dt.uint8
ALU = mybir.AluOpType
ACT = mybir.ActivationFunctionType
AX_X = mybir.AxisListType.X

P = 128
B, S, D = 4, 1024, 256
NT = S // P
KD = D // P
H1, HD1 = 4, 64
H2, HD2 = 16, 16
SK, KP = 77, 78
GH = 8
GK = GH * KP
NCH = -(-GK // P)
TAIL = GK - (NCH - 1) * P
BUCKETS, MAX_DIST = 32, 128
BIAS_TILES = 2
HANKEL = BIAS_TILES * P + KP - 1
NE, DFF = 16, 1024
NTOK = B * S
TT = NTOK // P
CAP = 320
FC = DFF // P
EPS = 1e-5
NEG = -1e9
CHUNK_HEAD = [min(c * P // KP, GH - 3) for c in range(NCH)]
TOK_TILES = [(0, 128), (128, 128), (256, 64)]


def batch_steps():
    out = [("QK", t, n) for t in (2, 0, 3, 1) for n in range(2)] + [("V", p, 0) for p in range(4)]
    out += [("K2", 0, 0), ("V2", 0, 0)]
    for i in range(NT + 2):
        slot = [
            ("S", i, 0), ("T2", i - 2, 1), ("C", i - 1, 0), ("S", i, 1), ("PV2", i - 2, 0), ("T", i, 0),
            ("W", i - 1, 0), ("S", i, 2), ("C2", i - 2, 0), ("PV", i, 0), ("T", i, 1), ("N", i - 1, 0),
            ("S", i, 3), ("PV", i, 1), ("X", i - 1, 0), ("W2", i - 2, 0), ("T", i, 2), ("Q2", i - 1, 0),
            ("PV", i, 2), ("N2", i - 2, 0), ("S2", i - 1, 0), ("T", i, 3), ("X2", i - 2, 0),
            ("S2", i - 1, 1), ("PV", i, 3), ("AM", i, 0), ("G", i - 2, 0), ("T2", i - 1, 0)]
        out += [s for s in slot if 0 <= s[1] < NT]
    return out


def transpose_groups(kind, i):
    if kind == "T":
        return [(j, min(4, i + 1 - j)) for j in range(0, i + 1, 4)]
    return [(0, 4), (4, NCH - 4)]


class Plan:
    RING, SLOTS = 3, 2

    def __init__(self):
        self.steps = batch_steps()
        self.ring, self.slot, self.unit = {}, {}, {}
        used, scored, units = 0, 0, 0
        for s in self.steps:
            kind, i, h = s
            if kind in ("S", "S2"):
                self.slot[s] = (scored % self.SLOTS, scored // self.SLOTS)
                scored += 1
            elif kind in ("T", "T2"):
                for n in range(len(transpose_groups(kind, i))):
                    self.ring[s + (n,)] = (used % self.RING, used // self.RING)
                    used += 1
            elif kind not in ("PV", "N", "N2"):
                self.ring[s + (0,)] = (used % self.RING, used // self.RING)
                used += 1
            if kind == "S":
                self.unit[(i, h)] = units
                units += 1
        assert used % self.RING == 0 and scored % self.SLOTS == 0
        self.ring_n, self.slot_n = used // self.RING, scored // self.SLOTS


def on_scalar(key):
    kind, i, h, n = key
    if kind == "T":
        return n == 0 if i >= 4 else h % 2 == 0
    if kind == "T2":
        return n == 0 and h == 0
    return kind in ("V", "C", "X", "Q2", "C2")


class Marks:

    def __init__(self, sem, plan):
        self.plan = plan
        self.ring_full = [sem(f"ring_full{n}") for n in range(plan.RING)]
        self.ring_emptied = [sem(f"ring_emptied{n}") for n in range(plan.RING)]
        self.scores_full = [sem(f"scores_full{n}") for n in range(plan.SLOTS)]
        self.scores_emptied = [sem(f"scores_emptied{n}") for n in range(plan.SLOTS)]

    def full(self, key):
        n, k = self.plan.ring[key]
        return self.ring_full[n], self.plan.ring_n, k + 1

    def emptied(self, key):
        n, k = self.plan.ring[key]
        return self.ring_emptied[n], self.plan.ring_n, k + 1

    def claim(self, key):
        n, k = self.plan.ring[key]
        return self.ring_emptied[n], self.plan.ring_n, k

    def scored(self, step):
        n, k = self.plan.slot[step]
        return self.scores_full[n], self.plan.slot_n, k + 1

    def scores_read(self, step):
        n, k = self.plan.slot[step]
        return self.scores_emptied[n], self.plan.slot_n, k + 1

    def claim_scores(self, step):
        n, k = self.plan.slot[step]
        return self.scores_emptied[n], self.plan.slot_n, k

    def wait(self, eng, b, *marks):
        for one in {id(s): s for s, _, _ in marks}.values():
            rise, count = max((r, k) for s, r, k in marks if s is one)
            if count:
                eng.wait_ge(one, b * rise + count)

    def drained(self, eng, b):
        for s in self.ring_emptied:
            eng.wait_ge(s, (b + 1) * self.plan.ring_n)
        for s in self.scores_emptied:
            eng.wait_ge(s, (b + 1) * self.plan.slot_n)


def spread(t, axis, shape):
    return t.unsqueeze(axis).broadcast_to(list(shape))


def exact_products(terms):
    out = []
    for (a_hi, a_lo), (b_hi, b_lo) in terms:
        out += [(a_hi, b_hi), (a_hi, b_lo), (a_lo, b_hi)]
    return out


def accumulate(eng, out, products):
    for n, (lhs, rhs) in enumerate(products):
        mm = eng.matmul(out, lhs, rhs, start=(n == 0), stop=(n == len(products) - 1))
    return mm


def attention(nc, a, logits):
    plan = Plan()
    steps = plan.steps
    NU = NT * H1
    vecd = nc.dram_tensor("bias_vector", (H2, HANKEL), F32)
    biasd = nc.dram_tensor("bias_rows", (BIAS_TILES, P, H2, KP), F32)
    norm = {s: n for n, s in enumerate(s for s in steps if s[0] in ("W", "W2"))}
    VEC_LINKS = 4 + 4 + 1 + (2 + 2 + 1 + 2 + 1) * NT

    with ExitStack() as ctx:
        def sem(name):
            return ctx.enter_context(nc.semaphore(name))

        def sb(name, shape, dt=F32):
            return ctx.enter_context(nc.sbuf_tensor(name, list(shape), dt))

        psS = ctx.enter_context(nc.psum_tensor("score_banks", [P, 2, 2, 512], F32))
        ring = [ctx.enter_context(nc.psum_tensor(f"ring_bank{n}", [P, 512], F32)) for n in range(plan.RING)]
        psO = ctx.enter_context(nc.psum_tensor("output_bank", [P, 512], F32))

        identf, identb, causal = sb("identf_sb", [P, P]), sb("identb_sb", [P, P], BF16), sb("causal_sb", [P, P], BF16)
        causal_f = sb("causal_f", [P, P])
        w_f = sb("w_qkv", [P, KD, 3 * D])
        w_hi, w_lo = sb("w_qkv_hi", [P, KD, 3 * D], F32R), sb("w_qkv_lo", [P, KD, 3 * D], F32R)
        wo1, wq2, wk2, wv2, wo2 = (sb(n, [P, KD, D]) for n in ("wo1", "wq2", "wk2", "wv2", "wo2"))
        gw = sb("gate_w", [P, KD, NE])
        memz = sb("memz_sb", [P, 2, 2, HD1 + 1])
        betas, g_e, g_d, g, omg = (sb(n, [P, H1]) for n in ("betas_sb", "exp_beta", "one_exp_beta", "gate", "one_gate"))
        bo_f, bo_hi, bo2 = sb("bo_sb", [64, D]), sb("bo_hi", [64, D], F32R), sb("bo_rows", [64, D], F32R)
        ones2 = sb("ones2", [64, P], F32R)
        blk_k, blk_v = sb("blk_k_sb", [P, GH, KP]), sb("blk_v_sb", [P, NCH * 3, HD2 + 1])
        padneg, masku, maskf = sb("padneg_sb", [64, KP]), sb("mask_u8", [P, B, KP], U8), sb("mask_f", [P, B, KP])
        mneg, mneg_hi, mrow = sb("mneg", [64, KP]), sb("mneg_hi", [64, KP], F32R), sb("mrow", [64, KP], F32R)
        rel, reld = sb("rel_sb", [BUCKETS, 2, H2]), sb("rel_diff", [BUCKETS, H2])
        onehot, vec = sb("onehot_sb", [BUCKETS, HANKEL]), sb("bias_vec", [H2, HANKEL])
        xT, x_hi, x_lo = sb("xT_sb", [P, KD, S]), sb("xT_hi", [P, KD, S], F32R), sb("xT_lo", [P, KD, S], F32R)
        qk_hi, qk_lo = sb("qk_hi", [P, 4, S], F32R), sb("qk_lo", [P, 4, S], F32R)
        sq, esq = sb("sigma_q", [P, 2, S]), sb("exp_q", [P, 2, 512])
        V = sb("v_sb", [P, NT, D])
        xin, x1, x2 = sb("x_in", [P, NT, D]), sb("x1_sb", [P, NT, D]), sb("x2_sb", [P, NT, D])
        ctxT = sb("ctxT_sb", [P, KD, GK])
        bias = sb("bias_sb", [P, BIAS_TILES, H2, KP])
        k2m, k2 = sb("k2_masked", [P, 2, KP]), sb("k2_blocks", [P, 2, GH, KP])
        v2 = sb("v2_blocks", [P, 2, NCH * 3, HD2 + 1])
        probs, probsT = sb("probs", [P, 2, S]), sb("probsT", [P, 2, NT, P])
        p2, p2T = sb("probs2", [P, 2, GK]), sb("probs2T", [P, 2, NCH, P])
        negmax, rowsum, rrow = sb("negmax", [P, 4]), sb("rowsum", [P, 2, H1]), sb("rrow", [P, H1])
        den, rden = sb("den", [P, H1]), sb("rden", [P, H1])
        am, c1, c1T = sb("mem_part", [P, D]), sb("c1", [P, D]), sb("c1T", [P, KD, P])
        y = sb("y_sum", [P, 2, D])
        stats, mv, vpe, rstd = sb("stats", [P, 2, 6]), sb("mean_var", [P, 2, 2]), sb("var_eps", [P, 2]), sb("rstd", [P, 2])
        x1T, q2T = sb("x1T", [P, KD, P]), sb("q2T", [P, KD, P])
        max2, rden2 = sb("max2", [P, 2, GH]), sb("rden2", [P, H2])
        c2, c2T, x2T = sb("c2", [P, D]), sb("c2T", [P, KD, P]), sb("x2T", [P, KD, P])
        waiter, mhalf, eps, zero = sb("waiter", [1, 1]), sb("minus_half", [P, 1]), sb("eps", [P, 1]), sb("zero_rows", [P, D])

        m = Marks(sem, plan)
        ld_w, ld_rel, ld_c, ld_xT, ld_x, ld_ctx, ld_bias = (sem(n) for n in (
            "ld_w", "ld_rel", "ld_c", "ld_xT", "ld_x", "ld_ctx", "ld_bias"))
        st_vec, st_bias, st_zero, st_x2, x2_free = (sem(n) for n in (
            "st_vec", "st_bias", "st_zero", "st_x2", "x2_free"))
        exp_beta, w_hi_done, w_scaled, w_ready, rel_ready, vec_full, vec_ready = (sem(n) for n in (
            "exp_beta_done", "w_hi_done", "w_scaled", "w_ready", "rel_ready", "vec_full", "vec_ready"))
        consts_ready, zero_done, x_hi_done, x_split, qk_copied, sigma_done = (sem(n) for n in (
            "consts_ready", "zero_done", "x_hi_done", "x_split", "qk_copied", "sigma_done"))
        mrow_ready, bias_masked, k2_ready, negmax_ready, pv_done, o_read = (sem(n) for n in (
            "mrow_ready", "bias_masked", "k2_ready", "negmax_ready", "pv_done", "o_read"))
        c1_ready, c2_ready, x1_ready, x2_ready, p2_ready = (sem(n) for n in (
            "c1_ready", "c2_ready", "x1_ready", "x2_ready", "p2_ready"))
        stats_ready, rstd_ready, vec_done, setup_done, var_ready, pool_set = (sem(n) for n in (
            "stats_ready", "rstd_ready", "vec_done", "setup_done", "var_ready", "pool_set"))

        def scores(step):
            return psS[:, plan.slot[step][0], :, :].rearrange("p b c -> p (b c)")

        def bank(key):
            return ring[plan.ring[key][0]]

        def blocks(t, n=KD):
            return t[:, 0:n * P].rearrange("p (j q) -> p j q", q=P)

        LOADS_C = 13
        block = ctx.enter_context(nc.Block())

        @block.sync
        def _(sp):
            def load_xT(b):
                sp.dma_start(xT[:, :, :], a["xT"][b].rearrange("(k p) s -> p k s", p=P)).then_inc(ld_xT, 16)

            def load_ctx(b):
                sp.dma_start(ctxT[:, :, :], a["ctxT"][b].rearrange("(k p) s -> p k s", p=P)).then_inc(ld_ctx, 16)

            def load_x(b):
                sp.dma_start(xin[:, :, :], a["x"][b].rearrange("(t p) d -> p t d", p=P)).then_inc(ld_x, 16)

            def load_bias():
                sp.dma_start(bias[:, :, :, :], biasd.ap().rearrange("t p h k -> p t h k")).then_inc(ld_bias, 16)

            def store_x2(b):
                sp.wait_ge(x2_ready, (b + 1) * NT)
                sp.dma_start(a["x2d"][b].rearrange("(t p) d -> p t d", p=P), x2[:, :, :]).then_inc(st_x2, 16)
                sp.wait_ge(st_x2, (b + 1) * 16)
                sp.sem_inc(x2_free, 1)

            for n, name in enumerate(("WqT", "WkT", "WvT")):
                sp.dma_start(w_f[:, :, n * D:(n + 1) * D], a[name].rearrange("(k p) n -> p k n", p=P)).then_inc(ld_w, 16)
            sp.dma_start(betas[:, :], a["betas"]).then_inc(ld_w, 16)
            sp.dma_start(memz[:, :, :, :], a["memz"]).then_inc(ld_w, 16)
            load_xT(0)
            sp.dma_start(rel[:, :, :], a["rel"]).then_inc(ld_rel, 16)
            sp.dma_start(onehot[:, :], a["onehot"]).then_inc(ld_rel, 16)
            for t, name in ((identf, "identf"), (causal_f, "causal"), (masku, "mask"),
                            (padneg, "padneg"), (blk_k, "blk_k"), (blk_v, "blk_v"), (bo_f, "bo")):
                sp.dma_start(t[:], a[name]).then_inc(ld_c, 16)
            for t, name in ((wk2, "Wk2T"), (wv2, "Wv2T"), (wo1, "Wo1T"), (wq2, "Wq2T"), (wo2, "Wo2T"), (gw, "gateT")):
                sp.dma_start(t[:, :, :], a[name].rearrange("(k p) n -> p k n", p=P)).then_inc(ld_c, 16)
            load_ctx(0)
            load_x(0)
            sp.wait_ge(vec_ready, 1)
            sp.dma_start(vecd.ap(), vec[:, :]).then_inc(st_vec, 16)
            sp.wait_ge(st_vec, 16)
            for t in range(BIAS_TILES):
                hankel = bass.AP(vecd, t * P, [[1, P], [HANKEL, H2], [1, KP]])
                sp.dma_start(biasd.ap()[t], hankel).then_inc(st_bias, 16)
            sp.wait_ge(st_bias, 16 * BIAS_TILES)
            load_bias()
            sp.wait_ge(zero_done, 1)
            rows = a["xd"].rearrange("(n p r) d -> n p r d", p=P, r=4)
            for n in range(NE * CAP // (4 * P)):
                sp.dma_start(rows[n], zero[:, :].unsqueeze(1).broadcast_to([P, 4, D])).then_inc(st_zero, 16)
            sp.sem_inc(x2_free, 1)
            with sp.Fori(0, B - 1) as b:
                sp.wait_ge(x_split, (b + 1) * 2)
                load_xT(b + 1)
                m.wait(sp, b, m.emptied(("V2", 0, 0, 0)))
                load_ctx(b + 1)
                m.wait(sp, b, m.full(("T2", BIAS_TILES - 1, 1, 0)))
                load_bias()
                m.wait(sp, b, m.emptied(("W", NT - 1, 0, 0)))
                load_x(b + 1)
                store_x2(b)
            store_x2(B - 1)
            sp.wait_ge(st_zero, 16 * (NE * CAP // (4 * P)))

        @block.gpsimd
        def _(pool):
            nc.gpsimd.memset(mhalf[:, :], -0.5).then_inc(pool_set, 1)
            nc.gpsimd.memset(eps[:, :], EPS).then_inc(pool_set, 1)
            pool.wait_ge(pool_set, 2)
            pool.wait_ge(consts_ready, 1)
            with pool.Fori(0, B) as b:
                pool.wait_ge(ld_bias, (b + 1) * 16)
                for t in range(BIAS_TILES):
                    mask = maskf[:, bass.ds(b, 1), :].broadcast_to([P, H2, KP])
                    nc.gpsimd.tensor_tensor(bias[:, t], bias[:, t], mask, ALU.mult).then_inc(bias_masked, 1)
                for s, n in norm.items():
                    w = int(s[0] == "W2")
                    pool.wait_ge(stats_ready, b * len(norm) + n + 1)
                    nc.gpsimd.tensor_tensor(vpe[:, w:w + 1], mv[:, w, 1:2], eps[:, :], ALU.add).then_inc(var_ready, 1)
                    pool.wait_ge(var_ready, b * len(norm) + n + 1)
                    nc.gpsimd.tensor_tensor(rstd[:, w:w + 1], vpe[:, w:w + 1], mhalf[:, :], ALU.pow).then_inc(rstd_ready, 1)

        @block.scalar
        def _(act):
            act.wait_ge(ld_w, 80)
            nc.scalar.activation(g_e[:, :], betas[:, :], ACT.Exp, scale=-1.0).then_inc(exp_beta, 1)
            act.wait_ge(w_scaled, KD)
            nc.scalar.copy(w_hi[:, :, :], w_f[:, :, :]).then_inc(w_hi_done, 1)
            with act.Fori(0, B) as b:
                copied, queries, s2 = 0, 0, 0
                act.wait_ge(ld_xT, (b + 1) * 16)
                for n in range(2):
                    cols = slice(n * 512, (n + 1) * 512)
                    nc.scalar.copy(x_hi[:, :, cols], xT[:, :, cols]).then_inc(x_hi_done, 1)
                for s in steps:
                    kind, i, h = s
                    if kind == "QK":
                        cols = slice(h * 512, (h + 1) * 512)
                        m.wait(act, b, m.full(s + (0,)))
                        if i < 2:
                            if queries >= 2:
                                act.wait_ge(sigma_done, b * 4 + queries - 1)
                            nc.scalar.activation(esq[:, h, :], bank(s + (0,))[:, :], ACT.Exp).then_inc(qk_copied, 1)
                            queries += 1
                        nc.scalar.copy(qk_hi[:, i, cols], bank(s + (0,))[:, :]).then_inc(qk_copied, 1)
                    elif kind == "S":
                        u, nk = plan.unit[(i, h)], (i + 1) * P
                        act.wait_ge(negmax_ready, b * NU + u + 1)
                        if u >= 2:
                            was = divmod(u - 2, H1)
                            m.wait(act, b, m.full(("T",) + was + (len(transpose_groups("T", was[0])) - 1,)))
                        nc.scalar.activation(probs[:, u % 2, 0:nk], scores(s)[:, 0:nk], ACT.Exp,
                                             bias=negmax[:, u % 4:u % 4 + 1],
                                             accum_out=rowsum[:, i % 2, h:h + 1]).then_inc(m.scores_emptied[plan.slot[s][0]], 1)
                    elif kind == "S2":
                        m.wait(act, b, m.scores_read(s))
                        nc.scalar.activation(p2[:, h, :], p2[:, h, :], ACT.Exp).then_inc(p2_ready, 1)
                    for key in plan.ring:
                        if key[:3] != s or not on_scalar(key):
                            continue
                        need = [m.full(key)]
                        full, done = bank(key), m.ring_emptied[plan.ring[key][0]]
                        if kind == "V":
                            m.wait(act, b, *need)
                            nc.scalar.copy(V[:, 2 * i:2 * i + 2, :],
                                           full[:, :].rearrange("p (t d) -> p t d", t=2)).then_inc(done, 1)
                        elif kind == "T":
                            u = plan.unit[(i, h)]
                            j, n = transpose_groups(kind, i)[key[3]]
                            m.wait(act, b, *need)
                            if u >= 2:
                                act.wait_ge(pv_done, b * NU + u - 1)
                            nc.scalar.copy(probsT[:, u % 2, j:j + n, :], blocks(full, n)).then_inc(done, 1)
                        elif kind == "T2":
                            j, n = transpose_groups(kind, i)[key[3]]
                            if i:
                                need.append(m.full(("PV2", i - 1, 0, 0)))
                            m.wait(act, b, *need)
                            nc.scalar.copy(p2T[:, h, j:j + n, :], blocks(full, n)).then_inc(done, 1)
                        else:
                            dst, user = {"C": (c1T, "W"), "X": (x1T, "Q2"), "C2": (c2T, "W2"), "Q2": (q2T, "S2")}[kind]
                            if i:
                                need.append(m.scored(("S2", i - 1, 1)) if user == "S2" else m.full((user, i - 1, 0, 0)))
                            m.wait(act, b, *need)
                            nc.scalar.copy(dst[:, :, :], blocks(full)).then_inc(done, 1)
                m.drained(act, b)

        @block.vector
        def _(dve):
            links = 0

            def link(ins):
                nonlocal links
                links += 1
                ins.then_inc(setup_done, 1)
                dve.wait_ge(setup_done, links)

            dve.wait_ge(ld_rel, 32)
            nc.vector.tensor_tensor(reld[:, :], rel[:, 0, :], rel[:, 1, :], ALU.subtract).then_inc(rel_ready, 1)
            nc.vector.memset(zero[:, :], 0.0).then_inc(zero_done, 1)
            dve.wait_ge(exp_beta, 1)
            link(nc.vector.tensor_scalar(g_d[:, :], g_e[:, :], 1.0, None, ALU.add))
            link(nc.vector.reciprocal(g[:, :], g_d[:, :]))
            link(nc.vector.tensor_tensor(omg[:, :], g_e[:, :], g[:, :], ALU.mult))
            for k in range(KD):
                wv = w_f[:, k, 2 * D:3 * D].rearrange("p (h d) -> p h d", h=H1)
                nc.vector.tensor_tensor(wv, wv, spread(omg[:, :], 2, [P, H1, HD1]), ALU.mult).then_inc(w_scaled, 1)
            for n in range(2):
                mem = memz[:, n, :, 0:HD1]
                nc.vector.tensor_tensor(mem, mem, spread(g[:, 2 * n:2 * n + 2], 2, [P, 2, HD1]), ALU.mult).then_inc(w_ready, 1)
            dve.wait_ge(w_hi_done, 1)
            nc.vector.tensor_tensor(w_lo[:, :, :], w_f[:, :, :], w_hi[:, :, :].bitcast(F32), ALU.subtract).then_inc(w_ready, 1)
            dve.wait_ge(vec_full, 1)
            nc.vector.tensor_copy(vec[:, :], psO[0:H2, 0:HANKEL]).then_inc(vec_ready, 1)
            dve.wait_ge(ld_c, 16 * LOADS_C)
            link(nc.vector.memset(ones2[:, :].bitcast(F32), 1.0))
            link(nc.vector.memset(bo2[:, :].bitcast(F32), 0.0))
            link(nc.vector.tensor_copy(identb[:, :], identf[:, :]))
            link(nc.vector.tensor_copy(causal[:, :], causal_f[:, :]))
            link(nc.vector.memset(mrow[:, :].bitcast(F32), 0.0))
            link(nc.vector.tensor_copy(bo_hi[:, :], bo_f[:, :]))
            link(nc.vector.tensor_copy(bo2[0:1, :], bo_f[0:1, :]))
            link(nc.vector.tensor_tensor(bo2[32:33, :], bo_f[32:33, :], bo_hi[32:33, :].bitcast(F32), ALU.subtract))
            for n in range(2):
                link(nc.vector.tensor_copy(v2[:, n, :, HD2:HD2 + 1], blk_v[:, :, HD2:HD2 + 1]))
            nc.vector.tensor_copy(maskf[:, :, :], masku[:, :, :]).then_inc(consts_ready, 1)
            dve.wait_ge(consts_ready, 1)
            with dve.Fori(0, B) as b:
                own, copied, queries = 0, 0, 0

                def linked(ins):
                    nonlocal own
                    own += 1
                    ins.then_inc(vec_done, 1)
                    dve.wait_ge(vec_done, b * VEC_LINKS + own)

                for n in range(2):
                    cols = slice(n * 512, (n + 1) * 512)
                    dve.wait_ge(x_hi_done, b * 2 + n + 1)
                    nc.vector.tensor_tensor(x_lo[:, :, cols], xT[:, :, cols], x_hi[:, :, cols].bitcast(F32),
                                            ALU.subtract).then_inc(x_split, 1)
                mask = maskf[:, bass.ds(b, 1), :].rearrange("p a k -> p (a k)")
                linked(nc.vector.tensor_scalar(mneg[:, :], mask[0:64, :], 1.0, -NEG, ALU.subtract, ALU.mult))
                linked(nc.vector.tensor_tensor(mneg[:, :], mneg[:, :], padneg[:, :], ALU.add))
                linked(nc.vector.tensor_copy(mneg_hi[:, :], mneg[:, :]))
                linked(nc.vector.tensor_copy(mrow[0:1, :], mneg[0:1, :]))
                nc.vector.tensor_tensor(mrow[32:33, :], mneg[32:33, :], mneg_hi[32:33, :].bitcast(F32),
                                        ALU.subtract).then_inc(mrow_ready, 1)
                for s in steps:
                    kind, i, h = s
                    key = s + (0,)
                    if key in plan.ring:
                        full, done = bank(key), m.ring_emptied[plan.ring[key][0]]
                    if kind == "QK":
                        cols = slice(h * 512, (h + 1) * 512)
                        copied += 2 if i < 2 else 1
                        dve.wait_ge(qk_copied, b * 12 + copied)
                        if i < 2:
                            linked(nc.vector.tensor_scalar(sq[:, i, cols], full[:, :], 0.0, None, ALU.max))
                        nc.vector.tensor_tensor(qk_lo[:, i, cols], full[:, :], qk_hi[:, i, cols].bitcast(F32),
                                                ALU.subtract).then_inc(done, 1)
                        if i < 2:
                            nc.vector.scalar_tensor_tensor(out=sq[:, i, cols], in0=esq[:, h, :], scalar=1.0,
                                                           in1=sq[:, i, cols], op0=ALU.min, op1=ALU.add).then_inc(sigma_done, 1)
                    elif kind == "K2":
                        m.wait(dve, b, m.full(key))
                        nc.vector.tensor_tensor(k2m[:, :, :], full[:, 0:2 * KP].rearrange("p (g k) -> p g k", g=2),
                                                maskf[:, bass.ds(b, 1), :].broadcast_to([P, 2, KP]), ALU.mult).then_inc(done, 1)
                        m.wait(dve, b, m.emptied(key))
                        for n in range(2):
                            nc.vector.tensor_tensor(k2[:, n, :, :], spread(k2m[:, n, :], 1, [P, GH, KP]),
                                                    blk_k[:, :, :], ALU.mult).then_inc(k2_ready, 1)
                    elif kind == "V2":
                        m.wait(dve, b, m.full(key))
                        src = full[:, 0:2 * NCH * 3 * HD2].rearrange("p (g c d) -> p g c d", g=2, d=HD2)
                        for rows, lo, hi in ((P, 0, 3 * (NCH - 1)), (TAIL, 3 * (NCH - 1), 3 * NCH)):
                            ins = nc.vector.tensor_tensor(
                                v2[0:rows, :, lo:hi, 0:HD2], src[0:rows, :, lo:hi, :],
                                spread(blk_v[0:rows, lo:hi, 0:HD2], 1, [rows, 2, hi - lo, HD2]), ALU.mult)
                            if lo == 0:
                                linked(ins)
                        ins.then_inc(done, 1)
                    elif kind == "S":
                        u = plan.unit[(i, h)]
                        m.wait(dve, b, m.scored(s))
                        nc.vector.tensor_reduce(negmax[:, u % 4:u % 4 + 1], scores(s)[:, 0:(i + 1) * P], AX_X,
                                                ALU.max, negate=True).then_inc(negmax_ready, 1)
                    elif kind == "S2":
                        m.wait(dve, b, m.scored(s))
                        sc = psS[:, plan.slot[s][0], :, 0:4 * KP].rearrange("p b (h k) -> p b h k", h=4)
                        mx = max2[:, h, :].rearrange("p (b h) -> p b h", b=2)
                        linked(nc.vector.tensor_reduce(mx, sc, AX_X, ALU.max))
                        if i:
                            m.wait(dve, b, m.full(("T2", i - 1, h, 1)))
                        nc.vector.tensor_tensor(
                            p2[:, h, :].rearrange("p (b h k) -> p b h k", b=2, h=4), sc,
                            spread(mx, 3, [P, 2, 4, KP]), ALU.subtract).then_inc(m.scores_emptied[plan.slot[s][0]], 1)
                    elif kind == "AM":
                        m.wait(dve, b, m.full(key))
                        src = full[:, 0:H1 * (HD1 + 1)].rearrange("p (h e) -> p h e", h=H1)
                        linked(nc.vector.tensor_scalar(den[:, :], src[:, :, HD1], 1e-6, None, ALU.add))
                        linked(nc.vector.reciprocal(rden[:, :], den[:, :]))
                        nc.vector.tensor_tensor(am[:, :].rearrange("p (h d) -> p h d", h=H1), src[:, :, 0:HD1],
                                                spread(rden[:, :], 2, [P, H1, HD1]), ALU.mult).then_inc(done, 1)
                    elif kind == "C":
                        dve.wait_ge(pv_done, b * NU + plan.unit[(i, H1 - 1)] + 1)
                        linked(nc.vector.reciprocal(rrow[:, :], rowsum[:, i % 2, :]))
                        if i:
                            m.wait(dve, b, m.full(("C", i - 1, 0, 0)))
                        nc.vector.tensor_tensor(c1[:, :].rearrange("p (h d) -> p h d", h=H1),
                                                psO[:, 0:D].rearrange("p (h d) -> p h d", h=H1),
                                                spread(rrow[:, :], 2, [P, H1, HD1]), ALU.mult).then_inc(o_read, 1)
                        dve.wait_ge(o_read, b * NT + i + 1)
                        m.wait(dve, b, m.emptied(("AM", i, 0, 0)))
                        nc.vector.tensor_tensor(c1[:, :], c1[:, :], am[:, :], ALU.add).then_inc(c1_ready, 1)
                    elif kind in ("W", "W2"):
                        w = int(kind == "W2")
                        m.wait(dve, b, m.full(key))
                        if s == ("W", 0, 0):
                            dve.wait_ge(ld_x, (b + 1) * 16)
                        nc.vector.tensor_tensor(y[:, w, :], full[:, 0:D], (x1 if w else xin)[:, i, :], ALU.add).then_inc(done, 1)
                        m.wait(dve, b, m.emptied(key))
                        linked(nc.vector.bn_stats(stats[:, w, :], y[:, w, :]))
                        nc.vector.memset(waiter[:, :], 0.0)
                        nc.vector.bn_aggr(mv[:, w, :], stats[:, w, :]).then_inc(stats_ready, 1)
                    elif kind in ("N", "N2"):
                        w = int(kind == "N2")
                        dve.wait_ge(rstd_ready, b * len(norm) + norm[("W2" if w else "W", i, 0)] + 1)
                        if s == ("N2", 0, 0):
                            dve.wait_ge(x2_free, b + 1)
                        nc.vector.tensor_scalar((x2 if w else x1)[:, i, :], y[:, w, :], mv[:, w, 0:1], rstd[:, w:w + 1],
                                                ALU.subtract, ALU.mult).then_inc(x2_ready if w else x1_ready, 1)
                        if not w:
                            dve.wait_ge(x1_ready, b * NT + i + 1)
                    elif kind == "PV2":
                        m.wait(dve, b, m.full(key))
                        src = full[:, 0:H2 * (HD2 + 1)].rearrange("p (h e) -> p h e", h=H2)
                        linked(nc.vector.reciprocal(rden2[:, :], src[:, :, HD2]))
                        if i:
                            m.wait(dve, b, m.full(("C2", i - 1, 0, 0)))
                        nc.vector.tensor_tensor(c2[:, :].rearrange("p (h d) -> p h d", h=H2), src[:, :, 0:HD2],
                                                spread(rden2[:, :], 2, [P, H2, HD2]), ALU.mult).then_inc(done, 1)
                    elif kind == "X2":
                        m.wait(dve, b, m.full(key), *([m.full(("G", i - 1, 0, 0))] if i else []))
                        nc.vector.tensor_copy(x2T[:, :, :], blocks(full)).then_inc(done, 1)
                    elif kind == "G":
                        m.wait(dve, b, m.full(key))
                        at = logits[:, bass.ds(b * NT + i, 1), :].rearrange("p a e -> p (a e)")
                        nc.vector.tensor_copy(at, full[:, 0:NE]).then_inc(done, 1)
                    elif kind in ("T", "T2"):
                        for n3, (j, n) in enumerate(transpose_groups(kind, i)):
                            key = s + (n3,)
                            if on_scalar(key):
                                continue
                            m.wait(dve, b, m.full(key), *([m.full(("PV2", i - 1, 0, 0))] if kind == "T2" and i else []))
                            full, done = bank(key), m.ring_emptied[plan.ring[key][0]]
                            if kind == "T":
                                u = plan.unit[(i, h)]
                                if u >= 2:
                                    dve.wait_ge(pv_done, b * NU + u - 1)
                                nc.vector.tensor_copy(probsT[:, u % 2, j:j + n, :], blocks(full, n)).then_inc(done, 1)
                            else:
                                rows = TAIL if j else P
                                nc.vector.tensor_copy(p2T[0:rows, h, j:j + n, :], blocks(full, n)[0:rows]).then_inc(done, 1)
                assert own == VEC_LINKS, own
                m.drained(dve, b)

        @block.tensor
        def _(pe):
            pe.wait_ge(ld_rel, 32)
            pe.wait_ge(rel_ready, 1)
            nc.tensor.matmul(psO[0:H2, 0:HANKEL], reld[:, :], onehot[:, :], start=True, stop=True).then_inc(vec_full, 1)
            pe.wait_ge(w_ready, 3)
            pe.wait_ge(vec_ready, 1)
            pe.wait_ge(ld_c, 16 * LOADS_C)
            pe.wait_ge(consts_ready, 1)
            with pe.Fori(0, B) as b:
                for s in steps:
                    kind, i, h = s
                    key = s + (0,)
                    need = []
                    if key in plan.ring and kind not in ("T", "T2"):
                        need = [m.claim(key)]
                        full, done = bank(key), m.ring_full[plan.ring[key][0]]
                    q = slice(i * P, (i + 1) * P)
                    if kind == "QK":
                        m.wait(pe, b, *need)
                        pe.wait_ge(x_split, b * 2 + h + 1)
                        w, cols = slice(i * P, (i + 1) * P), slice(h * 512, (h + 1) * 512)
                        accumulate(pe, full[:, :], exact_products(
                            [((w_hi[:, k, w], w_lo[:, k, w]), (x_hi[:, k, cols], x_lo[:, k, cols])) for k in range(KD)]
                        )).then_inc(done, 1)
                    elif kind == "V":
                        m.wait(pe, b, *need)
                        w = slice(2 * D, 3 * D)
                        for n in range(2):
                            t = slice((2 * i + n) * P, (2 * i + n + 1) * P)
                            mm = accumulate(pe, full[:, n * D:(n + 1) * D], exact_products(
                                [((x_hi[:, k, t], x_lo[:, k, t]), (w_hi[:, k, w], w_lo[:, k, w])) for k in range(KD)]))
                        mm.then_inc(done, 1)
                    elif kind == "K2":
                        m.wait(pe, b, *need)
                        pe.wait_ge(ld_ctx, (b + 1) * 16)
                        for n in range(2):
                            mm = accumulate(pe, full[:, n * KP:(n + 1) * KP], [
                                (wk2[:, k, n * P:(n + 1) * P], ctxT[:, k, 0:KP]) for k in range(KD)])
                        mm.then_inc(done, 1)
                    elif kind == "V2":
                        m.wait(pe, b, *need)
                        for n in range(2):
                            for c in range(NCH):
                                rows, at = min(P, GK - c * P), (n * NCH + c) * 3 * HD2
                                w = (n * GH + CHUNK_HEAD[c]) * HD2
                                mm = accumulate(pe, full[0:rows, at:at + 3 * HD2], [
                                    (ctxT[:, k, c * P:c * P + rows], wv2[:, k, w:w + 3 * HD2]) for k in range(KD)])
                        mm.then_inc(done, 1)
                    elif kind == "S":
                        if (i, h) == (0, 0):
                            need = [m.emptied(k) for k in plan.ring if k[0] == "QK"]
                        m.wait(pe, b, m.claim_scores(s), *need)
                        r, t, nk = slice(h % 2 * HD1, h % 2 * HD1 + HD1), h // 2, (i + 1) * P
                        for c in range(0, nk, 512):
                            cols = slice(c, min(c + 512, nk))
                            last = cols.stop == nk
                            products = exact_products([((qk_hi[r, t, q], qk_lo[r, t, q]),
                                                        (qk_hi[r, 2 + t, cols], qk_lo[r, 2 + t, cols]))])
                            for n, (lhs, rhs) in enumerate(products):
                                mm = pe.matmul(scores(s)[:, cols], lhs, rhs, start=(n == 0),
                                               stop=(n == len(products) - 1 and not last))
                        pe.matmul(scores(s)[:, i * P:nk], identb[:, :], causal[:, :], start=False,
                                  stop=True).then_inc(m.scores_full[plan.slot[s][0]], 1)
                    elif kind == "T":
                        m.wait(pe, b, m.scores_read(("S", i, h)))
                        u = plan.unit[(i, h)]
                        for n3, (j, n) in enumerate(transpose_groups(kind, i)):
                            m.wait(pe, b, m.claim(s + (n3,)))
                            for jj in range(j, j + n):
                                mm = pe.transpose(bank(s + (n3,))[:, (jj - j) * P:(jj - j + 1) * P],
                                                  probs[:, u % 2, jj * P:(jj + 1) * P], identf[:, :])
                            mm.then_inc(m.ring_full[plan.ring[s + (n3,)][0]], 1)
                    elif kind == "PV":
                        u = plan.unit[(i, h)]
                        if (i, h) == (0, 0):
                            need = [m.emptied(("V", p, 0, 0)) for p in range(4)]
                        m.wait(pe, b, *need, *[m.emptied(("T", i, h, n3)) for n3 in range(len(transpose_groups("T", i)))])
                        if h == 0 and i:
                            pe.wait_ge(o_read, b * NT + i)
                        d = slice(h * HD1, (h + 1) * HD1)
                        accumulate(pe, psO[:, d], [(probsT[:, u % 2, j, :], V[:, j, d]) for j in range(i + 1)]).then_inc(pv_done, 1)
                    elif kind == "AM":
                        m.wait(pe, b, *need)
                        if i == 0:
                            pe.wait_ge(sigma_done, (b + 1) * 4)
                        for n in range(2):
                            w = 2 * (HD1 + 1)
                            mm = pe.matmul(full[:, n * w:(n + 1) * w], sq[:, n, q], memz[:, n, :, :], start=True, stop=True)
                        mm.then_inc(done, 1)
                    elif kind in ("C", "X", "C2", "X2"):
                        src, ready = {"C": (c1, c1_ready), "X": (x1, x1_ready), "C2": (c2, None), "X2": (x2, x2_ready)}[kind]
                        if ready is None:
                            need.append(m.emptied(("PV2", i, 0, 0)))
                        m.wait(pe, b, *need)
                        if ready is not None:
                            pe.wait_ge(ready, b * NT + i + 1)
                        for k in range(KD):
                            part = src[:, i, k * P:(k + 1) * P] if kind in ("X", "X2") else src[:, k * P:(k + 1) * P]
                            mm = pe.transpose(full[:, k * P:(k + 1) * P], part, identf[:, :])
                        mm.then_inc(done, 1)
                    elif kind in ("W", "W2", "G"):
                        before, lhs, rhs = {"W": ("C", c1T, wo1), "W2": ("C2", c2T, wo2), "G": ("X2", x2T, gw)}[kind]
                        m.wait(pe, b, *need, m.emptied((before, i, 0, 0)))
                        products = [(lhs[:, k, :], rhs[:, k, :]) for k in range(KD)]
                        if kind == "W":
                            products.append((ones2[:, :], bo2[:, :]))
                        accumulate(pe, full[:, 0:NE if kind == "G" else D], products).then_inc(done, 1)
                    elif kind == "Q2":
                        m.wait(pe, b, *need, m.emptied(("X", i, 0, 0)))
                        for n in range(2):
                            mm = accumulate(pe, full[:, n * P:(n + 1) * P], [
                                (wq2[:, k, n * P:(n + 1) * P], x1T[:, k, :]) for k in range(KD)])
                        mm.then_inc(done, 1)
                    elif kind == "S2":
                        if (i, h) == (0, 0):
                            pe.wait_ge(k2_ready, (b + 1) * 2)
                            pe.wait_ge(mrow_ready, b + 1)
                        m.wait(pe, b, m.emptied(("Q2", i, 0, 0)), m.claim_scores(s))
                        if i < BIAS_TILES:
                            pe.wait_ge(bias_masked, b * BIAS_TILES + i + 1)
                        for n in range(2):
                            h4 = slice(4 * n, 4 * n + 4)
                            products = [(q2T[:, h, :], k2[:, h, h4, :])]
                            if i < BIAS_TILES:
                                products.append((identf[:, :], bias[:, i, h * GH + 4 * n:h * GH + 4 * n + 4, :]))
                            products.append((ones2[:, :], spread(mrow[:, :], 1, [64, 4, KP])))
                            mm = accumulate(pe, psS[:, plan.slot[s][0], n, 0:4 * KP], products)
                        mm.then_inc(m.scores_full[plan.slot[s][0]], 1)
                    elif kind == "T2":
                        pe.wait_ge(p2_ready, b * 2 * NT + 2 * i + h + 1)
                        for n3, (j, n) in enumerate(transpose_groups(kind, i)):
                            m.wait(pe, b, m.claim(s + (n3,)))
                            for c in range(j, j + n):
                                rows = min(P, GK - c * P)
                                mm = pe.transpose(bank(s + (n3,))[0:rows, (c - j) * P:(c - j + 1) * P],
                                                  p2[:, h, c * P:c * P + rows], identf[:, :])
                            mm.then_inc(m.ring_full[plan.ring[s + (n3,)][0]], 1)
                    elif kind == "PV2":
                        m.wait(pe, b, *need, *[m.emptied(("T2", i, n, n3)) for n in range(2) for n3 in range(2)])
                        for n in range(2):
                            for c in range(NCH):
                                rows, at = min(P, GK - c * P), (n * GH + CHUNK_HEAD[c]) * (HD2 + 1)
                                mm = pe.matmul(full[:, at:at + 3 * (HD2 + 1)], p2T[0:rows, n, c, :],
                                               v2[0:rows, n, 3 * c:3 * c + 3, :], start=(n == 0 and c == 0),
                                               stop=(n == 1 and c == NCH - 1), skip_group_check=True)
                        mm.then_inc(done, 1)
                m.drained(pe, b)


def router(nc, a, logits, x2r, weight, slot_g):
    with ExitStack() as ctx:
        def sem(name):
            return ctx.enter_context(nc.semaphore(name))

        def sb(name, shape, dt=F32):
            return ctx.enter_context(nc.sbuf_tensor(name, list(shape), dt))

        before_f = sb("before_f", [P, P])
        before, ones, iota = sb("before_sb", [P, P], BF16), sb("ones_sb", [P, P], BF16), sb("iota_sb", [P, NE])
        top, total, first, rank, keep, base, prob = (sb(n, [P, TT]) for n in (
            "top", "total", "first", "rank", "keep", "base", "prob"))
        shifted, ex, cand, picked = (sb(n, [P, TT, NE]) for n in ("shifted", "exp_l", "cand", "picked"))
        chosen = sb("chosen", [P, TT, NE], BF16)
        slot_s = sb("slot_s", [P, TT], I32)
        psR = ctx.enter_context(nc.psum_tensor("rank_bank", [P, TT, NE], F32))
        ld_c, ld_x2, shifted_ready, exp_ready, chosen_ready, ranked, slots_ready, sent, linked, order_ready = (sem(n) for n in (
            "r_ld_c", "r_ld_x2", "shifted_ready", "exp_ready", "chosen_ready", "ranked", "slots_ready", "rows_sent",
            "router_linked", "order_ready"))
        block = ctx.enter_context(nc.Block())

        @block.sync
        def _(sp):
            for t, name in ((before_f, "before"), (iota, "iota")):
                sp.dma_start(t[:, :], a[name]).then_inc(ld_c, 16)
            for b in range(B):
                sp.dma_start(x2r[:, b * NT:(b + 1) * NT, :],
                             a["x2d"][b].rearrange("(t p) d -> p t d", p=P)).then_inc(ld_x2, 16)

        @block.vector
        def _(dve):
            links = 0

            def link(ins):
                nonlocal links
                links += 1
                ins.then_inc(linked, 1)
                dve.wait_ge(linked, links)

            nc.vector.memset(ones[:, :], 1.0).then_inc(order_ready, 1)
            L = logits[:, :, :]
            wide = [P, TT, NE]
            link(nc.vector.tensor_reduce(top[:, :], L, AX_X, ALU.max))
            nc.vector.tensor_tensor(shifted[:, :, :], L, spread(top[:, :], 2, wide), ALU.subtract).then_inc(shifted_ready, 1)
            link(nc.vector.tensor_tensor(picked[:, :, :], L, spread(top[:, :], 2, wide), ALU.is_ge))
            dve.wait_ge(ld_c, 32)
            link(nc.vector.scalar_tensor_tensor(out=cand[:, :, :], in0=picked[:, :, :], scalar=-float(NE),
                                                in1=spread(iota[:, :], 1, wide), op0=ALU.mult, op1=ALU.add))
            link(nc.vector.tensor_reduce(first[:, :], cand[:, :, :], AX_X, ALU.min))
            nc.vector.tensor_tensor(chosen[:, :, :], cand[:, :, :], spread(first[:, :], 2, wide),
                                    ALU.is_equal).then_inc(chosen_ready, 1)
            nc.vector.tensor_copy(before[:, :], before_f[:, :]).then_inc(order_ready, 1)
            dve.wait_ge(exp_ready, 1)
            link(nc.vector.tensor_reduce(total[:, :], ex[:, :, :], AX_X, ALU.add))
            link(nc.vector.reciprocal(prob[:, :], total[:, :]))
            dve.wait_ge(ranked, 1)
            dve.wait_ge(chosen_ready, 1)
            link(nc.vector.tensor_tensor(picked[:, :, :], psR[:, :, :], chosen[:, :, :], ALU.mult))
            link(nc.vector.tensor_reduce(rank[:, :], picked[:, :, :], AX_X, ALU.add))
            link(nc.vector.tensor_scalar(keep[:, :], rank[:, :], float(CAP), None, ALU.is_lt))
            link(nc.vector.tensor_tensor(weight[:, :], prob[:, :], keep[:, :], ALU.mult))
            far = float(2 * NE * CAP)
            link(nc.vector.scalar_tensor_tensor(out=base[:, :], in0=first[:, :], scalar=float(CAP), in1=rank[:, :],
                                                op0=ALU.mult, op1=ALU.add))
            link(nc.vector.scalar_tensor_tensor(out=base[:, :], in0=keep[:, :], scalar=-far, in1=base[:, :],
                                                op0=ALU.mult, op1=ALU.add))
            nc.vector.tensor_scalar(slot_s[:, :], base[:, :], far + NE * CAP, None, ALU.add).then_inc(slots_ready, 1)
            nc.vector.tensor_scalar(slot_g[:, :], base[:, :], far + NE * CAP, float(NE * CAP - 1), ALU.add,
                                    ALU.min).then_inc(slots_ready, 1)

        @block.scalar
        def _(act):
            act.wait_ge(shifted_ready, 1)
            nc.scalar.activation(ex[:, :, :], shifted[:, :, :], ACT.Exp).then_inc(exp_ready, 1)

        @block.tensor
        def _(pe):
            pe.wait_ge(order_ready, 2)
            pe.wait_ge(chosen_ready, 1)
            nc.tensor.matmul(psR[:, :, :], before[:, :], chosen[:, :, :], start=True, stop=False)
            for t in range(TT - 1):
                mm = nc.tensor.matmul(psR[:, t + 1:TT, :], ones[:, :],
                                      chosen[:, t:t + 1, :].broadcast_to([P, TT - 1 - t, NE]),
                                      start=False, stop=(t == TT - 2))
            mm.then_inc(ranked, 1)

        @block.gpsimd
        def _(pool):
            pool.wait_ge(slots_ready, 2)
            pool.wait_ge(ld_x2, 16 * B)
            for t in range(TT):
                nc.gpsimd.indirect_dma_start(a["xd"], bass.IndirectOffsetOnAxis(ap=slot_s[:, t:t + 1], axis=0),
                                             x2r[:, t, :], None, bounds_check=NE * CAP - 1,
                                             oob_is_err=False).then_inc(sent, 16)
            pool.wait_ge(sent, 16 * TT)


def experts(nc, a):
    with ExitStack() as ctx:
        def sem(name):
            return ctx.enter_context(nc.semaphore(name))

        def sb(name, shape, dt=F32):
            return ctx.enter_context(nc.sbuf_tensor(name, list(shape), dt))

        identf = sb("identf_e", [P, P])
        xe = sb("xe", [P, 2, 3, D])
        xe_hi, xe_lo = sb("xe_hi", [P, KD, CAP], F32R), sb("xe_lo", [P, KD, CAP], F32R)
        w1s, w2s = sb("w1_in", [P, 2, KD, DFF]), sb("w2_in", [P, FC, D])
        w1h, w1l = sb("w1_hi", [P, 2, KD, DFF], F32R), sb("w1_lo", [P, 2, KD, DFF], F32R)
        w2h, w2l = sb("w2_hi", [P, FC, D], F32R), sb("w2_lo", [P, FC, D], F32R)
        hid = sb("hid", [P, FC, CAP])
        hid_hi, hid_lo = sb("hid_hi", [P, 2, FC, CAP], F32R), sb("hid_lo", [P, 2, FC, CAP], F32R)
        ye = sb("ye", [P, 3, D])
        psX = ctx.enter_context(nc.psum_tensor("rows_banks", [P, 2, 512], F32))
        psH = ctx.enter_context(nc.psum_tensor("hidden_banks", [P, 4, 512], F32))
        psY = ctx.enter_context(nc.psum_tensor("out_banks", [P, 2, 512], F32))
        ld_ident = sem("e_ld_ident")
        ld_w1, ld_xe = [sem(f"ld_w1_{u}") for u in range(2)], [sem(f"ld_xe_{u}") for u in range(2)]
        ld_w2 = sem("ld_w2")
        w1_hi_done, w1_split, w2_hi_done, w2_split = (sem(n) for n in ("w1_hi_done", "w1_split", "w2_hi_done", "w2_split"))
        rows_full, rows_hi, rows_split = sem("rows_full"), sem("rows_hi"), sem("rows_split")
        hidden_full, gelu_done, hidden_hi, hidden_split = (sem(n) for n in ("hidden_full", "gelu_done", "hidden_hi", "hidden_split"))
        first_done, out_full, out_copied, st_ye = (sem(n) for n in ("first_done", "out_full", "out_copied", "st_ye"))
        block = ctx.enter_context(nc.Block())

        def over_experts(eng, body):
            body(0, 0, 0)
            body(1, 1, 0)
            with eng.Fori(1, NE // 2 - 1) as j:
                body(j * 2, 0, j)
                body(j * 2 + 1, 1, j)
            body(NE - 2, 0, NE // 2 - 1)
            body(NE - 1, 1, NE // 2 - 1)

        @block.sync
        def _(sp):
            def load_w1(e, u):
                sp.dma_start(w1s[:, u], a["w1"][e].rearrange("(k p) f -> p k f", p=P)).then_inc(ld_w1[u], 16)

            def load_w2(e):
                sp.dma_start(w2s[:, :, :], a["w2"][e].rearrange("(f p) d -> p f d", p=P)).then_inc(ld_w2, 16)

            def load_rows(e, u):
                sp.dma_start(xe[:, u, 0:2, :], a["xde"][e][0:2 * P].rearrange("(t p) d -> p t d", p=P)).then_inc(ld_xe[u], 16)
                sp.dma_start(xe[0:CAP - 2 * P, u, 2, :], a["xde"][e][2 * P:CAP]).then_inc(ld_xe[u], 16)

            sp.dma_start(identf[:, :], a["identf"]).then_inc(ld_ident, 16)
            load_w1(0, 0)
            load_rows(0, 0)
            load_rows(1, 1)
            load_w1(1, 1)
            load_w2(0)
            with sp.Fori(0, NE // 2 - 1) as j:
                for u in range(2):
                    e = j * 2 + u
                    sp.wait_ge(w1_split, (e + 1) * KD)
                    load_w1(e + 2, u)
                    sp.wait_ge(rows_full, (e + 1) * 2)
                    load_rows(e + 2, u)
                    sp.wait_ge(w2_split, (e + 1) * 2)
                    load_w2(e + 1)
            sp.wait_ge(w2_split, (NE - 1) * 2)
            load_w2(NE - 1)

        @block.scalar
        def _(act):
            def w1_hi(e, u, half):
                act.wait_ge(ld_w1[u], (half + 1) * 16)
                for k in range(KD):
                    nc.scalar.copy(w1h[:, u, k, :], w1s[:, u, k, :]).then_inc(w1_hi_done, 1)

            def w2_hi(e):
                act.wait_ge(ld_w2, (e + 1) * 16)
                for n in range(2):
                    f = slice(n * FC // 2, (n + 1) * FC // 2)
                    nc.scalar.copy(w2h[:, f, :], w2s[:, f, :]).then_inc(w2_hi_done, 1)

            def body(e, u, half):
                first = isinstance(e, int) and e == 0
                last = isinstance(e, int) and e == NE - 1
                for k in range(KD):
                    act.wait_ge(rows_full, e * 2 + k + 1)
                    if not first:
                        act.wait_ge(first_done, e)
                    nc.scalar.copy(xe_hi[:, k, :], psX[:, k, 0:CAP]).then_inc(rows_hi, 1)
                if not last:
                    if not first:
                        act.wait_ge(first_done, e)
                    w1_hi(e + 1, 1 - u, half + u)
                for f in range(FC):
                    act.wait_ge(hidden_full, e * FC + f + 1)
                    if not first:
                        act.wait_ge(hidden_split, (e - 1) * FC + f + 1)
                    nc.scalar.activation(hid[:, f, :], psH[:, f % 4, 0:CAP], ACT.Gelu_apprx_tanh).then_inc(gelu_done, 1)
                if not first:
                    act.wait_ge(out_full, e * 3)
                w2_hi(e)

            w1_hi(0, 0, 0)
            over_experts(act, body)

        @block.vector
        def _(dve):
            def w1_lo(e, u):
                for k in range(KD):
                    dve.wait_ge(w1_hi_done, e * KD + k + 1)
                    nc.vector.tensor_tensor(w1l[:, u, k, :], w1s[:, u, k, :], w1h[:, u, k, :].bitcast(F32),
                                            ALU.subtract).then_inc(w1_split, 1)

            def w2_lo(e):
                for n in range(2):
                    f = slice(n * FC // 2, (n + 1) * FC // 2)
                    dve.wait_ge(w2_hi_done, e * 2 + n + 1)
                    nc.vector.tensor_tensor(w2l[:, f, :], w2s[:, f, :], w2h[:, f, :].bitcast(F32),
                                            ALU.subtract).then_inc(w2_split, 1)

            def copy_out(e, u, half):
                for t in range(3):
                    dve.wait_ge(out_full, e * 3 + t + 1)
                    if t == 0 and not (isinstance(e, int) and e == 0):
                        dve.wait_ge(st_ye, e * 32)
                    nc.vector.tensor_copy(ye[:, t, :], psY[:, (u + t) % 2, 0:D]).then_inc(out_copied, 1)

            def body(e, u, half):
                first = isinstance(e, int) and e == 0
                last = isinstance(e, int) and e == NE - 1
                for k in range(KD):
                    dve.wait_ge(rows_hi, e * 2 + k + 1)
                    nc.vector.tensor_tensor(xe_lo[:, k, :], psX[:, k, 0:CAP], xe_hi[:, k, :].bitcast(F32),
                                            ALU.subtract).then_inc(rows_split, 1)
                if not last:
                    w1_lo(e + 1, 1 - u)
                for f in range(FC):
                    dve.wait_ge(gelu_done, e * FC + f + 1)
                    nc.vector.tensor_copy(hid_hi[:, u, f, :], hid[:, f, :]).then_inc(hidden_hi, 1)
                    dve.wait_ge(hidden_hi, e * FC + f + 1)
                    nc.vector.tensor_tensor(hid_lo[:, u, f, :], hid[:, f, :], hid_hi[:, u, f, :].bitcast(F32),
                                            ALU.subtract).then_inc(hidden_split, 1)
                if not first:
                    copy_out(e - 1, 1 - u, None)
                w2_lo(e)

            w1_lo(0, 0)
            over_experts(dve, body)
            copy_out(NE - 1, 1, None)

        @block.gpsimd
        def _(pool):
            with pool.Fori(0, NE) as e:
                pool.wait_ge(out_copied, (e + 1) * 3)
                pool.dma_start(a["yde"][e][0:2 * P].rearrange("(t p) d -> p t d", p=P), ye[:, 0:2, :]).then_inc(st_ye, 16)
                pool.dma_start(a["yde"][e][2 * P:CAP], ye[3 * P - CAP:P, 2, :]).then_inc(st_ye, 16)
            pool.wait_ge(st_ye, NE * 32)

        @block.tensor
        def _(pe):
            def second(e, u):
                pe.wait_ge(w2_split, (e + 1) * 2)
                pe.wait_ge(hidden_split, (e + 1) * FC)
                for t, at in enumerate((0, P, CAP - P)):
                    n = (u + t) % 2
                    if not (isinstance(e, int) and e == 0 and t < 2):
                        pe.wait_ge(out_copied, e * 3 + t - 1)
                    accumulate(pe, psY[:, n, 0:D], exact_products(
                        [((hid_hi[:, u, f, at:at + P], hid_lo[:, u, f, at:at + P]), (w2h[:, f, :], w2l[:, f, :]))
                         for f in range(FC)])).then_inc(out_full, 1)

            def body(e, u, half):
                first = isinstance(e, int) and e == 0
                pe.wait_ge(ld_xe[u], (half + 1) * 32)
                if not first:
                    pe.wait_ge(rows_split, e * 2)
                for k in range(KD):
                    for t, (at, n) in enumerate(TOK_TILES):
                        mm = pe.transpose(psX[:, k, at:at + n], xe[0:n, u, t, k * P:(k + 1) * P], identf[0:n, 0:n])
                    mm.then_inc(rows_full, 1)
                pe.wait_ge(w1_split, (e + 1) * KD)
                pe.wait_ge(rows_split, (e + 1) * 2)
                for f in range(FC):
                    w = slice(f * P, (f + 1) * P)
                    if not (first and f < 4):
                        pe.wait_ge(gelu_done, e * FC + f - 3)
                    mm = accumulate(pe, psH[:, f % 4, 0:CAP], exact_products(
                        [((w1h[:, u, k, w], w1l[:, u, k, w]), (xe_hi[:, k, :], xe_lo[:, k, :])) for k in range(KD)]))
                    mm.then_inc(hidden_full, 1)
                pe.wait_ge(hidden_full, (e + 1) * FC)
                pe.sem_inc(first_done, 1)
                if not first:
                    second(e - 1, 1 - u)

            pe.wait_ge(ld_ident, 16)
            over_experts(pe, body)
            second(NE - 1, 1)


def combine(nc, a, x2r, weight, slot_g):
    with ExitStack() as ctx:
        def sem(name):
            return ctx.enter_context(nc.semaphore(name))

        def sb(name, shape, dt=F32):
            return ctx.enter_context(nc.sbuf_tensor(name, list(shape), dt))

        PER = 4
        got = sb("got", [P, TT, D])
        mhalf = sb("minus_half_c", [P, 1])
        stats, mv = sb("stats_c", [P, TT, 6]), sb("mean_var_c", [P, TT, 2])
        vpe, rstd = sb("var_eps_c", [P, TT]), sb("rstd_c", [P, TT])
        halves, gathered, summed, stats_done, stats_ready, var_ready, rstd_ready, normed, st_out = (sem(n) for n in (
            "half_set", "gathered", "summed", "stats_done", "c_stats_ready", "c_var_ready", "c_rstd_ready", "normed", "st_out"))
        landed = [sem(f"landed{n}") for n in range(TT)]
        block = ctx.enter_context(nc.Block())

        @block.gpsimd
        def _(pool):
            nc.gpsimd.memset(mhalf[:, :], -0.5).then_inc(halves, 1)
            for t in range(TT):
                nc.gpsimd.indirect_dma_start(got[:, t, :], None, a["yd"],
                                             bass.IndirectOffsetOnAxis(ap=slot_g[:, t:t + 1], axis=0),
                                             ).then_inc(landed[t], 16)
            pool.wait_ge(halves, 1)
            for n in range(TT // PER):
                s = slice(n * PER, (n + 1) * PER)
                pool.wait_ge(stats_ready, (n + 1) * PER)
                nc.gpsimd.tensor_scalar(vpe[:, s], mv[:, s, 1], EPS, None, ALU.add).then_inc(var_ready, 1)
                pool.wait_ge(var_ready, n + 1)
                nc.gpsimd.tensor_tensor(rstd[:, s], vpe[:, s], mhalf[:, :].broadcast_to([P, PER]), ALU.pow).then_inc(rstd_ready, 1)

        @block.vector
        def _(dve):
            for n in range(TT // PER + 1):
                for t in range(n * PER, min((n + 1) * PER, TT)):
                    dve.wait_ge(landed[t], 16)
                    nc.vector.scalar_tensor_tensor(out=x2r[:, t, :], in0=got[:, t, :], scalar=weight[:, t:t + 1],
                                                   in1=x2r[:, t, :], op0=ALU.mult, op1=ALU.add).then_inc(summed, 1)
                    dve.wait_ge(summed, t + 1)
                    nc.vector.bn_stats(stats[:, t, :], x2r[:, t, :]).then_inc(stats_done, 1)
                    dve.wait_ge(stats_done, t + 1)
                    nc.vector.bn_aggr(mv[:, t, :], stats[:, t, :]).then_inc(stats_ready, 1)
                if n:
                    dve.wait_ge(rstd_ready, n)
                    dve.wait_ge(stats_ready, n * PER)
                    for t in range((n - 1) * PER, n * PER):
                        nc.vector.tensor_scalar(got[:, t, :], x2r[:, t, :], mv[:, t, 0:1], rstd[:, t:t + 1],
                                                ALU.subtract, ALU.mult).then_inc(normed, 1)

        @block.sync
        def _(sp):
            for n in range(TT // PER):
                sp.wait_ge(normed, (n + 1) * PER)
                sp.dma_start(a["out"].rearrange("(t p) d -> p t d", p=P)[:, n * PER:(n + 1) * PER, :],
                             got[:, n * PER:(n + 1) * PER, :]).then_inc(st_out, 16)
            sp.wait_ge(st_out, 16 * (TT // PER))


def decoder_layer(nc, a):
    xd = nc.dram_tensor("dispatched_rows", (NE * CAP, D), F32)
    yd = nc.dram_tensor("expert_rows", (NE * CAP, D), F32)
    a = dict(a, xd=xd.ap(), yd=yd.ap(), x2d=nc.dram_tensor("x2_rows", (B, S, D), F32).ap(),
             xde=xd.ap().rearrange("(e c) d -> e c d", e=NE), yde=yd.ap().rearrange("(e c) d -> e c d", e=NE))
    with ExitStack() as ctx:
        logits = ctx.enter_context(nc.sbuf_tensor("logits", [P, TT, NE], F32))
        attention(nc, a, logits)
        x2r = ctx.enter_context(nc.sbuf_tensor("x2_tokens", [P, TT, D], F32))
        weight = ctx.enter_context(nc.sbuf_tensor("token_weight", [P, TT], F32))
        slot_g = ctx.enter_context(nc.sbuf_tensor("token_slot", [P, TT], I32))
        router(nc, a, logits, x2r, weight, slot_g)
        experts(nc, a)
        combine(nc, a, x2r, weight, slot_g)


def bucket(distance):
    import numpy as np
    half, exact = BUCKETS // 2, BUCKETS // 4
    far = np.abs(distance)
    step = np.log(np.maximum(far, 1).astype(np.float32) / np.float32(exact)) / np.float32(np.log(MAX_DIST / exact))
    large = np.minimum(exact + (step * np.float32(half - exact)).astype(np.int32), half - 1)
    return (distance > 0) * half + np.where(far < exact, far, large)


def constants():
    import numpy as np
    i = np.arange(P)
    r = np.arange(NCH * P).reshape(NCH, P)
    mine = (r // KP)[:, :, None] == (np.array(CHUNK_HEAD)[:, None, None] + np.arange(3))
    pad = np.zeros((64, KP), np.float32)
    pad[:, 0:KP - SK] = -1e30
    return {
        "identf": np.eye(P, dtype=np.float32),
        "causal": ((i[None, :] > i[:, None]) * -1e30).astype(np.float32),
        "before": (i[:, None] < i[None, :]).astype(np.float32),
        "iota": np.tile(np.arange(NE, dtype=np.float32), (P, 1)),
        "onehot": (bucket(KP - 1 - np.arange(HANKEL))[None, :] == np.arange(BUCKETS)[:, None]).astype(np.float32),
        "padneg": pad,
        "blk_k": np.repeat((i[:, None] // HD2 == np.arange(GH)).astype(np.float32)[:, :, None], KP, axis=2),
        "blk_v": np.ascontiguousarray(np.repeat(mine.transpose(1, 0, 2).reshape(P, NCH * 3, 1), HD2 + 1, axis=2).astype(np.float32)),
    }


def kernel(**inputs):
    import concourse.bacc as bacc
    import numpy as np
    from concourse.bass_utils import run_bass_kernel_spmd

    v = {k: np.asarray(x) for k, x in inputs.items()}

    def T(name):
        return np.ascontiguousarray(v[name].T)

    ctxT = np.zeros((B, D, GH, KP), np.float32)
    ctxT[:, :, :, KP - SK:] = v["ctx_1024"][:, ::-1].transpose(0, 2, 1)[:, :, None, :]
    mask = np.zeros((P, B, KP), bool)
    mask[:, :, KP - SK:] = v["mask_Bx1x1xS2_bk0"][:, 0, 0, ::-1][None]
    memz = np.zeros((2, HD1, 2, 2, HD1 + 1), np.float32)
    for h in range(H1):
        memz[h % 2, :, h // 2, h % 2, 0:HD1] = v["L0_attn_mem"][h]
        memz[h % 2, :, h // 2, h % 2, HD1:] = v["L0_attn_z"][h]
    rel = v["L0_xattn_rel_bias"].T
    arrays = {
        "x": v["x"], "xT": np.ascontiguousarray(v["x"].transpose(0, 2, 1)), "ctxT": ctxT.reshape(B, D, GK), "mask": mask,
        "WqT": T("L0_attn_Wq"), "WkT": T("L0_attn_Wk"), "WvT": T("L0_attn_Wv"), "Wo1T": T("L0_attn_Wo"),
        "bo": np.tile(v["L0_attn_bo"], (64, 1)), "betas": np.tile(v["L0_attn_betas"].reshape(1, H1), (P, 1)),
        "memz": memz.reshape(P, 2, 2, HD1 + 1),
        "Wq2T": T("L0_xattn_Wq"), "Wk2T": T("L0_xattn_Wk"), "Wv2T": T("L0_xattn_Wv"), "Wo2T": T("L0_xattn_Wo"),
        "rel": np.ascontiguousarray(np.stack([rel, np.tile(rel[BUCKETS // 2 - 1], (BUCKETS, 1))], axis=1)),
        "gateT": T("L0_ffn_gate_w"), "w1": v["L0_ffn_w1"], "w2": v["L0_ffn_w2"], **constants(),
    }
    nc = bacc.Bacc("TRN2", target_bir_lowering=False, num_devices=1)
    aps = {k: nc.dram_tensor(f"in_{k}", x.shape, mybir.dt.from_np(x.dtype), kind="ExternalInput").ap() for k, x in arrays.items()}
    aps["out"] = nc.dram_tensor("out_0", (NTOK, D), F32, kind="ExternalOutput").ap()
    decoder_layer(nc, aps)
    r = run_bass_kernel_spmd(nc, [{f"in_{k}": x for k, x in arrays.items()}], core_ids=[0])
    return r.results[0]["out_0"].reshape(B, S, D)
```

```python
from contextlib import ExitStack

import concourse.bass as bass
from concourse import mybir

F32 = mybir.dt.float32
F32R = mybir.dt.float32r
BF16 = mybir.dt.bfloat16
I32 = mybir.dt.int32
U8 = mybir.dt.uint8
ALU = mybir.AluOpType
ACT = mybir.ActivationFunctionType
AX_X = mybir.AxisListType.X

P = 128
B, S, D = 4, 1024, 256
NT = S // P
KD = D // P
H1, HD1 = 4, 64
H2, HD2 = 16, 16
SK, KP = 77, 78
GH = 8
GK = GH * KP
NCH = -(-GK // P)
TAIL = GK - (NCH - 1) * P
BUCKETS, MAX_DIST = 32, 128
BIAS_TILES = 2
HANKEL = BIAS_TILES * P + KP - 1
NE, DFF = 16, 1024
NTOK = B * S
TT = NTOK // P
CAP = 320
FC = DFF // P
EPS = 1e-5
NEG = -1e9
CHUNK_HEAD = [min(c * P // KP, GH - 3) for c in range(NCH)]
TOK_TILES = [(0, 128), (128, 128), (256, 64)]


PAIRS = [(NT - 1 - n, n) for n in range(NT // 2)]
ORDER = [i for pair in PAIRS for i in pair]


REST = {
    ("O", 0): (0.37, 1.21), ("C", 0): (0.55, 1.65), ("W", 0): (1.32, 1.98), ("N", 0): (2.2, 2.97),
    ("X", 0): (2.31, 3.08), ("Q2", 0): (3.3, 4.18), ("S2", 0): (3.85, 4.73), ("S2", 1): (4.51, 5.61),
    ("T2", 0): (5.39, 6.38), ("T2", 1): (6.05, 6.71), ("PV2", 0): (7.15, 7.48), ("C2", 0): (7.81, 8.25),
    ("W2", 0): (9.08, 8.91), ("N2", 0): (9.35, 9.68), ("X2", 0): (9.46, 9.79), ("G", 0): (10.01, 10.45),
}
AM_AT = (-0.8, -0.7)
NEXT_AT = [1.3, 2.11, 2.92, 3.74, 4.55, 5.36, 6.17, 6.98, 7.8, 8.61, 9.42, 10.23]
SPLIT_AT = (12.9, 20.9)
T_LAG, PV_LAG = 1.4, 2.7


def body_steps(with_next):
    units = [(i, h) for pair in PAIRS for h in range(H1) for i in pair]
    at = []
    for u, (i, h) in enumerate(units):
        at += [(u - 1, ("S", i, h)), (u - 1 + T_LAG, ("T", i, h)), (u - 1 + PV_LAG, ("PV", i, h))]
    for n, pair in enumerate(PAIRS):
        end = (n + 1) * len(pair) * H1
        for i, x in zip(pair, AM_AT):
            at.append((end + x, ("AM", i, 0)))
        for (kind, h), where in REST.items():
            at += [(end + x, (kind, i, h)) for i, x in zip(pair, where)]
    if with_next:
        steps = [("QK", t, n) for t in (2, 0, 3, 1) for n in range(2)] + [("V", p, 0) for p in range(4)]
        at += [(len(units) + x, s) for x, s in zip(NEXT_AT, steps)]
        at += [(x, ("XS", n, 0)) for n, x in enumerate(SPLIT_AT)]
    at.sort(key=lambda one: one[0])
    return [s for _, s in at] + ([("V2", 0, 0), ("K2", 0, 0)] if with_next else [])


def first_steps():
    return ([("XS", n, 0) for n in range(2)] + [("QK", t, n) for t in (2, 0, 3, 1) for n in range(2)]
            + [("V", p, 0) for p in range(4)] + [("V2", 0, 0), ("K2", 0, 0)])


def transpose_groups(kind, i):
    if kind == "T":
        return [(j, min(4, i + 1 - j)) for j in range(0, i + 1, 4)]
    return [(0, 4), (4, NCH - 4)]


LINKS = {"QK": 1, "K2": 5, "V2": 1, "S2": 1, "AM": 2, "O": 2, "W": 1, "W2": 1, "PV2": 1}


def links_of(step):
    kind, i, h = step
    return 0 if kind == "QK" and i >= 2 else LINKS.get(kind, 0)


class Stage:
    RING, SLOTS = 3, 2

    def __init__(self, steps, before=None, times=1):
        self.steps = steps
        self.ring, self.slot = {}, {}
        self.ring_rise, self.slot_rise = [0] * self.RING, [0] * self.SLOTS
        used, scored = 0, 0
        for s in steps:
            kind, i, h = s
            if kind in ("S", "S2"):
                n = scored % self.SLOTS
                self.slot[s] = (n, self.slot_rise[n])
                self.slot_rise[n] += 1
                scored += 1
            elif kind not in ("O", "PV", "N", "N2", "XS"):
                for g in range(len(transpose_groups(kind, i)) if kind in ("T", "T2") else 1):
                    n = used % self.RING
                    self.ring[s + (g,)] = (n, self.ring_rise[n])
                    self.ring_rise[n] += 1
                    used += 1
        self.links_rise = sum(links_of(s) for s in steps)
        if before is None:
            self.ring_base, self.slot_base, self.links_base = [0] * self.RING, [0] * self.SLOTS, 0
        else:
            self.ring_base = [x + times * y for x, y in zip(before.ring_base, before.ring_rise)]
            self.slot_base = [x + times * y for x, y in zip(before.slot_base, before.slot_rise)]
            self.links_base = before.links_base + times * before.links_rise


def on_scalar(key):
    kind, i, h, n = key
    if kind in ("T", "T2"):
        return n == 0
    return kind in ("V", "C", "X", "Q2", "C2", "X2")


class Banks:

    def __init__(self, sem):
        self.ring_full = [sem(f"ring_full{n}") for n in range(Stage.RING)]
        self.ring_emptied = [sem(f"ring_emptied{n}") for n in range(Stage.RING)]
        self.scores_full = [sem(f"scores_full{n}") for n in range(Stage.SLOTS)]
        self.scores_emptied = [sem(f"scores_emptied{n}") for n in range(Stage.SLOTS)]


class Marks:

    def __init__(self, banks, stage):
        self.banks, self.stage = banks, stage

    def ring(self, sems, key, more):
        n, k = self.stage.ring[key]
        return sems[n], self.stage.ring_rise[n], self.stage.ring_base[n] + k + more

    def slot(self, sems, step, more):
        n, k = self.stage.slot[step]
        return sems[n], self.stage.slot_rise[n], self.stage.slot_base[n] + k + more

    def full(self, key):
        return self.ring(self.banks.ring_full, key, 1)

    def emptied(self, key):
        return self.ring(self.banks.ring_emptied, key, 1)

    def claim(self, key):
        return self.ring(self.banks.ring_emptied, key, 0)

    def scored(self, step):
        return self.slot(self.banks.scores_full, step, 1)

    def scores_read(self, step):
        return self.slot(self.banks.scores_emptied, step, 1)

    def claim_scores(self, step):
        return self.slot(self.banks.scores_emptied, step, 0)

    def before(self):
        return [(self.banks.ring_emptied[n], self.stage.ring_rise[n], self.stage.ring_base[n]) for n in range(Stage.RING)]

    def wait(self, eng, it, *marks):
        for one in {id(s): s for s, _, _ in marks}.values():
            rise, count = max((r, k) for s, r, k in marks if s is one)
            if count:
                eng.wait_ge(one, it * rise + count)


def spread(t, axis, shape):
    return t.unsqueeze(axis).broadcast_to(list(shape))


def exact_products(terms):
    out = []
    for (a_hi, a_lo), (b_hi, b_lo) in terms:
        out += [(a_hi, b_hi), (a_hi, b_lo), (a_lo, b_hi)]
    return out


def accumulate(eng, out, products):
    for n, (lhs, rhs) in enumerate(products):
        mm = eng.matmul(out, lhs, rhs, start=(n == 0), stop=(n == len(products) - 1))
    return mm


def attention(nc, a, logits):
    first = Stage(first_steps())
    body = Stage(body_steps(True), first)
    last = Stage(body_steps(False), body, B - 1)
    unit = {s[1:]: u for u, s in enumerate(s for s in last.steps if s[0] == "S")}
    s2_at = {s[1:]: n for n, s in enumerate(s for s in last.steps if s[0] == "S2")}
    NU = len(unit)
    vecd = nc.dram_tensor("bias_vector", (H2, HANKEL), F32)
    biasd = nc.dram_tensor("bias_rows", (BIAS_TILES, P, H2, KP), F32)
    norm = {s: n for n, s in enumerate(s for s in last.steps if s[0] in ("W", "W2"))}

    with ExitStack() as ctx:
        def sem(name):
            return ctx.enter_context(nc.semaphore(name))

        def sb(name, shape, dt=F32):
            return ctx.enter_context(nc.sbuf_tensor(name, list(shape), dt))

        psS = ctx.enter_context(nc.psum_tensor("score_banks", [P, 2, 2, 512], F32))
        ring = [ctx.enter_context(nc.psum_tensor(f"ring_bank{n}", [P, 512], F32)) for n in range(Stage.RING)]
        psO = ctx.enter_context(nc.psum_tensor("output_bank", [P, 512], F32))

        identf, identb, causal = sb("identf_sb", [P, P]), sb("identb_sb", [P, P], BF16), sb("causal_sb", [P, P], BF16)
        w_hi, w_lo = sb("w_qkv_hi", [P, KD, 3 * D], F32R), sb("w_qkv_lo", [P, KD, 3 * D], F32R)
        wo1, wq2, wk2, wv2, wo2 = (sb(n, [P, KD, D]) for n in ("wo1", "wq2", "wk2", "wv2", "wo2"))
        gw = sb("gate_w", [P, KD, NE])
        memz = sb("memz_sb", [P, 2, 2, HD1 + 1])
        betas, g_e, g_d, g, omg = (sb(n, [P, H1]) for n in ("betas_sb", "exp_beta", "one_exp_beta", "gate", "one_gate"))
        bo_hi, bo2 = sb("bo_hi", [64, D], F32R), sb("bo_rows", [64, D], F32R)
        ones2 = sb("ones2", [64, P], F32R)
        blk_k, blk_v = sb("blk_k_sb", [P, GH, KP]), sb("blk_v_sb", [P, NCH * 3, HD2 + 1])
        padneg, masku, maskf = sb("padneg_sb", [64, KP]), sb("mask_u8", [P, B, KP], U8), sb("mask_f", [P, B, KP])
        mneg, mneg_hi, mrow = sb("mneg", [64, KP]), sb("mneg_hi", [64, KP], F32R), sb("mrow", [64, KP], F32R)
        xT, x_hi, x_lo = sb("xT_sb", [P, KD, S]), sb("xT_hi", [P, KD, S], F32R), sb("xT_lo", [P, KD, S], F32R)
        qk_hi, qk_lo = sb("qk_hi", [P, 4, S], F32R), sb("qk_lo", [P, 4, S], F32R)
        sq, esq = sb("sigma_q", [P, 2, S]), sb("exp_q", [P, 512])
        V = sb("v_sb", [P, NT, D])
        xin = sb("x_in", [P, NT, D])
        x1, x2 = sb("x1_sb", [P, 2, D]), sb("x2_sb", [P, 2, D])
        ctxT = sb("ctxT_sb", [P, KD, GK])
        bias = sb("bias_sb", [P, BIAS_TILES, H2, KP])
        k2m, k2m_lo = sb("k2_masked", [P, 2, KP]), sb("k2_masked_lo", [P, 2, KP])
        k2m_r = sb("k2_masked_round", [P, 2, KP], F32R)
        k2_hi, k2_lo = sb("k2_hi", [P, 2, GH, KP], F32R), sb("k2_lo", [P, 2, GH, KP], F32R)
        v2 = sb("v2_blocks", [P, 2, NCH * 3, HD2 + 1])
        probs, probsT = sb("probs", [P, 2, S]), sb("probsT", [P, 2, NT, P])
        w_f = probs[:, :, 0:3 * D]
        spare = probsT[:, :, :, :].rearrange("p u j q -> p (u j q)")
        causal_f, bo_f = spare[:, 0:P], spare[0:64, P:P + D]
        rel = spare[0:BUCKETS, P + D + 2 * HANKEL:P + D + 2 * HANKEL + 2 * H2].rearrange("p (n h) -> p n h", n=2)
        reld = spare[0:BUCKETS, P + D + 2 * HANKEL + 2 * H2:P + D + 2 * HANKEL + 3 * H2]
        onehot, vec = (spare[0:n, P + D + k * HANKEL:P + D + (k + 1) * HANKEL] for k, n in enumerate((BUCKETS, H2)))
        p2, p2T = sb("probs2", [P, 2, 2, GK]), sb("probs2T", [P, 2, 2, NCH, P])
        negmax, rowsum, rrow = sb("negmax", [P, 4]), sb("rowsum", [P, 4, H1]), sb("rrow", [P, 2, H1])
        den, rden = sb("den", [P, 2, H1]), sb("rden", [P, 2, H1])
        am, c1, c1T = sb("mem_part", [P, 2, D]), sb("c1", [P, 2, D]), sb("c1T", [P, 2, KD, P])
        y = sb("y_sum", [P, 4, D])
        stats, mv, vpe, rstd = sb("stats", [P, 4, 6]), sb("mean_var", [P, 4, 2]), sb("var_eps", [P, 4]), sb("rstd", [P, 4])
        x1T, q2_hi, q2_lo = sb("x1T", [P, 2, KD, P]), sb("q2_hi", [P, 2, KD, P], F32R), sb("q2_lo", [P, 2, KD, P], F32R)
        max2, rden2 = sb("max2", [P, 2, GH]), sb("rden2", [P, 2, H2])
        c2, c2T, x2T = sb("c2", [P, 2, D]), sb("c2T", [P, 2, KD, P]), sb("x2T", [P, 2, KD, P])
        waiter, mhalf, eps, zero = sb("waiter", [1, 1]), sb("minus_half", [P, 1]), sb("eps", [P, 1]), sb("zero_rows", [P, 32])

        banks = Banks(sem)
        ld_w, ld_rel, ld_c, ld_xT, ld_x, ld_ctx, ld_bias = (sem(n) for n in (
            "ld_w", "ld_rel", "ld_c", "ld_xT", "ld_x", "ld_ctx", "ld_bias"))
        st_vec, st_bias, st_zero = (sem(n) for n in ("st_vec", "st_bias", "st_zero"))
        st_x2, tile_turn = [sem(f"st_x2_{w}") for w in range(2)], sem("tile_turn")
        exp_beta, w_hi_done, w_scaled, w_ready, rel_ready, vec_full, vec_ready = (sem(n) for n in (
            "exp_beta_done", "w_hi_done", "w_scaled", "w_ready", "rel_ready", "vec_full", "vec_ready"))
        consts_ready, zero_done, x_hi_done, x_split, qk_copied, sigma_done = (sem(n) for n in (
            "consts_ready", "zero_done", "x_hi_done", "x_split", "qk_copied", "sigma_done"))
        mrow_ready, bias_masked, k2_ready, k2_parts, k2_lo_ready, q2_hi_done, negmax_ready, pv_done = (sem(n) for n in (
            "mrow_ready", "bias_masked", "k2_ready", "k2_parts", "k2_lo_ready", "q2_hi_done", "negmax_ready", "pv_done"))
        c1_ready, c2_ready, x1_ready, x2_ready, p2_ready = (sem(n) for n in (
            "c1_ready", "c2_ready", "x1_ready", "x2_ready", "p2_ready"))
        stats_ready, rstd_ready, vec_done, setup_done, var_ready, pool_set = (sem(n) for n in (
            "stats_ready", "rstd_ready", "vec_done", "setup_done", "var_ready", "pool_set"))

        def scores(m, step):
            return psS[:, m.stage.slot[step][0], :, :].rearrange("p b c -> p (b c)")

        def bank(m, key):
            return ring[m.stage.ring[key][0]]

        def side(i):
            return ORDER.index(i) % 2

        def over_stages(eng, walk):
            walk(Marks(banks, first), 0, None, 0)
            with eng.Fori(0, B - 1) as b:
                walk(Marks(banks, body), b, b, b + 1)
            walk(Marks(banks, last), 0, B - 1, None)

        def blocks(t, n=KD):
            return t[:, 0:n * P].rearrange("p (j q) -> p j q", q=P)

        LOADS_C = 13
        block = ctx.enter_context(nc.Block())

        @block.sync
        def _(sp):
            def load_xT(b):
                sp.dma_start(xT[:, :, :], a["xT"][b].rearrange("(k p) s -> p k s", p=P)).then_inc(ld_xT, 16)

            def load_ctx(b):
                sp.dma_start(ctxT[:, :, :], a["ctxT"][b].rearrange("(k p) s -> p k s", p=P)).then_inc(ld_ctx, 16)

            def load_x(b):
                sp.dma_start(xin[:, :, :], a["x"][b].rearrange("(t p) d -> p t d", p=P)).then_inc(ld_x, 16)

            def load_bias():
                sp.dma_start(bias[:, :, :, :], biasd.ap().rearrange("t p h k -> p t h k")).then_inc(ld_bias, 16)

            def store_x2(b, i):
                sp.wait_ge(x2_ready, b * NT + ORDER.index(i) + 1)
                sp.sem_inc(tile_turn, 1)
                sp.dma_start(a["x2d"][b][i * P:(i + 1) * P, :], x2[:, side(i), :]).then_inc(st_x2[side(i)], 16)

            for n, name in enumerate(("WqT", "WkT", "WvT")):
                sp.dma_start(w_f[:, :, n * D:(n + 1) * D], a[name].rearrange("(k p) n -> p k n", p=P)).then_inc(ld_w, 16)
            sp.dma_start(betas[:, :], a["betas"]).then_inc(ld_w, 16)
            sp.dma_start(memz[:, :, :, :], a["memz"]).then_inc(ld_w, 16)
            load_xT(0)
            sp.dma_start(rel[:, :, :], a["rel"]).then_inc(ld_rel, 16)
            sp.dma_start(onehot[:, :], a["onehot"]).then_inc(ld_rel, 16)
            for t, name in ((identf, "identf"), (causal_f, "causal"), (masku, "mask"),
                            (padneg, "padneg"), (blk_k, "blk_k"), (blk_v, "blk_v"), (bo_f, "bo")):
                sp.dma_start(t[:], a[name]).then_inc(ld_c, 16)
            for t, name in ((wk2, "Wk2T"), (wv2, "Wv2T"), (wo1, "Wo1T"), (wq2, "Wq2T"), (wo2, "Wo2T"), (gw, "gateT")):
                sp.dma_start(t[:, :, :], a[name].rearrange("(k p) n -> p k n", p=P)).then_inc(ld_c, 16)
            load_ctx(0)
            load_x(0)
            sp.wait_ge(vec_ready, 1)
            sp.dma_start(vecd.ap(), vec[:, :]).then_inc(st_vec, 16)
            sp.wait_ge(st_vec, 16)
            for t in range(BIAS_TILES):
                hankel = bass.AP(vecd, t * P, [[1, P], [HANKEL, H2], [1, KP]])
                sp.dma_start(biasd.ap()[t], hankel).then_inc(st_bias, 16)
            sp.wait_ge(st_bias, 16 * BIAS_TILES)
            load_bias()
            sp.wait_ge(zero_done, 1)
            rows = a["xd"].rearrange("(n p r) (k d) -> n p (r k) d", p=P, r=4, d=32)
            for n in range(NE * CAP // (4 * P)):
                sp.dma_start(rows[n], zero[:, :].unsqueeze(1).broadcast_to([P, 4 * D // 32, 32])).then_inc(st_zero, 16)
            for w in range(2):
                sp.sem_inc(st_x2[w], 16)
            with sp.Fori(0, B - 1) as b:
                sp.wait_ge(x_split, (b + 1) * 2)
                load_xT(b + 1)
                sp.wait_ge(k2_ready, (b + 1) * 2)
                load_ctx(b + 1)
                for n, pair in enumerate(PAIRS):
                    if n == NT // 2 - 1:
                        sp.wait_ge(stats_ready, b * len(norm) + norm[("W", ORDER[-1], 0)] + 1)
                        load_x(b + 1)
                    for i in pair:
                        store_x2(b, i)
                    if n == BIAS_TILES - 1:
                        sp.wait_ge(p2_ready, b * len(s2_at) + s2_at[(BIAS_TILES - 1, 1)] + 1)
                        load_bias()
            for i in ORDER:
                store_x2(B - 1, i)
            for w in range(2):
                sp.wait_ge(st_x2[w], 16 * (1 + B * NT // 2))
            sp.wait_ge(st_zero, 16 * (NE * CAP // (4 * P)))

        @block.gpsimd
        def _(pool):
            nc.gpsimd.memset(mhalf[:, :], -0.5).then_inc(pool_set, 1)
            nc.gpsimd.memset(eps[:, :], EPS).then_inc(pool_set, 1)
            pool.wait_ge(pool_set, 2)
            pool.wait_ge(consts_ready, 1)
            with pool.Fori(0, B) as b:
                pool.wait_ge(k2_parts, b + 1)
                for n in range(2):
                    nc.gpsimd.tensor_tensor(k2_lo[:, n, :, :], spread(k2m_lo[:, n, :], 1, [P, GH, KP]),
                                            blk_k[:, :, :], ALU.mult).then_inc(k2_lo_ready, 1)
                pool.wait_ge(ld_bias, (b + 1) * 16)
                for t in range(BIAS_TILES):
                    mask = maskf[:, bass.ds(b, 1), :].broadcast_to([P, H2, KP])
                    nc.gpsimd.tensor_tensor(bias[:, t], bias[:, t], mask, ALU.mult).then_inc(bias_masked, 1)
                for s, n in norm.items():
                    w = 2 * (s[0] == "W2") + side(s[1])
                    pool.wait_ge(stats_ready, b * len(norm) + n + 1)
                    nc.gpsimd.tensor_tensor(vpe[:, w:w + 1], mv[:, w, 1:2], eps[:, :], ALU.add).then_inc(var_ready, 1)
                    pool.wait_ge(var_ready, b * len(norm) + n + 1)
                    nc.gpsimd.tensor_tensor(rstd[:, w:w + 1], vpe[:, w:w + 1], mhalf[:, :], ALU.pow).then_inc(rstd_ready, 1)

        @block.scalar
        def _(act):
            act.wait_ge(ld_w, 80)
            nc.scalar.activation(g_e[:, :], betas[:, :], ACT.Exp, scale=-1.0).then_inc(exp_beta, 1)
            act.wait_ge(w_scaled, KD)
            nc.scalar.copy(w_hi[:, :, :], w_f[:, :, :]).then_inc(w_hi_done, 1)

            def walk(m, it, b, nb):
                queries = 0
                for s in m.stage.steps:
                    kind, i, h = s
                    if kind == "XS":
                        if i == 0:
                            act.wait_ge(ld_xT, (nb + 1) * 16)
                        cols = slice(i * 512, (i + 1) * 512)
                        nc.scalar.copy(x_hi[:, :, cols], xT[:, :, cols]).then_inc(x_hi_done, 1)
                    elif kind == "QK":
                        cols = slice(h * 512, (h + 1) * 512)
                        m.wait(act, it, m.full(s + (0,)))
                        if i < 2:
                            if queries:
                                act.wait_ge(sigma_done, nb * 4 + queries)
                            nc.scalar.activation(esq[:, :], bank(m, s + (0,))[:, :], ACT.Exp).then_inc(qk_copied, 1)
                            queries += 1
                        nc.scalar.copy(qk_hi[:, i, cols], bank(m, s + (0,))[:, :]).then_inc(qk_copied, 1)
                    elif kind == "S":
                        u, nk = unit[(i, h)], (i + 1) * P
                        act.wait_ge(negmax_ready, b * NU + u + 1)
                        nc.scalar.activation(probs[:, u % 2, 0:nk], scores(m, s)[:, 0:nk], ACT.Exp,
                                             bias=negmax[:, u % 4:u % 4 + 1],
                                             accum_out=rowsum[:, ORDER.index(i) % 4, h:h + 1]).then_inc(
                                                 banks.scores_emptied[m.stage.slot[s][0]], 1)
                    elif kind == "S2":
                        m.wait(act, it, m.scores_read(s))
                        row = p2[:, side(i), h, :]
                        nc.scalar.activation(row, row, ACT.Exp).then_inc(p2_ready, 1)
                    for key in m.stage.ring:
                        if key[:3] != s or not on_scalar(key):
                            continue
                        m.wait(act, it, m.full(key))
                        full, done = bank(m, key), banks.ring_emptied[m.stage.ring[key][0]]
                        if kind == "V":
                            nc.scalar.copy(V[:, 2 * i:2 * i + 2, :],
                                           full[:, :].rearrange("p (t d) -> p t d", t=2)).then_inc(done, 1)
                        elif kind == "T":
                            j, n = transpose_groups(kind, i)[key[3]]
                            nc.scalar.copy(probsT[:, unit[(i, h)] % 2, j:j + n, :], blocks(full, n)).then_inc(done, 1)
                        elif kind == "T2":
                            j, n = transpose_groups(kind, i)[key[3]]
                            nc.scalar.copy(p2T[:, side(i), h, j:j + n, :], blocks(full, n)).then_inc(done, 1)
                        else:
                            dst = {"C": c1T, "X": x1T, "C2": c2T, "Q2": q2_hi, "X2": x2T}[kind]
                            nc.scalar.copy(dst[:, side(i)], blocks(full)).then_inc(q2_hi_done if kind == "Q2" else done, 1)

            act.wait_ge(consts_ready, 1)
            act.wait_ge(st_vec, 16)
            over_stages(act, walk)

        @block.vector
        def _(dve):
            links = 0

            def link(ins):
                nonlocal links
                links += 1
                ins.then_inc(setup_done, 1)
                dve.wait_ge(setup_done, links)

            dve.wait_ge(ld_rel, 32)
            nc.vector.tensor_tensor(reld[:, :], rel[:, 0, :], rel[:, 1, :], ALU.subtract).then_inc(rel_ready, 1)
            nc.vector.memset(zero[:, :], 0.0).then_inc(zero_done, 1)
            dve.wait_ge(exp_beta, 1)
            link(nc.vector.tensor_scalar(g_d[:, :], g_e[:, :], 1.0, None, ALU.add))
            link(nc.vector.reciprocal(g[:, :], g_d[:, :]))
            link(nc.vector.tensor_tensor(omg[:, :], g_e[:, :], g[:, :], ALU.mult))
            for k in range(KD):
                wv = w_f[:, k, 2 * D:3 * D].rearrange("p (h d) -> p h d", h=H1)
                nc.vector.tensor_tensor(wv, wv, spread(omg[:, :], 2, [P, H1, HD1]), ALU.mult).then_inc(w_scaled, 1)
            for n in range(2):
                mem = memz[:, n, :, 0:HD1]
                nc.vector.tensor_tensor(mem, mem, spread(g[:, 2 * n:2 * n + 2], 2, [P, 2, HD1]), ALU.mult).then_inc(w_ready, 1)
            dve.wait_ge(w_hi_done, 1)
            nc.vector.tensor_tensor(w_lo[:, :, :], w_f[:, :, :], w_hi[:, :, :].bitcast(F32), ALU.subtract).then_inc(w_ready, 1)
            dve.wait_ge(vec_full, 1)
            nc.vector.tensor_copy(vec[:, :], psO[0:H2, 0:HANKEL]).then_inc(vec_ready, 1)
            dve.wait_ge(ld_c, 16 * LOADS_C)
            link(nc.vector.memset(ones2[:, :].bitcast(F32), 1.0))
            link(nc.vector.memset(bo2[:, :].bitcast(F32), 0.0))
            link(nc.vector.tensor_copy(identb[:, :], identf[:, :]))
            link(nc.vector.tensor_copy(causal[:, :], causal_f[:, :]))
            link(nc.vector.memset(mrow[:, :].bitcast(F32), 0.0))
            link(nc.vector.tensor_copy(bo_hi[:, :], bo_f[:, :]))
            link(nc.vector.tensor_copy(bo2[0:1, :], bo_f[0:1, :]))
            link(nc.vector.tensor_tensor(bo2[32:33, :], bo_f[32:33, :], bo_hi[32:33, :].bitcast(F32), ALU.subtract))
            for n in range(2):
                link(nc.vector.tensor_copy(v2[:, n, :, HD2:HD2 + 1], blk_v[:, :, HD2:HD2 + 1]))
            nc.vector.tensor_copy(maskf[:, :, :], masku[:, :, :]).then_inc(consts_ready, 1)
            dve.wait_ge(consts_ready, 1)

            def walk(m, it, b, nb):
                own, copied, queries = 0, 0, 0

                def linked(ins):
                    nonlocal own
                    own += 1
                    ins.then_inc(vec_done, 1)
                    dve.wait_ge(vec_done, it * m.stage.links_rise + (m.stage.links_base + own))

                for s in m.stage.steps:
                    kind, i, h = s
                    key = s + (0,)
                    if key in m.stage.ring:
                        full, done = bank(m, key), banks.ring_emptied[m.stage.ring[key][0]]
                    if kind == "XS":
                        cols = slice(i * 512, (i + 1) * 512)
                        dve.wait_ge(x_hi_done, nb * 2 + i + 1)
                        nc.vector.tensor_tensor(x_lo[:, :, cols], xT[:, :, cols], x_hi[:, :, cols].bitcast(F32),
                                                ALU.subtract).then_inc(x_split, 1)
                    elif kind == "QK":
                        cols = slice(h * 512, (h + 1) * 512)
                        copied += 2 if i < 2 else 1
                        dve.wait_ge(qk_copied, nb * 12 + copied)
                        if i < 2:
                            linked(nc.vector.tensor_scalar(sq[:, i, cols], full[:, :], 0.0, None, ALU.max))
                        nc.vector.tensor_tensor(qk_lo[:, i, cols], full[:, :], qk_hi[:, i, cols].bitcast(F32),
                                                ALU.subtract).then_inc(done, 1)
                        if i < 2:
                            nc.vector.scalar_tensor_tensor(out=sq[:, i, cols], in0=esq[:, :], scalar=1.0,
                                                           in1=sq[:, i, cols], op0=ALU.min, op1=ALU.add).then_inc(sigma_done, 1)
                    elif kind == "K2":
                        m.wait(dve, it, m.full(key))
                        nc.vector.tensor_tensor(k2m[:, :, :], full[:, 0:2 * KP].rearrange("p (g k) -> p g k", g=2),
                                                maskf[:, bass.ds(nb, 1), :].broadcast_to([P, 2, KP]), ALU.mult).then_inc(done, 1)
                        m.wait(dve, it, m.emptied(key))
                        linked(nc.vector.tensor_copy(k2m_r[:, :, :], k2m[:, :, :]))
                        nc.vector.tensor_tensor(k2m_lo[:, :, :], k2m[:, :, :], k2m_r[:, :, :].bitcast(F32),
                                                ALU.subtract).then_inc(k2_parts, 1)
                        for n in range(2):
                            nc.vector.tensor_tensor(k2_hi[:, n, :, :], spread(k2m_r[:, n, :].bitcast(F32), 1, [P, GH, KP]),
                                                    blk_k[:, :, :], ALU.mult).then_inc(k2_ready, 1)
                        mask = maskf[:, bass.ds(nb, 1), :].rearrange("p a k -> p (a k)")
                        linked(nc.vector.tensor_scalar(mneg[:, :], mask[0:64, :], 1.0, -NEG, ALU.subtract, ALU.mult))
                        linked(nc.vector.tensor_tensor(mneg[:, :], mneg[:, :], padneg[:, :], ALU.add))
                        linked(nc.vector.tensor_copy(mneg_hi[:, :], mneg[:, :]))
                        linked(nc.vector.tensor_copy(mrow[0:1, :], mneg[0:1, :]))
                        nc.vector.tensor_tensor(mrow[32:33, :], mneg[32:33, :], mneg_hi[32:33, :].bitcast(F32),
                                                ALU.subtract).then_inc(mrow_ready, 1)
                    elif kind == "Q2":
                        dve.wait_ge(q2_hi_done, b * NT + ORDER.index(i) + 1)
                        nc.vector.tensor_tensor(q2_lo[:, side(i)], blocks(full), q2_hi[:, side(i)].bitcast(F32),
                                                ALU.subtract).then_inc(done, 1)
                    elif kind == "V2":
                        m.wait(dve, it, m.full(key))
                        src = full[:, 0:2 * NCH * 3 * HD2].rearrange("p (g c d) -> p g c d", g=2, d=HD2)
                        for rows, lo, hi in ((P, 0, 3 * (NCH - 1)), (TAIL, 3 * (NCH - 1), 3 * NCH)):
                            ins = nc.vector.tensor_tensor(
                                v2[0:rows, :, lo:hi, 0:HD2], src[0:rows, :, lo:hi, :],
                                spread(blk_v[0:rows, lo:hi, 0:HD2], 1, [rows, 2, hi - lo, HD2]), ALU.mult)
                            if lo == 0:
                                linked(ins)
                        ins.then_inc(done, 1)
                    elif kind == "S":
                        u = unit[(i, h)]
                        m.wait(dve, it, m.scored(s))
                        nc.vector.tensor_reduce(negmax[:, u % 4:u % 4 + 1], scores(m, s)[:, 0:(i + 1) * P], AX_X,
                                                ALU.max, negate=True).then_inc(negmax_ready, 1)
                    elif kind == "S2":
                        m.wait(dve, it, m.scored(s))
                        sc = psS[:, m.stage.slot[s][0], :, 0:4 * KP].rearrange("p b (h k) -> p b h k", h=4)
                        mx = max2[:, h, :].rearrange("p (b h) -> p b h", b=2)
                        linked(nc.vector.tensor_reduce(mx, sc, AX_X, ALU.max))
                        nc.vector.tensor_tensor(
                            p2[:, side(i), h, :].rearrange("p (b h k) -> p b h k", b=2, h=4), sc,
                            spread(mx, 3, [P, 2, 4, KP]), ALU.subtract).then_inc(banks.scores_emptied[m.stage.slot[s][0]], 1)
                    elif kind == "AM":
                        m.wait(dve, it, m.full(key))
                        src = full[:, 0:H1 * (HD1 + 1)].rearrange("p (h e) -> p h e", h=H1)
                        linked(nc.vector.tensor_scalar(den[:, side(i), :], src[:, :, HD1], 1e-6, None, ALU.add))
                        linked(nc.vector.reciprocal(rden[:, side(i), :], den[:, side(i), :]))
                        nc.vector.tensor_tensor(am[:, side(i), :].rearrange("p (h d) -> p h d", h=H1), src[:, :, 0:HD1],
                                                spread(rden[:, side(i), :], 2, [P, H1, HD1]), ALU.mult).then_inc(done, 1)
                    elif kind == "O":
                        w = side(i)
                        dve.wait_ge(pv_done, b * NU + unit[(i, H1 - 1)] + 1)
                        linked(nc.vector.reciprocal(rrow[:, w, :], rowsum[:, ORDER.index(i) % 4, :]))
                        linked(nc.vector.tensor_tensor(c1[:, w, :].rearrange("p (h d) -> p h d", h=H1),
                                                       psO[:, w * D:(w + 1) * D].rearrange("p (h d) -> p h d", h=H1),
                                                       spread(rrow[:, w, :], 2, [P, H1, HD1]), ALU.mult))
                        m.wait(dve, it, m.emptied(("AM", i, 0, 0)))
                        nc.vector.tensor_tensor(c1[:, w, :], c1[:, w, :], am[:, w, :], ALU.add).then_inc(c1_ready, 1)
                    elif kind in ("W", "W2"):
                        w = 2 * (kind == "W2") + side(i)
                        m.wait(dve, it, m.full(key))
                        if s == ("W", ORDER[0], 0):
                            dve.wait_ge(ld_x, (b + 1) * 16)
                        residual = xin[:, i, :] if kind == "W" else x1[:, side(i), :]
                        nc.vector.tensor_tensor(y[:, w, :], full[:, 0:D], residual, ALU.add).then_inc(done, 1)
                        m.wait(dve, it, m.emptied(key))
                        linked(nc.vector.bn_stats(stats[:, w, :], y[:, w, :]))
                        nc.vector.memset(waiter[:, :], 0.0)
                        nc.vector.bn_aggr(mv[:, w, :], stats[:, w, :]).then_inc(stats_ready, 1)
                    elif kind in ("N", "N2"):
                        w = 2 * (kind == "N2") + side(i)
                        dve.wait_ge(rstd_ready, b * len(norm) + norm[("W" + kind[1:], i, 0)] + 1)
                        if kind == "N2":
                            dve.wait_ge(st_x2[side(i)], (b * (NT // 2) + (ORDER.index(i) // 2 + 1)) * 16)
                        nc.vector.tensor_scalar((x2 if kind == "N2" else x1)[:, side(i), :], y[:, w, :], mv[:, w, 0:1],
                                                rstd[:, w:w + 1], ALU.subtract, ALU.mult).then_inc(
                                                    x2_ready if kind == "N2" else x1_ready, 1)
                        if kind == "N":
                            dve.wait_ge(x1_ready, b * NT + ORDER.index(i) + 1)
                    elif kind == "PV2":
                        m.wait(dve, it, m.full(key))
                        src = full[:, 0:H2 * (HD2 + 1)].rearrange("p (h e) -> p h e", h=H2)
                        linked(nc.vector.reciprocal(rden2[:, side(i), :], src[:, :, HD2]))
                        nc.vector.tensor_tensor(c2[:, side(i), :].rearrange("p (h d) -> p h d", h=H2), src[:, :, 0:HD2],
                                                spread(rden2[:, side(i), :], 2, [P, H2, HD2]), ALU.mult).then_inc(done, 1)
                    elif kind == "G":
                        m.wait(dve, it, m.full(key))
                        at = logits[:, bass.ds(b * NT + i, 1), :].rearrange("p a e -> p (a e)")
                        nc.vector.tensor_copy(at, full[:, 0:NE]).then_inc(done, 1)
                    elif kind in ("T", "T2"):
                        for n3, (j, n) in enumerate(transpose_groups(kind, i)):
                            key = s + (n3,)
                            if on_scalar(key):
                                continue
                            m.wait(dve, it, m.full(key))
                            full, done = bank(m, key), banks.ring_emptied[m.stage.ring[key][0]]
                            if kind == "T":
                                nc.vector.tensor_copy(probsT[:, unit[(i, h)] % 2, j:j + n, :], blocks(full, n)).then_inc(done, 1)
                            else:
                                rows = TAIL if j else P
                                nc.vector.tensor_copy(p2T[0:rows, side(i), h, j:j + n, :], blocks(full, n)[0:rows]).then_inc(done, 1)
                assert own == m.stage.links_rise, (own, m.stage.links_rise)

            over_stages(dve, walk)

        @block.tensor
        def _(pe):
            pe.wait_ge(ld_rel, 32)
            pe.wait_ge(rel_ready, 1)
            nc.tensor.matmul(psO[0:H2, 0:HANKEL], reld[:, :], onehot[:, :], start=True, stop=True).then_inc(vec_full, 1)
            pe.wait_ge(w_ready, 3)
            pe.wait_ge(vec_ready, 1)
            pe.wait_ge(ld_c, 16 * LOADS_C)
            pe.wait_ge(consts_ready, 1)

            def walk(m, it, b, nb):
                for s in m.stage.steps:
                    kind, i, h = s
                    key = s + (0,)
                    need = []
                    if key in m.stage.ring and kind not in ("T", "T2"):
                        need = [m.claim(key)]
                        full, done = bank(m, key), banks.ring_full[m.stage.ring[key][0]]
                    q = slice(i * P, (i + 1) * P)
                    if kind == "QK":
                        m.wait(pe, it, *need)
                        pe.wait_ge(x_split, nb * 2 + h + 1)
                        w, cols = slice(i * P, (i + 1) * P), slice(h * 512, (h + 1) * 512)
                        accumulate(pe, full[:, :], exact_products(
                            [((w_hi[:, k, w], w_lo[:, k, w]), (x_hi[:, k, cols], x_lo[:, k, cols])) for k in range(KD)]
                        )).then_inc(done, 1)
                    elif kind == "V":
                        m.wait(pe, it, *need)
                        w = slice(2 * D, 3 * D)
                        for n in range(2):
                            t = slice((2 * i + n) * P, (2 * i + n + 1) * P)
                            mm = accumulate(pe, full[:, n * D:(n + 1) * D], exact_products(
                                [((x_hi[:, k, t], x_lo[:, k, t]), (w_hi[:, k, w], w_lo[:, k, w])) for k in range(KD)]))
                        mm.then_inc(done, 1)
                    elif kind == "K2":
                        m.wait(pe, it, *need)
                        for n in range(2):
                            mm = accumulate(pe, full[:, n * KP:(n + 1) * KP], [
                                (wk2[:, k, n * P:(n + 1) * P], ctxT[:, k, 0:KP]) for k in range(KD)])
                        mm.then_inc(done, 1)
                    elif kind == "V2":
                        m.wait(pe, it, *need)
                        pe.wait_ge(ld_ctx, (nb + 1) * 16)
                        for n in range(2):
                            for c in range(NCH):
                                rows, at = min(P, GK - c * P), (n * NCH + c) * 3 * HD2
                                w = (n * GH + CHUNK_HEAD[c]) * HD2
                                mm = accumulate(pe, full[0:rows, at:at + 3 * HD2], [
                                    (ctxT[:, k, c * P:c * P + rows], wv2[:, k, w:w + 3 * HD2]) for k in range(KD)])
                        mm.then_inc(done, 1)
                    elif kind == "S":
                        if unit[(i, h)] == 0:
                            need = m.before()
                        m.wait(pe, it, m.claim_scores(s), *need)
                        r, t, nk = slice(h % 2 * HD1, h % 2 * HD1 + HD1), h // 2, (i + 1) * P
                        for c in range(0, nk, 512):
                            cols = slice(c, min(c + 512, nk))
                            last = cols.stop == nk
                            products = exact_products([((qk_hi[r, t, q], qk_lo[r, t, q]),
                                                        (qk_hi[r, 2 + t, cols], qk_lo[r, 2 + t, cols]))])
                            for n, (lhs, rhs) in enumerate(products):
                                mm = pe.matmul(scores(m, s)[:, cols], lhs, rhs, start=(n == 0),
                                               stop=(n == len(products) - 1 and not last))
                        pe.matmul(scores(m, s)[:, i * P:nk], identb[:, :], causal[:, :], start=False,
                                  stop=True).then_inc(banks.scores_full[m.stage.slot[s][0]], 1)
                    elif kind == "T":
                        m.wait(pe, it, m.scores_read(("S", i, h)))
                        u = unit[(i, h)]
                        for n3, (j, n) in enumerate(transpose_groups(kind, i)):
                            m.wait(pe, it, m.claim(s + (n3,)))
                            for jj in range(j, j + n):
                                mm = pe.transpose(bank(m, s + (n3,))[:, (jj - j) * P:(jj - j + 1) * P],
                                                  probs[:, u % 2, jj * P:(jj + 1) * P], identf[:, :])
                            mm.then_inc(banks.ring_full[m.stage.ring[s + (n3,)][0]], 1)
                    elif kind == "PV":
                        u = unit[(i, h)]
                        if h == 0 and ORDER.index(i) >= 2:
                            pe.wait_ge(c1_ready, b * NT + ORDER.index(i) - 1)
                        m.wait(pe, it, *[m.emptied(("T", i, h, n3)) for n3 in range(len(transpose_groups("T", i)))])
                        w = side(i) * D
                        d = slice(h * HD1, (h + 1) * HD1)
                        accumulate(pe, psO[:, w + h * HD1:w + (h + 1) * HD1], [(probsT[:, u % 2, j, :], V[:, j, d]) for j in range(i + 1)]).then_inc(pv_done, 1)
                    elif kind == "AM":
                        m.wait(pe, it, *need)
                        if i == ORDER[0]:
                            pe.wait_ge(sigma_done, (b + 1) * 4)
                        for n in range(2):
                            w = 2 * (HD1 + 1)
                            mm = pe.matmul(full[:, n * w:(n + 1) * w], sq[:, n, q], memz[:, n, :, :], start=True, stop=True)
                        mm.then_inc(done, 1)
                    elif kind in ("C", "X", "C2", "X2"):
                        src, ready = {"C": (c1, c1_ready), "X": (x1, x1_ready), "C2": (c2, None), "X2": (x2, x2_ready)}[kind]
                        if ready is None:
                            need.append(m.emptied(("PV2", i, 0, 0)))
                        m.wait(pe, it, *need)
                        if ready is not None:
                            pe.wait_ge(ready, b * NT + ORDER.index(i) + 1)
                        for k in range(KD):
                            mm = pe.transpose(full[:, k * P:(k + 1) * P], src[:, side(i), k * P:(k + 1) * P], identf[:, :])
                        mm.then_inc(done, 1)
                    elif kind in ("W", "W2", "G"):
                        before, lhs, rhs = {"W": ("C", c1T, wo1), "W2": ("C2", c2T, wo2), "G": ("X2", x2T, gw)}[kind]
                        m.wait(pe, it, *need, m.emptied((before, i, 0, 0)))
                        products = [(lhs[:, side(i), k, :], rhs[:, k, :]) for k in range(KD)]
                        if kind == "W":
                            products.append((ones2[:, :], bo2[:, :]))
                        accumulate(pe, full[:, 0:NE if kind == "G" else D], products).then_inc(done, 1)
                    elif kind == "Q2":
                        m.wait(pe, it, *need, m.emptied(("X", i, 0, 0)))
                        for n in range(2):
                            mm = accumulate(pe, full[:, n * P:(n + 1) * P], [
                                (wq2[:, k, n * P:(n + 1) * P], x1T[:, side(i), k, :]) for k in range(KD)])
                        mm.then_inc(done, 1)
                    elif kind == "S2":
                        if s2_at[(i, h)] == 0:
                            pe.wait_ge(k2_ready, (b + 1) * 2)
                            pe.wait_ge(k2_lo_ready, (b + 1) * 2)
                            pe.wait_ge(mrow_ready, b + 1)
                        m.wait(pe, it, m.emptied(("Q2", i, 0, 0)), m.claim_scores(s))
                        if i < BIAS_TILES:
                            pe.wait_ge(bias_masked, (b + 1) * BIAS_TILES)
                        for n in range(2):
                            h4 = slice(4 * n, 4 * n + 4)
                            products = exact_products([((q2_hi[:, side(i), h, :], q2_lo[:, side(i), h, :]),
                                                        (k2_hi[:, h, h4, :], k2_lo[:, h, h4, :]))])
                            if i < BIAS_TILES:
                                products.append((identf[:, :], bias[:, i, h * GH + 4 * n:h * GH + 4 * n + 4, :]))
                            products.append((ones2[:, :], spread(mrow[:, :], 1, [64, 4, KP])))
                            mm = accumulate(pe, psS[:, m.stage.slot[s][0], n, 0:4 * KP], products)
                        mm.then_inc(banks.scores_full[m.stage.slot[s][0]], 1)
                    elif kind == "T2":
                        pe.wait_ge(p2_ready, b * len(s2_at) + s2_at[(i, h)] + 1)
                        for n3, (j, n) in enumerate(transpose_groups(kind, i)):
                            m.wait(pe, it, m.claim(s + (n3,)))
                            for c in range(j, j + n):
                                rows = min(P, GK - c * P)
                                mm = pe.transpose(bank(m, s + (n3,))[0:rows, (c - j) * P:(c - j + 1) * P],
                                                  p2[:, side(i), h, c * P:c * P + rows], identf[:, :])
                            mm.then_inc(banks.ring_full[m.stage.ring[s + (n3,)][0]], 1)
                    elif kind == "PV2":
                        m.wait(pe, it, *need, *[m.emptied(("T2", i, n, n3)) for n in range(2) for n3 in range(2)])
                        for n in range(2):
                            for c in range(NCH):
                                rows, at = min(P, GK - c * P), (n * GH + CHUNK_HEAD[c]) * (HD2 + 1)
                                mm = pe.matmul(full[:, at:at + 3 * (HD2 + 1)], p2T[0:rows, side(i), n, c, :],
                                               v2[0:rows, n, 3 * c:3 * c + 3, :], start=(n == 0 and c == 0),
                                               stop=(n == 1 and c == NCH - 1), skip_group_check=True)
                        mm.then_inc(done, 1)

            over_stages(pe, walk)


def mixture(nc, a, logits, x2r, weight, slot_g):
    with ExitStack() as ctx:
        def sem(name):
            return ctx.enter_context(nc.semaphore(name))

        def sb(name, shape, dt=F32):
            return ctx.enter_context(nc.sbuf_tensor(name, list(shape), dt))

        before_f = sb("before_f", [P, P])
        before, ones, iota = sb("before_sb", [P, P], BF16), sb("ones_sb", [P, P], BF16), sb("iota_sb", [P, NE])
        top, total, first, rank, keep, base, prob = (sb(n, [P, TT]) for n in (
            "top", "total", "first", "rank", "keep", "base", "prob"))
        shifted, ex, cand, picked = (sb(n, [P, TT, NE]) for n in ("shifted", "exp_l", "cand", "picked"))
        chosen = sb("chosen", [P, TT, NE], BF16)
        slot_s = sb("slot_s", [P, TT], I32)
        psR = ctx.enter_context(nc.psum_tensor("rank_bank", [P, TT, NE], F32))
        ld_c, shifted_ready, exp_ready, chosen_ready, ranked, slots_ready, sent, linked, order_ready = (sem(n) for n in (
            "r_ld_c", "shifted_ready", "exp_ready", "chosen_ready", "ranked", "slots_ready", "rows_sent",
            "router_linked", "order_ready"))

        identf = sb("identf_e", [P, P])
        xe = sb("xe", [P, 2, 3, D])
        xe_hi, xe_lo = sb("xe_hi", [P, KD, CAP], F32R), sb("xe_lo", [P, KD, CAP], F32R)
        w1s, w2s = sb("w1_in", [P, 2, KD, DFF]), sb("w2_in", [P, FC, D])
        w1h, w1l = sb("w1_hi", [P, 2, KD, DFF], F32R), sb("w1_lo", [P, 2, KD, DFF], F32R)
        w2h, w2l = sb("w2_hi", [P, 2, FC, D], F32R), sb("w2_lo", [P, 2, FC, D], F32R)
        hid = sb("hid", [P, FC, CAP])
        hid_hi, hid_lo = sb("hid_hi", [P, 2, FC, CAP], F32R), sb("hid_lo", [P, 2, FC, CAP], F32R)
        ye = sb("ye", [P, 3, D])
        psX = ctx.enter_context(nc.psum_tensor("rows_banks", [P, 2, 512], F32))
        psH = ctx.enter_context(nc.psum_tensor("hidden_banks", [P, 3, 512], F32))
        psY = ctx.enter_context(nc.psum_tensor("out_banks", [P, 2, 512], F32))
        HB = 3
        ld_ident, ld_w2 = sem("e_ld_ident"), sem("ld_w2")
        ld_w1, ld_xe = [sem(f"ld_w1_{u}") for u in range(2)], [sem(f"ld_xe_{u}") for u in range(2)]
        w1_hi_done, w1_split, w2_hi_done, w2_split = (sem(n) for n in ("w1_hi_done", "w1_split", "w2_hi_done", "w2_split"))
        rows_full, rows_hi, rows_split = sem("rows_full"), sem("rows_hi"), sem("rows_split")
        hidden_full, gelu_done, hidden_hi, hidden_split = (sem(n) for n in ("hidden_full", "gelu_done", "hidden_hi", "hidden_split"))
        out_full, out_copied, st_ye = (sem(n) for n in ("out_full", "out_copied", "st_ye"))
        ld_x2 = [sem(f"r_ld_x2_{b}") for b in range(B)]
        block = ctx.enter_context(nc.Block())

        def over_experts(eng, body):
            body(0, 0, 0)
            with eng.Fori(0, NE // 2 - 1) as j:
                body(j * 2 + 1, 1, j)
                body(j * 2 + 2, 0, j + 1)
            body(NE - 1, 1, NE // 2 - 1)

        def is_expert(e, n):
            return isinstance(e, int) and e == n

        @block.sync
        def _(sp):
            def load_w1(e, u):
                sp.dma_start(w1s[:, u], a["w1"][e].rearrange("(k p) f -> p k f", p=P)).then_inc(ld_w1[u], 16)

            def load_w2(e):
                sp.dma_start(w2s[:, :, :], a["w2"][e].rearrange("(f p) d -> p f d", p=P)).then_inc(ld_w2, 16)

            def load_rows(e, u):
                sp.dma_start(xe[:, u, 0:2, :], a["xde"][e][0:2 * P].rearrange("(t p) d -> p t d", p=P)).then_inc(ld_xe[u], 16)
                sp.dma_start(xe[0:CAP - 2 * P, u, 2, :], a["xde"][e][2 * P:CAP]).then_inc(ld_xe[u], 16)

            for t, name in ((before_f, "before"), (iota, "iota")):
                sp.dma_start(t[:, :], a[name]).then_inc(ld_c, 16)
            for b in range(B):
                sp.dma_start(x2r[:, b * NT:(b + 1) * NT, :],
                             a["x2d"][b].rearrange("(t p) d -> p t d", p=P)).then_inc(ld_x2[b], 16)
            sp.dma_start(identf[:, :], a["identf"]).then_inc(ld_ident, 16)
            load_w1(0, 0)
            load_w1(1, 1)
            load_w2(0)
            sp.wait_ge(sent, 16 * TT)
            load_rows(0, 0)
            load_rows(1, 1)
            with sp.Fori(0, NE // 2 - 1) as j:
                for u in range(2):
                    e = j * 2 + u
                    sp.wait_ge(w1_split, (e + 1) * KD)
                    load_w1(e + 2, u)
                    sp.wait_ge(rows_full, (e + 1) * 2)
                    load_rows(e + 2, u)
                    sp.wait_ge(w2_split, (e + 1) * 2)
                    load_w2(e + 1)
            sp.wait_ge(w2_split, (NE - 1) * 2)
            load_w2(NE - 1)

        @block.scalar
        def _(act):
            def w1_hi(e, u, half):
                act.wait_ge(ld_w1[u], (half + 1) * 16)
                for k in range(KD):
                    nc.scalar.copy(w1h[:, u, k, :], w1s[:, u, k, :]).then_inc(w1_hi_done, 1)

            def w2_hi(e, u):
                act.wait_ge(ld_w2, (e + 1) * 16)
                for n in range(2):
                    f = slice(n * FC // 2, (n + 1) * FC // 2)
                    nc.scalar.copy(w2h[:, u, f, :], w2s[:, f, :]).then_inc(w2_hi_done, 1)

            def xe_high(e):
                for k in range(KD):
                    act.wait_ge(rows_full, e * 2 + k + 1)
                    nc.scalar.copy(xe_hi[:, k, :], psX[:, k, 0:CAP]).then_inc(rows_hi, 1)

            def body(e, u, half):
                for f in range(FC):
                    act.wait_ge(hidden_full, e * FC + f + 1)
                    if not is_expert(e, 0):
                        act.wait_ge(hidden_split, (e - 1) * FC + f + 1)
                    nc.scalar.activation(hid[:, f, :], psH[:, f % HB, 0:CAP], ACT.Gelu_apprx_tanh).then_inc(gelu_done, 1)
                if not is_expert(e, NE - 1):
                    xe_high(e + 1)
                    w1_hi(e + 1, 1 - u, half + u)
                w2_hi(e, u)

            act.wait_ge(shifted_ready, 1)
            nc.scalar.activation(ex[:, :, :], shifted[:, :, :], ACT.Exp).then_inc(exp_ready, 1)
            w1_hi(0, 0, 0)
            xe_high(0)
            over_experts(act, body)

        @block.vector
        def _(dve):
            def w1_lo(e, u, k):
                dve.wait_ge(w1_hi_done, e * KD + k + 1)
                nc.vector.tensor_tensor(w1l[:, u, k, :], w1s[:, u, k, :], w1h[:, u, k, :].bitcast(F32),
                                        ALU.subtract).then_inc(w1_split, 1)

            def w2_lo(e, u, n):
                f = slice(n * FC // 2, (n + 1) * FC // 2)
                dve.wait_ge(w2_hi_done, e * 2 + n + 1)
                nc.vector.tensor_tensor(w2l[:, u, f, :], w2s[:, f, :], w2h[:, u, f, :].bitcast(F32),
                                        ALU.subtract).then_inc(w2_split, 1)

            def xe_low(e):
                for k in range(KD):
                    dve.wait_ge(rows_hi, e * 2 + k + 1)
                    nc.vector.tensor_tensor(xe_lo[:, k, :], psX[:, k, 0:CAP], xe_hi[:, k, :].bitcast(F32),
                                            ALU.subtract).then_inc(rows_split, 1)

            def copy_out(e, u, t):
                dve.wait_ge(out_full, e * 3 + t + 1)
                if t == 0 and not is_expert(e, 0):
                    dve.wait_ge(st_ye, e * 32)
                nc.vector.tensor_copy(ye[:, t, :], psY[:, (u + t) % 2, 0:D]).then_inc(out_copied, 1)

            def body(e, u, half):
                first, last = is_expert(e, 0), is_expert(e, NE - 1)
                for f in range(FC):
                    dve.wait_ge(gelu_done, e * FC + f + 1)
                    nc.vector.tensor_copy(hid_hi[:, u, f, :], hid[:, f, :]).then_inc(hidden_hi, 1)
                    dve.wait_ge(hidden_hi, e * FC + f + 1)
                    nc.vector.tensor_tensor(hid_lo[:, u, f, :], hid[:, f, :], hid_hi[:, u, f, :].bitcast(F32),
                                            ALU.subtract).then_inc(hidden_split, 1)
                if not last:
                    xe_low(e + 1)
                for n in range(3):
                    if n < KD and not last:
                        w1_lo(e + 1, 1 - u, n)
                    if n:
                        w2_lo(e, u, n - 1)
                    if not first:
                        copy_out(e - 1, 1 - u, n)

            links = 0

            def link(ins):
                nonlocal links
                links += 1
                ins.then_inc(linked, 1)
                dve.wait_ge(linked, links)

            nc.vector.memset(ones[:, :], 1.0).then_inc(order_ready, 1)
            L = logits[:, :, :]
            wide = [P, TT, NE]
            link(nc.vector.tensor_reduce(top[:, :], L, AX_X, ALU.max))
            nc.vector.tensor_tensor(shifted[:, :, :], L, spread(top[:, :], 2, wide), ALU.subtract).then_inc(shifted_ready, 1)
            link(nc.vector.tensor_tensor(picked[:, :, :], L, spread(top[:, :], 2, wide), ALU.is_ge))
            dve.wait_ge(ld_c, 32)
            link(nc.vector.scalar_tensor_tensor(out=cand[:, :, :], in0=picked[:, :, :], scalar=-float(NE),
                                                in1=spread(iota[:, :], 1, wide), op0=ALU.mult, op1=ALU.add))
            link(nc.vector.tensor_reduce(first[:, :], cand[:, :, :], AX_X, ALU.min))
            nc.vector.tensor_tensor(chosen[:, :, :], cand[:, :, :], spread(first[:, :], 2, wide),
                                    ALU.is_equal).then_inc(chosen_ready, 1)
            nc.vector.tensor_copy(before[:, :], before_f[:, :]).then_inc(order_ready, 1)
            dve.wait_ge(exp_ready, 1)
            link(nc.vector.tensor_reduce(total[:, :], ex[:, :, :], AX_X, ALU.add))
            link(nc.vector.reciprocal(prob[:, :], total[:, :]))
            dve.wait_ge(ranked, 1)
            dve.wait_ge(chosen_ready, 1)
            link(nc.vector.tensor_tensor(picked[:, :, :], psR[:, :, :], chosen[:, :, :], ALU.mult))
            link(nc.vector.tensor_reduce(rank[:, :], picked[:, :, :], AX_X, ALU.add))
            link(nc.vector.tensor_scalar(keep[:, :], rank[:, :], float(CAP), None, ALU.is_lt))
            link(nc.vector.tensor_tensor(weight[:, :], prob[:, :], keep[:, :], ALU.mult))
            far = float(2 * NE * CAP)
            link(nc.vector.scalar_tensor_tensor(out=base[:, :], in0=first[:, :], scalar=float(CAP), in1=rank[:, :],
                                                op0=ALU.mult, op1=ALU.add))
            link(nc.vector.scalar_tensor_tensor(out=base[:, :], in0=keep[:, :], scalar=-far, in1=base[:, :],
                                                op0=ALU.mult, op1=ALU.add))
            nc.vector.tensor_scalar(slot_s[:, :], base[:, :], far + NE * CAP, None, ALU.add).then_inc(slots_ready, 1)
            nc.vector.tensor_scalar(slot_g[:, :], base[:, :], far + NE * CAP, float(NE * CAP - 1), ALU.add,
                                    ALU.min).then_inc(slots_ready, 1)
            for k in range(KD):
                w1_lo(0, 0, k)
            xe_low(0)
            over_experts(dve, body)
            for t in range(3):
                copy_out(NE - 1, 1, t)

        @block.gpsimd
        def _(pool):
            pool.wait_ge(slots_ready, 2)
            for t in range(TT):
                if t % NT == 0:
                    pool.wait_ge(ld_x2[t // NT], 16)
                nc.gpsimd.indirect_dma_start(a["xd"], bass.IndirectOffsetOnAxis(ap=slot_s[:, t:t + 1], axis=0),
                                             x2r[:, t, :], None, bounds_check=NE * CAP - 1,
                                             oob_is_err=False).then_inc(sent, 16)
            with pool.Fori(0, NE) as e:
                pool.wait_ge(out_copied, (e + 1) * 3 + 2)
                pool.dma_start(a["yde"][e][0:2 * P].rearrange("(t p) d -> p t d", p=P), ye[:, 0:2, :]).then_inc(st_ye, 16)
                pool.dma_start(a["yde"][e][2 * P:CAP], ye[3 * P - CAP:P, 2, :]).then_inc(st_ye, 16)
            pool.wait_ge(st_ye, NE * 32)

        @block.tensor
        def _(pe):
            def rows(e, u, half):
                pe.wait_ge(ld_xe[u], (half + 1) * 32)
                if not is_expert(e, 0):
                    pe.wait_ge(rows_split, e * 2)
                for k in range(KD):
                    for t, (at, n) in enumerate(TOK_TILES):
                        mm = pe.transpose(psX[:, k, at:at + n], xe[0:n, u, t, k * P:(k + 1) * P], identf[0:n, 0:n])
                    mm.then_inc(rows_full, 1)

            def second(e, u):
                pe.wait_ge(w2_split, (e + 1) * 2)
                pe.wait_ge(hidden_split, (e + 1) * FC)
                for t, at in enumerate((0, P, CAP - P)):
                    n = (u + t) % 2
                    pe.wait_ge(out_copied, e * 3 + t + 1)
                    accumulate(pe, psY[:, n, 0:D], exact_products(
                        [((hid_hi[:, u, f, at:at + P], hid_lo[:, u, f, at:at + P]), (w2h[:, u, f, :], w2l[:, u, f, :]))
                         for f in range(FC)])).then_inc(out_full, 1)

            def body(e, u, half):
                pe.wait_ge(w1_split, (e + 1) * KD)
                pe.wait_ge(rows_split, (e + 1) * 2)
                for f in range(FC):
                    w = slice(f * P, (f + 1) * P)
                    if not (is_expert(e, 0) and f < HB):
                        pe.wait_ge(gelu_done, e * FC + (f + 1 - HB if f >= HB else 0))
                    mm = accumulate(pe, psH[:, f % HB, 0:CAP], exact_products(
                        [((w1h[:, u, k, w], w1l[:, u, k, w]), (xe_hi[:, k, :], xe_lo[:, k, :])) for k in range(KD)]))
                    mm.then_inc(hidden_full, 1)
                if not is_expert(e, NE - 1):
                    rows(e + 1, 1 - u, half + u)
                if not is_expert(e, 0):
                    second(e - 1, 1 - u)

            pe.wait_ge(order_ready, 2)
            pe.wait_ge(chosen_ready, 1)
            nc.tensor.matmul(psR[:, :, :], before[:, :], chosen[:, :, :], start=True, stop=False)
            for t in range(TT - 1):
                mm = nc.tensor.matmul(psR[:, t + 1:TT, :], ones[:, :],
                                      chosen[:, t:t + 1, :].broadcast_to([P, TT - 1 - t, NE]),
                                      start=False, stop=(t == TT - 2))
            mm.then_inc(ranked, 1)
            pe.sem_inc(out_copied, 2)
            pe.wait_ge(ld_ident, 16)
            rows(0, 0, 0)
            over_experts(pe, body)
            second(NE - 1, 1)


def combine(nc, a, x2r, weight, slot_g):
    with ExitStack() as ctx:
        def sem(name):
            return ctx.enter_context(nc.semaphore(name))

        def sb(name, shape, dt=F32):
            return ctx.enter_context(nc.sbuf_tensor(name, list(shape), dt))

        PER, AHEAD = 4, 8
        got = sb("got", [P, TT, D])
        mhalf = sb("minus_half_c", [P, 1])
        stats, mv = sb("stats_c", [P, TT, 6]), sb("mean_var_c", [P, TT, 2])
        less, vpe, rstd, shift = (sb(n, [P, TT]) for n in ("minus_mean", "var_eps_c", "rstd_c", "shift_c"))
        halves, summed, stats_done, stats_ready, less_done, var_ready, rstd_ready, shift_ready, normed, st_out = (sem(n) for n in (
            "half_set", "summed", "stats_done", "c_stats_ready", "less_done", "c_var_ready", "c_rstd_ready", "shift_ready", "normed", "st_out"))
        landed = [sem(f"landed{n}") for n in range(TT)]
        block = ctx.enter_context(nc.Block())

        @block.gpsimd
        def _(pool):
            nc.gpsimd.memset(mhalf[:, :], -0.5).then_inc(halves, 1)
            pool.wait_ge(halves, 1)
            for t in range(TT + AHEAD):
                if t < TT:
                    nc.gpsimd.indirect_dma_start(got[:, t, :], None, a["yd"],
                                                 bass.IndirectOffsetOnAxis(ap=slot_g[:, t:t + 1], axis=0),
                                                 ).then_inc(landed[t], 16)
                n, rest = divmod(t - AHEAD + 1, PER)
                if n < 1 or rest:
                    continue
                s = slice((n - 1) * PER, n * PER)
                pool.wait_ge(var_ready, n)
                nc.gpsimd.tensor_tensor(rstd[:, s], vpe[:, s], mhalf[:, :].broadcast_to([P, PER]), ALU.pow).then_inc(rstd_ready, 1)

        @block.vector
        def _(dve):
            for t in range(TT + AHEAD):
                if t < TT:
                    dve.wait_ge(landed[t], 16)
                    nc.vector.scalar_tensor_tensor(out=x2r[:, t, :], in0=got[:, t, :], scalar=weight[:, t:t + 1],
                                                   in1=x2r[:, t, :], op0=ALU.mult, op1=ALU.add).then_inc(summed, 1)
                if 1 <= t <= TT:
                    dve.wait_ge(summed, t)
                    nc.vector.bn_stats(stats[:, t - 1, :], x2r[:, t - 1, :]).then_inc(stats_done, 1)
                if 2 <= t <= TT + 1:
                    dve.wait_ge(stats_done, t - 1)
                    nc.vector.bn_aggr(mv[:, t - 2, :], stats[:, t - 2, :]).then_inc(stats_ready, 1)
                    n, rest = divmod(t - 1, PER)
                    if not rest:
                        s = slice((n - 1) * PER, n * PER)
                        dve.wait_ge(stats_ready, n * PER)
                        nc.vector.tensor_scalar(less[:, s], mv[:, s, 0], -1.0, None, ALU.mult).then_inc(less_done, 1)
                        nc.vector.tensor_scalar(vpe[:, s], mv[:, s, 1], EPS, None, ALU.add).then_inc(var_ready, 1)
                n, rest = divmod(t - AHEAD + 1, PER)
                if n >= 1 and not rest:
                    s = slice((n - 1) * PER, n * PER)
                    dve.wait_ge(less_done, n)
                    dve.wait_ge(rstd_ready, n)
                    nc.vector.tensor_tensor(shift[:, s], less[:, s], rstd[:, s], ALU.mult).then_inc(shift_ready, 1)

        @block.scalar
        def _(act):
            for t in range(TT):
                act.wait_ge(shift_ready, t // PER + 1)
                nc.scalar.activation(got[:, t, :], x2r[:, t, :], ACT.Identity, bias=shift[:, t:t + 1],
                                     scale=rstd[:, t:t + 1]).then_inc(normed, 1)

        @block.sync
        def _(sp):
            for n in range(TT // PER):
                sp.wait_ge(normed, (n + 1) * PER)
                sp.dma_start(a["out"].rearrange("(t p) d -> p t d", p=P)[:, n * PER:(n + 1) * PER, :],
                             got[:, n * PER:(n + 1) * PER, :]).then_inc(st_out, 16)
            sp.wait_ge(st_out, 16 * (TT // PER))


def decoder_layer(nc, a):
    xd = nc.dram_tensor("dispatched_rows", (NE * CAP, D), F32)
    yd = nc.dram_tensor("expert_rows", (NE * CAP, D), F32)
    a = dict(a, xd=xd.ap(), yd=yd.ap(), x2d=nc.dram_tensor("x2_rows", (B, S, D), F32).ap(),
             xde=xd.ap().rearrange("(e c) d -> e c d", e=NE), yde=yd.ap().rearrange("(e c) d -> e c d", e=NE))
    with ExitStack() as ctx:
        logits = ctx.enter_context(nc.sbuf_tensor("logits", [P, TT, NE], F32))
        attention(nc, a, logits)
        x2r = ctx.enter_context(nc.sbuf_tensor("x2_tokens", [P, TT, D], F32))
        weight = ctx.enter_context(nc.sbuf_tensor("token_weight", [P, TT], F32))
        slot_g = ctx.enter_context(nc.sbuf_tensor("token_slot", [P, TT], I32))
        mixture(nc, a, logits, x2r, weight, slot_g)
        combine(nc, a, x2r, weight, slot_g)


def bucket(distance):
    import numpy as np
    half, exact = BUCKETS // 2, BUCKETS // 4
    far = np.abs(distance)
    step = np.log(np.maximum(far, 1).astype(np.float32) / np.float32(exact)) / np.float32(np.log(MAX_DIST / exact))
    large = np.minimum(exact + (step * np.float32(half - exact)).astype(np.int32), half - 1)
    return (distance > 0) * half + np.where(far < exact, far, large)


def constants():
    import numpy as np
    i = np.arange(P)
    r = np.arange(NCH * P).reshape(NCH, P)
    mine = (r // KP)[:, :, None] == (np.array(CHUNK_HEAD)[:, None, None] + np.arange(3))
    pad = np.zeros((64, KP), np.float32)
    pad[:, 0:KP - SK] = -1e30
    return {
        "identf": np.eye(P, dtype=np.float32),
        "causal": ((i[None, :] > i[:, None]) * -1e30).astype(np.float32),
        "before": (i[:, None] < i[None, :]).astype(np.float32),
        "iota": np.tile(np.arange(NE, dtype=np.float32), (P, 1)),
        "onehot": (bucket(KP - 1 - np.arange(HANKEL))[None, :] == np.arange(BUCKETS)[:, None]).astype(np.float32),
        "padneg": pad,
        "blk_k": np.repeat((i[:, None] // HD2 == np.arange(GH)).astype(np.float32)[:, :, None], KP, axis=2),
        "blk_v": np.ascontiguousarray(np.repeat(mine.transpose(1, 0, 2).reshape(P, NCH * 3, 1), HD2 + 1, axis=2).astype(np.float32)),
    }


def kernel(**inputs):
    import concourse.bacc as bacc
    import numpy as np
    from concourse.bass_utils import run_bass_kernel_spmd

    v = {k: np.asarray(x) for k, x in inputs.items()}

    def T(name):
        return np.ascontiguousarray(v[name].T)

    ctxT = np.zeros((B, D, GH, KP), np.float32)
    ctxT[:, :, :, KP - SK:] = v["ctx_1024"][:, ::-1].transpose(0, 2, 1)[:, :, None, :]
    mask = np.zeros((P, B, KP), bool)
    mask[:, :, KP - SK:] = v["mask_Bx1x1xS2_bk0"][:, 0, 0, ::-1][None]
    memz = np.zeros((2, HD1, 2, 2, HD1 + 1), np.float32)
    for h in range(H1):
        memz[h % 2, :, h // 2, h % 2, 0:HD1] = v["L0_attn_mem"][h]
        memz[h % 2, :, h // 2, h % 2, HD1:] = v["L0_attn_z"][h]
    rel = v["L0_xattn_rel_bias"].T
    arrays = {
        "x": v["x"], "xT": np.ascontiguousarray(v["x"].transpose(0, 2, 1)), "ctxT": ctxT.reshape(B, D, GK), "mask": mask,
        "WqT": T("L0_attn_Wq"), "WkT": T("L0_attn_Wk"), "WvT": T("L0_attn_Wv"), "Wo1T": T("L0_attn_Wo"),
        "bo": np.tile(v["L0_attn_bo"], (64, 1)), "betas": np.tile(v["L0_attn_betas"].reshape(1, H1), (P, 1)),
        "memz": memz.reshape(P, 2, 2, HD1 + 1),
        "Wq2T": T("L0_xattn_Wq"), "Wk2T": T("L0_xattn_Wk"), "Wv2T": T("L0_xattn_Wv"), "Wo2T": T("L0_xattn_Wo"),
        "rel": np.ascontiguousarray(np.stack([rel, np.tile(rel[BUCKETS // 2 - 1], (BUCKETS, 1))], axis=1)),
        "gateT": T("L0_ffn_gate_w"), "w1": v["L0_ffn_w1"], "w2": v["L0_ffn_w2"], **constants(),
    }
    nc = bacc.Bacc("TRN2", target_bir_lowering=False, num_devices=1)
    aps = {k: nc.dram_tensor(f"in_{k}", x.shape, mybir.dt.from_np(x.dtype), kind="ExternalInput").ap() for k, x in arrays.items()}
    aps["out"] = nc.dram_tensor("out_0", (NTOK, D), F32, kind="ExternalOutput").ap()
    decoder_layer(nc, aps)
    r = run_bass_kernel_spmd(nc, [{f"in_{k}": x for k, x in arrays.items()}], core_ids=[0])
    return r.results[0]["out_0"].reshape(B, S, D)
```

```python
from contextlib import ExitStack

import concourse.bass as bass
from concourse import mybir

F32 = mybir.dt.float32
F32R = mybir.dt.float32r
BF16 = mybir.dt.bfloat16
I32 = mybir.dt.int32
U8 = mybir.dt.uint8
ALU = mybir.AluOpType
ACT = mybir.ActivationFunctionType
AX_X = mybir.AxisListType.X

P = 128
B, S, D = 4, 1024, 256
NT = S // P
KD = D // P
H1, HD1 = 4, 64
H2, HD2 = 16, 16
SK, KP = 77, 78
GH = 8
GK = GH * KP
NCH = -(-GK // P)
TAIL = GK - (NCH - 1) * P
BUCKETS, MAX_DIST = 32, 128
BIAS_TILES = 2
HANKEL = BIAS_TILES * P + KP - 1
NE, DFF = 16, 1024
NTOK = B * S
TT = NTOK // P
CAP = NTOK * 5 // (NE * 4)
FC = DFF // P
EPS = 1e-5
NEG = -1e9
CHUNK_HEAD = [min(c * P // KP, GH - 3) for c in range(NCH)]
TOK_TILES = [(0, 128), (128, 128), (256, 64)]


PAIRS = [(NT - 1 - n, n) for n in range(NT // 2)]
ORDER = [i for pair in PAIRS for i in pair]


REST = {
    ("O", 0): (0.37, 1.21), ("C", 0): (0.55, 1.65), ("W", 0): (1.32, 1.98), ("N", 0): (2.4, 2.97),
    ("X", 0): (2.51, 3.08), ("Q2", 0): (3.5, 4.18), ("S2", 0): (4.05, 4.73), ("S2", 1): (4.71, 5.61),
    ("T2", 0): (5.09, 6.58), ("T2", 1): (6.75, 6.71), ("PV2", 0): (7.35, 7.48), ("C2", 0): (7.51, 8.25),
    ("W2", 0): (8.78, 9.01), ("N2", 0): (9.55, 9.68), ("X2", 0): (9.76, 9.79), ("G", 0): (10.31, 10.45),
}
AM_AT = (-2.0, -1.9)
NEXT_AT = [1.6, 2.47, 3.33, 4.21, 5.08, 5.94, 6.81, 7.68, 8.55, 9.42, 10.29, 11.16]
SPLIT_AT = (11.7, 19.7)
CONTEXT_AT = (12.0, 12.3)
T_LAG, PV_LAG = 1.55, 3.1
ROUTE_AT = {"RC": 9.5, "RE": 9.8, "R": 10.5, "RS": 11.1, "RW": 11.5}
ACT_LATER = {"S": -0.07}
VEC_LATER = {"N": -0.3}


def body_steps(with_next, later={}):
    units = [(i, h) for pair in PAIRS for h in range(H1) for i in pair]
    at = []
    for u, (i, h) in enumerate(units):
        at += [(u - 1, ("S", i, h)), (u - 1 + T_LAG, ("T", i, h)), (u - 1 + PV_LAG, ("PV", i, h))]
    for n, pair in enumerate(PAIRS):
        end = (n + 1) * len(pair) * H1
        for i, x in zip(pair, AM_AT):
            at.append((end + x, ("AM", i, 0)))
        for (kind, h), where in REST.items():
            at += [(end + x, (kind, i, h)) for i, x in zip(pair, where)]
    if with_next:
        steps = [("QK", t, n) for t in (2, 0, 3, 1) for n in range(2)] + [("V", p, 0) for p in range(4)]
        at += [(len(units) + x, s) for x, s in zip(NEXT_AT, steps)]
        at += [(x, ("XS", n, 0)) for n, x in enumerate(SPLIT_AT)]
        at += [(len(units) + x, s) for x, s in zip(CONTEXT_AT, (("V2", 0, 0), ("K2", 0, 0)))]
    if not with_next:
        at += [(8 * b + x, (kind, b, 0)) for b in range(B - 1) for kind, x in ROUTE_AT.items()]
    at.sort(key=lambda one: one[0] + later.get(one[1][0], 0))
    return [s for _, s in at]


def first_steps():
    return ([("XS", n, 0) for n in range(2)] + [("QK", t, n) for t in (2, 0, 3, 1) for n in range(2)]
            + [("V", p, 0) for p in range(4)] + [("V2", 0, 0), ("K2", 0, 0)])


def transpose_groups(kind, i):
    if kind == "T":
        return [(j, min(4, i + 1 - j)) for j in range(0, i + 1, 4)]
    return [(0, 4), (4, NCH - 4)]


LINKS = {"QK": 1, "K2": 5, "V2": 1, "S2": 1, "AM": 2, "O": 2, "W": 1, "W2": 1, "PV2": 1}


def links_of(step):
    kind, i, h = step
    return 0 if kind == "QK" and i >= 2 else LINKS.get(kind, 0)


class Stage:
    RING, SLOTS = 3, 2

    def __init__(self, steps_of, before=None, times=1):
        steps = self.steps = steps_of({})
        self.act_steps, self.vec_steps = steps_of(ACT_LATER), steps_of(VEC_LATER)
        self.ring, self.slot = {}, {}
        self.ring_rise, self.slot_rise = [0] * self.RING, [0] * self.SLOTS
        used, scored = 0, 0
        for s in steps:
            kind, i, h = s
            if kind in ("S", "S2"):
                n = scored % self.SLOTS
                self.slot[s] = (n, self.slot_rise[n])
                self.slot_rise[n] += 1
                scored += 1
            elif kind not in ("O", "PV", "N", "N2", "XS", "RC", "RE", "RS", "RW"):
                for g in range(len(transpose_groups(kind, i)) if kind in ("T", "T2") else 1):
                    n = used % self.RING
                    self.ring[s + (g,)] = (n, self.ring_rise[n])
                    self.ring_rise[n] += 1
                    used += 1
        self.links_rise = sum(links_of(s) for s in steps)
        if before is None:
            self.ring_base, self.slot_base, self.links_base = [0] * self.RING, [0] * self.SLOTS, 0
        else:
            self.ring_base = [x + times * y for x, y in zip(before.ring_base, before.ring_rise)]
            self.slot_base = [x + times * y for x, y in zip(before.slot_base, before.slot_rise)]
            self.links_base = before.links_base + times * before.links_rise


ON_SCALAR = [("T", 0), ("T2", 0), ("V", 0), ("C", 0), ("X", 0), ("Q2", 0), ("C2", 0), ("X2", 0)]


def on_scalar(key):
    kind, i, h, n = key
    return (kind, n) in ON_SCALAR


class Banks:

    def __init__(self, sem):
        self.ring_full = [sem(f"ring_full{n}") for n in range(Stage.RING)]
        self.ring_emptied = [sem(f"ring_emptied{n}") for n in range(Stage.RING)]
        self.scores_full = [sem(f"scores_full{n}") for n in range(Stage.SLOTS)]
        self.scores_emptied = [sem(f"scores_emptied{n}") for n in range(Stage.SLOTS)]


class Marks:

    def __init__(self, banks, stage):
        self.banks, self.stage = banks, stage

    def ring(self, sems, key, more):
        n, k = self.stage.ring[key]
        return sems[n], self.stage.ring_rise[n], self.stage.ring_base[n] + k + more

    def slot(self, sems, step, more):
        n, k = self.stage.slot[step]
        return sems[n], self.stage.slot_rise[n], self.stage.slot_base[n] + k + more

    def full(self, key):
        return self.ring(self.banks.ring_full, key, 1)

    def emptied(self, key):
        return self.ring(self.banks.ring_emptied, key, 1)

    def claim(self, key):
        return self.ring(self.banks.ring_emptied, key, 0)

    def scored(self, step):
        return self.slot(self.banks.scores_full, step, 1)

    def scores_read(self, step):
        return self.slot(self.banks.scores_emptied, step, 1)

    def claim_scores(self, step):
        return self.slot(self.banks.scores_emptied, step, 0)

    def before(self):
        return [(self.banks.ring_emptied[n], self.stage.ring_rise[n], self.stage.ring_base[n]) for n in range(Stage.RING)]

    def wait(self, eng, it, *marks):
        for one in {id(s): s for s, _, _ in marks}.values():
            rise, count = max((r, k) for s, r, k in marks if s is one)
            if count:
                eng.wait_ge(one, it * rise + count)


def spread(t, axis, shape):
    return t.unsqueeze(axis).broadcast_to(list(shape))


def exact_products(terms):
    out = []
    for (a_hi, a_lo), (b_hi, b_lo) in terms:
        out += [(a_hi, b_hi), (a_hi, b_lo), (a_lo, b_hi)]
    return out


def accumulate(eng, out, products):
    for n, (lhs, rhs) in enumerate(products):
        mm = eng.matmul(out, lhs, rhs, start=(n == 0), stop=(n == len(products) - 1))
    return mm


class Routing:

    def __init__(self, ctx, nc):
        def sb(name, shape, dt=F32):
            return ctx.enter_context(nc.sbuf_tensor(name, list(shape), dt))

        def sem(name):
            return ctx.enter_context(nc.semaphore(name))

        self.logits, self.weight, self.slot_g = sb("logits", [P, TT, NE]), sb("token_weight", [P, TT]), sb("token_slot", [P, TT], I32)
        self.before, self.ones, self.iota = sb("before_sb", [P, P], BF16), sb("ones_sb", [P, P], BF16), sb("iota_sb", [P, NE])
        self.top, self.total, self.first, self.rank, self.keep, self.base, self.far, self.prob = (sb(n, [P, NT]) for n in (
            "top", "total", "first", "rank", "keep", "base", "far", "prob"))
        self.chosen, self.slot_s = sb("chosen", [P, NT, NE], BF16), sb("slot_s", [P, NT], I32)
        self.counts = sb("counts", [P, B + 1, NE])
        self.shifted_ready, self.exp_ready, self.chosen_ready, self.slots_ready, self.sent, self.linked = (sem(n) for n in (
            "shifted_ready", "exp_ready", "chosen_ready", "slots_ready", "rows_sent", "route_linked"))
        self.links = 0

    def work_in(self, space):
        self.shifted, self.ex, self.picked, self.cand = (
            space[:, n * NT * NE:(n + 1) * NT * NE].rearrange("p (t e) -> p t e", e=NE) for n in range(4))
        self.ranks, self.mine = self.picked, self.cand

    def compare(self, nc, dve, b):
        L, wide = self.logits[:, b * NT:(b + 1) * NT, :], [P, NT, NE]
        self.link(dve, nc.vector.tensor_reduce(self.top[:, :], L, AX_X, ALU.max))
        nc.vector.tensor_tensor(self.shifted[:, :, :], L, spread(self.top[:, :], 2, wide), ALU.subtract).then_inc(self.shifted_ready, 1)
        self.link(dve, nc.vector.tensor_tensor(self.picked[:, :, :], L, spread(self.top[:, :], 2, wide), ALU.is_ge))

    def choose(self, nc, dve):
        wide = [P, NT, NE]
        self.link(dve, nc.vector.scalar_tensor_tensor(out=self.cand[:, :, :], in0=self.picked[:, :, :], scalar=-float(NE),
                                                      in1=spread(self.iota[:, :], 1, wide), op0=ALU.mult, op1=ALU.add))
        self.link(dve, nc.vector.tensor_reduce(self.first[:, :], self.cand[:, :, :], AX_X, ALU.min))
        nc.vector.tensor_tensor(self.chosen[:, :, :], self.cand[:, :, :], spread(self.first[:, :], 2, wide),
                                ALU.is_equal).then_inc(self.chosen_ready, 1)

    def exponentials(self, nc, act, b):
        act.wait_ge(self.shifted_ready, b + 1)
        nc.scalar.activation(self.ex[:, :, :], self.shifted[:, :, :], ACT.Exp).then_inc(self.exp_ready, 1)

    def ranking(self, nc, pe, b, out, done):
        pe.wait_ge(self.chosen_ready, b + 1)
        out = out[:, 0:(NT + 1) * NE].rearrange("p (t e) -> p t e", e=NE)
        nc.tensor.matmul(out[:, 0:NT, :], self.before[:, :], self.chosen[:, :, :], start=True, stop=False, skip_group_check=True)
        for t in range(NT):
            mm = nc.tensor.matmul(out[:, t + 1:NT + 1, :], self.ones[:, :],
                                  self.chosen[:, t:t + 1, :].broadcast_to([P, NT - t, NE]),
                                  start=False, stop=(t == NT - 1), skip_group_check=True)
        mm.then_inc(done, 1)

    def rank_tokens(self, nc, dve, b, bank, done):
        wide = [P, NT, NE]
        bank = bank[:, 0:(NT + 1) * NE].rearrange("p (t e) -> p t e", e=NE)
        self.link(dve, nc.vector.tensor_tensor(self.ranks[:, :, :], bank[:, 0:NT, :], spread(self.counts[:, b, :], 1, wide), ALU.add))
        nc.vector.tensor_tensor(self.counts[:, b + 1, :], bank[:, NT, :], self.counts[:, b, :], ALU.add).then_inc(done, 1)
        self.link(dve, nc.vector.tensor_tensor(self.mine[:, :, :], self.ranks[:, :, :], self.chosen[:, :, :], ALU.mult))
        self.link(dve, nc.vector.tensor_reduce(self.rank[:, :], self.mine[:, :, :], AX_X, ALU.add))
        self.link(dve, nc.vector.tensor_scalar(self.keep[:, :], self.rank[:, :], float(CAP), None, ALU.is_lt))

    def find_slots(self, nc, dve, b):
        tiles = slice(b * NT, (b + 1) * NT)
        past = float(2 * NE * CAP)
        self.link(dve, nc.vector.scalar_tensor_tensor(out=self.base[:, :], in0=self.first[:, :], scalar=float(CAP),
                                                      in1=self.rank[:, :], op0=ALU.mult, op1=ALU.add))
        self.link(dve, nc.vector.scalar_tensor_tensor(out=self.far[:, :], in0=self.keep[:, :], scalar=-past, in1=self.base[:, :],
                                                      op0=ALU.mult, op1=ALU.add))
        if b:
            dve.wait_ge(self.sent, b * NT * 16)
        nc.vector.tensor_scalar(self.slot_s[:, :], self.far[:, :], past + NE * CAP, None, ALU.add).then_inc(self.slots_ready, 1)
        self.link(dve, nc.vector.tensor_scalar(self.slot_g[:, tiles], self.far[:, :], past + NE * CAP, float(NE * CAP - 1),
                                               ALU.add, ALU.min))

    def weigh(self, nc, dve, b):
        tiles = slice(b * NT, (b + 1) * NT)
        dve.wait_ge(self.exp_ready, b + 1)
        self.link(dve, nc.vector.tensor_reduce(self.total[:, :], self.ex[:, :, :], AX_X, ALU.add))
        self.link(dve, nc.vector.reciprocal(self.prob[:, :], self.total[:, :]))
        self.link(dve, nc.vector.tensor_tensor(self.weight[:, tiles], self.prob[:, :], self.keep[:, :], ALU.mult))

    def send(self, nc, pool, b, xd, rows):
        pool.wait_ge(self.slots_ready, b + 1)
        for t in range(NT):
            nc.gpsimd.indirect_dma_start(xd, bass.IndirectOffsetOnAxis(ap=self.slot_s[:, t:t + 1], axis=0),
                                         rows[:, t, :], None, bounds_check=NE * CAP - 1, oob_is_err=False).then_inc(self.sent, 16)

    def link(self, dve, ins):
        self.links += 1
        ins.then_inc(self.linked, 1)
        dve.wait_ge(self.linked, self.links)


def attention(nc, a, routing):
    logits = routing.logits
    first = Stage(lambda later: first_steps())
    body = Stage(lambda later: body_steps(True, later), first)
    last = Stage(lambda later: body_steps(False, later), body, B - 1)
    unit = {s[1:]: u for u, s in enumerate(s for s in last.steps if s[0] == "S")}
    s2_at = {s[1:]: n for n, s in enumerate(s for s in last.steps if s[0] == "S2")}
    NU = len(unit)
    vecd = nc.dram_tensor("bias_vector", (H2, HANKEL), F32)
    biasd = nc.dram_tensor("bias_rows", (BIAS_TILES, P, H2, KP), F32)
    norm = {s: n for n, s in enumerate(s for s in last.steps if s[0] in ("W", "W2"))}

    with ExitStack() as ctx:
        def sem(name):
            return ctx.enter_context(nc.semaphore(name))

        def sb(name, shape, dt=F32):
            return ctx.enter_context(nc.sbuf_tensor(name, list(shape), dt))

        psS = ctx.enter_context(nc.psum_tensor("score_banks", [P, 2, 2, 512], F32))
        ring = [ctx.enter_context(nc.psum_tensor(f"ring_bank{n}", [P, 512], F32)) for n in range(Stage.RING)]
        psO = ctx.enter_context(nc.psum_tensor("output_bank", [P, 512], F32))

        identf, identb, causal = sb("identf_sb", [P, P]), sb("identb_sb", [P, P], BF16), sb("causal_sb", [P, P], BF16)
        w_hi, w_lo = sb("w_qkv_hi", [P, KD, 3 * D], F32R), sb("w_qkv_lo", [P, KD, 3 * D], F32R)
        wo1, wq2, wk2, wv2, wo2 = (sb(n, [P, KD, D]) for n in ("wo1", "wq2", "wk2", "wv2", "wo2"))
        gw = sb("gate_w", [P, KD, NE])
        memz = sb("memz_sb", [P, 2, 2, HD1 + 1])
        betas, g_e, g_d, g, omg = (sb(n, [P, H1]) for n in ("betas_sb", "exp_beta", "one_exp_beta", "gate", "one_gate"))
        bo = sb("bo_sb", [P, D])
        ones2 = sb("ones2", [64, P], F32R)
        blk_k, blk_v = sb("blk_k_sb", [P, GH]), sb("blk_v_sb", [P, NCH * 3])
        padneg, masku, maskf = sb("padneg_sb", [64, KP]), sb("mask_u8", [P, B, KP], U8), sb("mask_f", [P, B, KP])
        mneg, mneg_hi, mrow = sb("mneg", [64, KP]), sb("mneg_hi", [64, KP], F32R), sb("mrow", [64, KP], F32R)
        xT, x_hi, x_lo = sb("xT_sb", [P, KD, S]), sb("xT_hi", [P, KD, S], F32R), sb("xT_lo", [P, KD, S], F32R)
        qk_hi, qk_lo = sb("qk_hi", [P, 4, S], F32R), sb("qk_lo", [P, 4, S], F32R)
        sq, esq = sb("sigma_q", [P, 2, S]), sb("exp_q", [P, 512])
        V = sb("v_sb", [P, NT, D])
        xin = sb("x_in", [P, NT, D])
        x1, x2 = sb("x1_sb", [P, 2, D]), sb("x2_sb", [P, 2, D])
        ctxT = sb("ctxT_sb", [P, KD, GK])
        bias = sb("bias_sb", [P, BIAS_TILES, H2, KP])
        k2m, k2m_lo = sb("k2_masked", [P, 2, KP]), sb("k2_masked_lo", [P, 2, KP])
        k2m_r = sb("k2_masked_round", [P, 2, KP], F32R)
        k2_hi, k2_lo = sb("k2_hi", [P, 2, GH, KP], F32R), sb("k2_lo", [P, 2, GH, KP], F32R)
        v2 = sb("v2_blocks", [P, 2, NCH * 3, HD2 + 1])
        probs, probsT = sb("probs", [P, 2, S]), sb("probsT", [P, 2, NT, P])
        w_f = probs[:, :, 0:3 * D]
        spare = probsT[:, :, :, :].rearrange("p u j q -> p (u j q)")
        causal_f, before_f = spare[:, 0:P], spare[:, P + 2 * HANKEL + 3 * H2:2 * P + 2 * HANKEL + 3 * H2]
        rel = spare[0:BUCKETS, P + 2 * HANKEL:P + 2 * HANKEL + 2 * H2].rearrange("p (n h) -> p n h", n=2)
        reld = spare[0:BUCKETS, P + 2 * HANKEL + 2 * H2:P + 2 * HANKEL + 3 * H2]
        onehot, vec = (spare[0:n, P + k * HANKEL:P + (k + 1) * HANKEL] for k, n in enumerate((BUCKETS, H2)))
        p2, p2T = sb("probs2", [P, 2, 2, GK]), sb("probs2T", [P, 2, 2, NCH, P])
        negmax, rowsum, rrow = sb("negmax", [P, 4]), sb("rowsum", [P, 4, H1]), sb("rrow", [P, 2, H1])
        den, rden = sb("den", [P, 2, H1]), sb("rden", [P, 2, H1])
        am, c1, c1T = sb("mem_part", [P, 2, D]), sb("c1", [P, 2, D]), sb("c1T", [P, 2, KD, P])
        y = sb("y_sum", [P, 4, D])
        stats, mv, vpe, rstd = sb("stats", [P, 4, 6]), sb("mean_var", [P, 4, 2]), sb("var_eps", [P, 4]), sb("rstd", [P, 4])
        x1T, q2_hi, q2_lo = sb("x1T", [P, 2, KD, P]), sb("q2_hi", [P, 2, KD, P], F32R), sb("q2_lo", [P, 2, KD, P], F32R)
        max2, rden2 = sb("max2", [P, 2, GH]), sb("rden2", [P, 2, H2])
        c2, c2T, x2T = sb("c2", [P, 2, D]), sb("c2T", [P, 2, KD, P]), sb("x2T", [P, 2, KD, P])
        waiter, mhalf, eps, zero = sb("waiter", [1, 1]), sb("minus_half", [P, 1]), sb("eps", [P, 1]), sb("zero_rows", [P, 32])

        banks = Banks(sem)
        ld_w, ld_rel, ld_c, ld_xT, ld_x, ld_ctx, ld_bias = (sem(n) for n in (
            "ld_w", "ld_rel", "ld_c", "ld_xT", "ld_x", "ld_ctx", "ld_bias"))
        st_vec, st_bias, st_zero = (sem(n) for n in ("st_vec", "st_bias", "st_zero"))
        ld_rows = sem("ld_rows")
        st_x2, tile_turn = [sem(f"st_x2_{w}") for w in range(2)], sem("tile_turn")
        exp_beta, w_hi_done, w_scaled, w_ready, rel_ready, vec_full, vec_ready = (sem(n) for n in (
            "exp_beta_done", "w_hi_done", "w_scaled", "w_ready", "rel_ready", "vec_full", "vec_ready"))
        consts_ready, zero_done, x_hi_done, x_split, qk_copied, sigma_done = (sem(n) for n in (
            "consts_ready", "zero_done", "x_hi_done", "x_split", "qk_copied", "sigma_done"))
        mrow_ready, x_biased, bias_masked, k2_ready, k2_parts, k2_lo_ready, q2_hi_done, negmax_ready, pv_done = (sem(n) for n in (
            "mrow_ready", "x_biased", "bias_masked", "k2_ready", "k2_parts", "k2_lo_ready", "q2_hi_done", "negmax_ready", "pv_done"))
        c1_ready, c2_ready, x1_ready, x2_ready, p2_ready = (sem(n) for n in (
            "c1_ready", "c2_ready", "x1_ready", "x2_ready", "p2_ready"))
        stats_ready, rstd_ready, vec_done, setup_done, var_ready, pool_set = (sem(n) for n in (
            "stats_ready", "rstd_ready", "vec_done", "setup_done", "var_ready", "pool_set"))

        def scores(m, step):
            return psS[:, m.stage.slot[step][0], :, :].rearrange("p b c -> p (b c)")

        def bank(m, key):
            return ring[m.stage.ring[key][0]]

        def side(i):
            return ORDER.index(i) % 2

        def over_stages(eng, walk, settled=lambda: None):
            walk(Marks(banks, first), 0, None, 0)
            settled()
            with eng.Fori(0, B - 1) as b:
                walk(Marks(banks, body), b, b, b + 1)
            walk(Marks(banks, last), 0, B - 1, None)

        def blocks(t, n=KD):
            return t[:, 0:n * P].rearrange("p (j q) -> p j q", q=P)

        LOADS_C = 15
        routing.work_in(esq)
        block = ctx.enter_context(nc.Block())

        @block.sync
        def _(sp):
            def load_xT(b):
                sp.dma_start(xT[:, :, :], a["xT"][b].rearrange("(k p) s -> p k s", p=P)).then_inc(ld_xT, 16)

            def load_ctx(b):
                sp.dma_start(ctxT[:, :, :], a["ctxT"][b].rearrange("(k p) s -> p k s", p=P)).then_inc(ld_ctx, 16)

            def load_x(b):
                sp.dma_start(xin[:, :, :], a["x"][b].rearrange("(t p) d -> p t d", p=P)).then_inc(ld_x, 16)

            def load_bias():
                sp.dma_start(bias[:, :, :, :], biasd.ap().rearrange("t p h k -> p t h k")).then_inc(ld_bias, 16)

            def store_x2(b, i):
                sp.wait_ge(x2_ready, b * NT + ORDER.index(i) + 1)
                sp.sem_inc(tile_turn, 1)
                sp.dma_start(a["x2d"][b][i * P:(i + 1) * P, :], x2[:, side(i), :]).then_inc(st_x2[side(i)], 16)

            for n, name in enumerate(("WqT", "WkT", "WvT")):
                sp.dma_start(w_f[:, :, n * D:(n + 1) * D], a[name].rearrange("(k p) n -> p k n", p=P)).then_inc(ld_w, 16)
            sp.dma_start(betas[:, :], a["betas"]).then_inc(ld_w, 16)
            sp.dma_start(memz[:, :, :, :], a["memz"]).then_inc(ld_w, 16)
            load_xT(0)
            sp.dma_start(rel[:, :, :], a["rel"]).then_inc(ld_rel, 16)
            sp.dma_start(onehot[:, :], a["onehot"]).then_inc(ld_rel, 16)
            for t, name in ((identf, "identf"), (causal_f, "causal"), (before_f, "before"), (routing.iota, "iota"), (masku, "mask"),
                            (padneg, "padneg"), (blk_k, "blk_k"), (blk_v, "blk_v"), (bo, "bo")):
                sp.dma_start(t[:], a[name]).then_inc(ld_c, 16)
            for t, name in ((wk2, "Wk2T"), (wv2, "Wv2T"), (wo1, "Wo1T"), (wq2, "Wq2T"), (wo2, "Wo2T"), (gw, "gateT")):
                sp.dma_start(t[:, :, :], a[name].rearrange("(k p) n -> p k n", p=P)).then_inc(ld_c, 16)
            load_ctx(0)
            load_x(0)
            sp.wait_ge(vec_ready, 1)
            sp.dma_start(vecd.ap(), vec[:, :]).then_inc(st_vec, 16)
            sp.wait_ge(st_vec, 16)
            for t in range(BIAS_TILES):
                hankel = bass.AP(vecd, t * P, [[1, P], [HANKEL, H2], [1, KP]])
                sp.dma_start(biasd.ap()[t], hankel).then_inc(st_bias, 16)
            sp.wait_ge(st_bias, 16 * BIAS_TILES)
            load_bias()
            sp.wait_ge(zero_done, 1)
            rows = a["xd"].rearrange("(n p r) (k d) -> n p (r k) d", p=P, r=4, d=32)
            for n in range(NE * CAP // (4 * P)):
                sp.dma_start(rows[n], zero[:, :].unsqueeze(1).broadcast_to([P, 4 * D // 32, 32])).then_inc(st_zero, 16)
            for w in range(2):
                sp.sem_inc(st_x2[w], 16)
            with sp.Fori(0, B - 1) as b:
                sp.wait_ge(x_split, (b + 1) * 2)
                load_xT(b + 1)
                sp.wait_ge(k2_ready, (b + 1) * 2)
                load_ctx(b + 1)
                for n, pair in enumerate(PAIRS):
                    if n == NT // 2 - 1:
                        sp.wait_ge(stats_ready, b * len(norm) + norm[("W", ORDER[-1], 0)] + 1)
                        load_x(b + 1)
                    for i in pair:
                        store_x2(b, i)
                    if n == BIAS_TILES - 1:
                        sp.wait_ge(p2_ready, b * len(s2_at) + s2_at[(BIAS_TILES - 1, 1)] + 1)
                        load_bias()
            sp.wait_ge(x_split, B * 2)
            for w in range(2):
                sp.wait_ge(st_x2[w], 16 * (1 + (B - 1) * NT // 2))
            for n, pair in enumerate(PAIRS):
                if n < B - 1:
                    if n:
                        sp.wait_ge(routing.sent, n * NT * 16)
                    sp.dma_start(xT[:, :, :].rearrange("p k (t d) -> p (k t) d", d=D),
                                 a["x2d"][n].rearrange("(t p) d -> p t d", p=P)).then_inc(ld_rows, 16)
                for i in pair:
                    store_x2(B - 1, i)
            for w in range(2):
                sp.wait_ge(st_x2[w], 16 * (1 + B * NT // 2))
            sp.wait_ge(st_zero, 16 * (NE * CAP // (4 * P)))

        @block.gpsimd
        def _(pool):
            nc.gpsimd.memset(mhalf[:, :], -0.5).then_inc(pool_set, 1)
            nc.gpsimd.memset(eps[:, :], EPS).then_inc(pool_set, 1)
            pool.wait_ge(pool_set, 2)
            pool.wait_ge(consts_ready, 1)

            def batch(b, behind):
                pool.wait_ge(ld_x, (b + 1) * 16)
                nc.gpsimd.tensor_tensor(xin[:, :, :], xin[:, :, :], spread(bo[:, :], 1, [P, NT, D]), ALU.add).then_inc(x_biased, 1)
                pool.wait_ge(k2_parts, b + 1)
                for n in range(2):
                    nc.gpsimd.tensor_tensor(k2_lo[:, n, :, :], spread(k2m_lo[:, n, :], 1, [P, GH, KP]),
                                            spread(blk_k[:, :], 2, [P, GH, KP]), ALU.mult).then_inc(k2_lo_ready, 1)
                pool.wait_ge(ld_bias, (b + 1) * 16)
                for t in range(BIAS_TILES):
                    mask = maskf[:, bass.ds(b, 1), :].broadcast_to([P, H2, KP])
                    nc.gpsimd.tensor_tensor(bias[:, t], bias[:, t], mask, ALU.mult).then_inc(bias_masked, 1)
                for s, n in norm.items():
                    w = 2 * (s[0] == "W2") + side(s[1])
                    pool.wait_ge(stats_ready, b * len(norm) + n + 1)
                    nc.gpsimd.tensor_tensor(vpe[:, w:w + 1], mv[:, w, 1:2], eps[:, :], ALU.add).then_inc(var_ready, 1)
                    pool.wait_ge(var_ready, b * len(norm) + n + 1)
                    nc.gpsimd.tensor_tensor(rstd[:, w:w + 1], vpe[:, w:w + 1], mhalf[:, :], ALU.pow).then_inc(rstd_ready, 1)
                    behind(s)

            def send_rows(s):
                kind, i, h = s
                n = ORDER.index(i) // 2
                if kind == "W" and side(i) == 1 and n < B - 1:
                    pool.wait_ge(ld_rows, (n + 1) * 16)
                    routing.send(nc, pool, n, a["xd"], xT[:, :, :].rearrange("p k (t d) -> p (k t) d", d=D))

            with pool.Fori(0, B - 1) as b:
                batch(b, lambda s: None)
            pool.wait_ge(st_zero, 16 * (NE * CAP // (4 * P)))
            batch(B - 1, send_rows)
            pool.wait_ge(routing.sent, (B - 1) * NT * 16)

        @block.scalar
        def _(act):
            act.wait_ge(ld_w, 80)
            nc.scalar.activation(g_e[:, :], betas[:, :], ACT.Exp, scale=-1.0).then_inc(exp_beta, 1)
            nc.scalar.copy(w_hi[:, :, 0:2 * D], w_f[:, :, 0:2 * D]).then_inc(w_hi_done, 1)
            act.wait_ge(w_scaled, KD)
            nc.scalar.copy(w_hi[:, :, 2 * D:], w_f[:, :, 2 * D:]).then_inc(w_hi_done, 1)

            def walk(m, it, b, nb):
                queries = 0
                for s in m.stage.act_steps:
                    kind, i, h = s
                    if kind == "XS":
                        if i == 0:
                            act.wait_ge(ld_xT, (nb + 1) * 16)
                        cols = slice(i * 512, (i + 1) * 512)
                        nc.scalar.copy(x_hi[:, :, cols], xT[:, :, cols]).then_inc(x_hi_done, 1)
                    elif kind == "QK":
                        cols = slice(h * 512, (h + 1) * 512)
                        m.wait(act, it, m.full(s + (0,)))
                        if i < 2:
                            if queries:
                                act.wait_ge(sigma_done, nb * 4 + queries)
                            nc.scalar.activation(esq[:, :], bank(m, s + (0,))[:, :], ACT.Exp).then_inc(qk_copied, 1)
                            queries += 1
                        nc.scalar.copy(qk_hi[:, i, cols], bank(m, s + (0,))[:, :]).then_inc(qk_copied, 1)
                    elif kind == "S":
                        u, nk = unit[(i, h)], (i + 1) * P
                        act.wait_ge(negmax_ready, b * NU + u + 1)
                        nc.scalar.activation(probs[:, u % 2, 0:nk], scores(m, s)[:, 0:nk], ACT.Exp,
                                             bias=negmax[:, u % 4:u % 4 + 1],
                                             accum_out=rowsum[:, ORDER.index(i) % 4, h:h + 1]).then_inc(
                                                 banks.scores_emptied[m.stage.slot[s][0]], 1)
                    elif kind == "RE":
                        routing.exponentials(nc, act, i)
                    elif kind == "S2":
                        m.wait(act, it, m.scores_read(s))
                        row = p2[:, side(i), h, :]
                        nc.scalar.activation(row, row, ACT.Exp).then_inc(p2_ready, 1)
                    for key in m.stage.ring:
                        if key[:3] != s or not on_scalar(key):
                            continue
                        m.wait(act, it, m.full(key))
                        full, done = bank(m, key), banks.ring_emptied[m.stage.ring[key][0]]
                        if kind == "V":
                            nc.scalar.copy(V[:, 2 * i:2 * i + 2, :],
                                           full[:, :].rearrange("p (t d) -> p t d", t=2)).then_inc(done, 1)
                        elif kind == "T":
                            j, n = transpose_groups(kind, i)[key[3]]
                            nc.scalar.copy(probsT[:, unit[(i, h)] % 2, j:j + n, :], blocks(full, n)).then_inc(done, 1)
                        elif kind == "T2":
                            j, n = transpose_groups(kind, i)[key[3]]
                            rows = TAIL if j else P
                            nc.scalar.copy(p2T[0:rows, side(i), h, j:j + n, :], blocks(full, n)[0:rows]).then_inc(done, 1)
                        else:
                            dst = {"C": c1T, "X": x1T, "C2": c2T, "Q2": q2_hi, "X2": x2T}[kind]
                            nc.scalar.copy(dst[:, side(i)], blocks(full)).then_inc(q2_hi_done if kind == "Q2" else done, 1)

            def settled():
                act.wait_ge(consts_ready, 1)
                act.wait_ge(st_vec, 16)

            over_stages(act, walk, settled)

        @block.vector
        def _(dve):
            links = 0

            def link(ins):
                nonlocal links
                links += 1
                ins.then_inc(setup_done, 1)
                dve.wait_ge(setup_done, links)

            dve.wait_ge(ld_rel, 32)
            nc.vector.tensor_tensor(reld[:, :], rel[:, 0, :], rel[:, 1, :], ALU.subtract).then_inc(rel_ready, 1)
            nc.vector.memset(zero[:, :], 0.0).then_inc(zero_done, 1)

            def w_low(n, part):
                dve.wait_ge(w_hi_done, n)
                nc.vector.tensor_tensor(w_lo[:, :, part], w_f[:, :, part], w_hi[:, :, part].bitcast(F32),
                                        ALU.subtract).then_inc(w_ready, 1)

            dve.wait_ge(exp_beta, 1)
            link(nc.vector.tensor_scalar(g_d[:, :], g_e[:, :], 1.0, None, ALU.add))
            link(nc.vector.reciprocal(g[:, :], g_d[:, :]))
            link(nc.vector.tensor_tensor(omg[:, :], g_e[:, :], g[:, :], ALU.mult))
            for k in range(KD):
                wv = w_f[:, k, 2 * D:3 * D].rearrange("p (h d) -> p h d", h=H1)
                nc.vector.tensor_tensor(wv, wv, spread(omg[:, :], 2, [P, H1, HD1]), ALU.mult).then_inc(w_scaled, 1)
            for n in range(2):
                mem = memz[:, n, :, 0:HD1]
                nc.vector.tensor_tensor(mem, mem, spread(g[:, 2 * n:2 * n + 2], 2, [P, 2, HD1]), ALU.mult).then_inc(w_ready, 1)
            w_low(1, slice(0, 2 * D))
            w_low(2, slice(2 * D, 3 * D))
            dve.wait_ge(vec_full, 1)
            nc.vector.tensor_copy(vec[:, :], psO[0:H2, 0:HANKEL]).then_inc(vec_ready, 1)

            def set_constants():
                dve.wait_ge(ld_c, 16 * LOADS_C)
                link(nc.vector.memset(ones2[:, :].bitcast(F32), 1.0))
                link(nc.vector.tensor_copy(identb[:, :], identf[:, :]))
                link(nc.vector.tensor_copy(causal[:, :], causal_f[:, :]))
                link(nc.vector.tensor_copy(routing.before[:, :], before_f[:, :]))
                link(nc.vector.memset(routing.ones[:, :], 1.0))
                link(nc.vector.memset(routing.counts[:, 0, :], 0.0))
                link(nc.vector.memset(mrow[:, :].bitcast(F32), 0.0))
                for n in range(2):
                    link(nc.vector.tensor_copy(v2[:, n, :, HD2], blk_v[:, :]))
                nc.vector.tensor_copy(maskf[:, :, :], masku[:, :, :]).then_inc(consts_ready, 1)
                dve.wait_ge(consts_ready, 1)

            def walk(m, it, b, nb):
                own, copied, queries = 0, 0, 0

                def linked(ins):
                    nonlocal own
                    own += 1
                    ins.then_inc(vec_done, 1)
                    dve.wait_ge(vec_done, it * m.stage.links_rise + (m.stage.links_base + own))

                for s in m.stage.vec_steps:
                    kind, i, h = s
                    key = s + (0,)
                    if key in m.stage.ring:
                        full, done = bank(m, key), banks.ring_emptied[m.stage.ring[key][0]]
                    if kind == "XS":
                        cols = slice(i * 512, (i + 1) * 512)
                        dve.wait_ge(x_hi_done, nb * 2 + i + 1)
                        nc.vector.tensor_tensor(x_lo[:, :, cols], xT[:, :, cols], x_hi[:, :, cols].bitcast(F32),
                                                ALU.subtract).then_inc(x_split, 1)
                    elif kind == "QK":
                        cols = slice(h * 512, (h + 1) * 512)
                        copied += 2 if i < 2 else 1
                        dve.wait_ge(qk_copied, nb * 12 + copied)
                        if i < 2:
                            linked(nc.vector.tensor_scalar(sq[:, i, cols], full[:, :], 0.0, None, ALU.max))
                        nc.vector.tensor_tensor(qk_lo[:, i, cols], full[:, :], qk_hi[:, i, cols].bitcast(F32),
                                                ALU.subtract).then_inc(done, 1)
                        if i < 2:
                            nc.vector.scalar_tensor_tensor(out=sq[:, i, cols], in0=esq[:, :], scalar=1.0,
                                                           in1=sq[:, i, cols], op0=ALU.min, op1=ALU.add).then_inc(sigma_done, 1)
                    elif kind == "K2":
                        m.wait(dve, it, m.full(key))
                        nc.vector.tensor_tensor(k2m[:, :, :], full[:, 0:2 * KP].rearrange("p (g k) -> p g k", g=2),
                                                maskf[:, bass.ds(nb, 1), :].broadcast_to([P, 2, KP]), ALU.mult).then_inc(done, 1)
                        m.wait(dve, it, m.emptied(key))
                        linked(nc.vector.tensor_copy(k2m_r[:, :, :], k2m[:, :, :]))
                        nc.vector.tensor_tensor(k2m_lo[:, :, :], k2m[:, :, :], k2m_r[:, :, :].bitcast(F32),
                                                ALU.subtract).then_inc(k2_parts, 1)
                        for n in range(2):
                            nc.vector.tensor_tensor(k2_hi[:, n, :, :], spread(k2m_r[:, n, :].bitcast(F32), 1, [P, GH, KP]),
                                                    spread(blk_k[:, :], 2, [P, GH, KP]), ALU.mult).then_inc(k2_ready, 1)
                        mask = maskf[:, bass.ds(nb, 1), :].rearrange("p a k -> p (a k)")
                        linked(nc.vector.tensor_scalar(mneg[:, :], mask[0:64, :], 1.0, -NEG, ALU.subtract, ALU.mult))
                        linked(nc.vector.tensor_tensor(mneg[:, :], mneg[:, :], padneg[:, :], ALU.add))
                        linked(nc.vector.tensor_copy(mneg_hi[:, :], mneg[:, :]))
                        linked(nc.vector.tensor_copy(mrow[0:1, :], mneg[0:1, :]))
                        nc.vector.tensor_tensor(mrow[32:33, :], mneg[32:33, :], mneg_hi[32:33, :].bitcast(F32),
                                                ALU.subtract).then_inc(mrow_ready, 1)
                    elif kind == "Q2":
                        dve.wait_ge(q2_hi_done, b * NT + ORDER.index(i) + 1)
                        nc.vector.tensor_tensor(q2_lo[:, side(i)], blocks(full), q2_hi[:, side(i)].bitcast(F32),
                                                ALU.subtract).then_inc(done, 1)
                    elif kind == "V2":
                        if b is None:
                            set_constants()
                        m.wait(dve, it, m.full(key))
                        src = full[:, 0:2 * NCH * 3 * HD2].rearrange("p (g c d) -> p g c d", g=2, d=HD2)
                        for rows, lo, hi in ((P, 0, 3 * (NCH - 1)), (TAIL, 3 * (NCH - 1), 3 * NCH)):
                            ins = nc.vector.tensor_tensor(
                                v2[0:rows, :, lo:hi, 0:HD2], src[0:rows, :, lo:hi, :],
                                blk_v[0:rows, lo:hi].unsqueeze(1).unsqueeze(3).broadcast_to([rows, 2, hi - lo, HD2]), ALU.mult)
                            if lo == 0:
                                linked(ins)
                        ins.then_inc(done, 1)
                    elif kind == "S":
                        u = unit[(i, h)]
                        m.wait(dve, it, m.scored(s))
                        nc.vector.tensor_reduce(negmax[:, u % 4:u % 4 + 1], scores(m, s)[:, 0:(i + 1) * P], AX_X,
                                                ALU.max, negate=True).then_inc(negmax_ready, 1)
                    elif kind == "RC":
                        routing.compare(nc, dve, i)
                    elif kind == "RE":
                        routing.choose(nc, dve)
                    elif kind == "R":
                        m.wait(dve, it, m.full(key))
                        routing.rank_tokens(nc, dve, i, full, done)
                    elif kind == "RS":
                        routing.find_slots(nc, dve, i)
                    elif kind == "RW":
                        routing.weigh(nc, dve, i)
                    elif kind == "S2":
                        m.wait(dve, it, m.scored(s))
                        sc = psS[:, m.stage.slot[s][0], :, 0:4 * KP].rearrange("p b (h k) -> p b h k", h=4)
                        mx = max2[:, h, :].rearrange("p (b h) -> p b h", b=2)
                        linked(nc.vector.tensor_reduce(mx, sc, AX_X, ALU.max))
                        nc.vector.tensor_tensor(
                            p2[:, side(i), h, :].rearrange("p (b h k) -> p b h k", b=2, h=4), sc,
                            spread(mx, 3, [P, 2, 4, KP]), ALU.subtract).then_inc(banks.scores_emptied[m.stage.slot[s][0]], 1)
                    elif kind == "AM":
                        m.wait(dve, it, m.full(key))
                        src = full[:, 0:H1 * (HD1 + 1)].rearrange("p (h e) -> p h e", h=H1)
                        linked(nc.vector.tensor_scalar(den[:, side(i), :], src[:, :, HD1], 1e-6, None, ALU.add))
                        linked(nc.vector.reciprocal(rden[:, side(i), :], den[:, side(i), :]))
                        nc.vector.tensor_tensor(am[:, side(i), :].rearrange("p (h d) -> p h d", h=H1), src[:, :, 0:HD1],
                                                spread(rden[:, side(i), :], 2, [P, H1, HD1]), ALU.mult).then_inc(done, 1)
                    elif kind == "O":
                        w = side(i)
                        dve.wait_ge(pv_done, b * NU + unit[(i, H1 - 1)] + 1)
                        linked(nc.vector.reciprocal(rrow[:, w, :], rowsum[:, ORDER.index(i) % 4, :]))
                        linked(nc.vector.tensor_tensor(c1[:, w, :].rearrange("p (h d) -> p h d", h=H1),
                                                       psO[:, w * D:(w + 1) * D].rearrange("p (h d) -> p h d", h=H1),
                                                       spread(rrow[:, w, :], 2, [P, H1, HD1]), ALU.mult))
                        m.wait(dve, it, m.emptied(("AM", i, 0, 0)))
                        nc.vector.tensor_tensor(c1[:, w, :], c1[:, w, :], am[:, w, :], ALU.add).then_inc(c1_ready, 1)
                    elif kind in ("W", "W2"):
                        w = 2 * (kind == "W2") + side(i)
                        m.wait(dve, it, m.full(key))
                        if s == ("W", ORDER[0], 0):
                            dve.wait_ge(x_biased, b + 1)
                        residual = xin[:, i, :] if kind == "W" else x1[:, side(i), :]
                        nc.vector.tensor_tensor(y[:, w, :], full[:, 0:D], residual, ALU.add).then_inc(done, 1)
                        m.wait(dve, it, m.emptied(key))
                        linked(nc.vector.bn_stats(stats[:, w, :], y[:, w, :]))
                        nc.vector.memset(waiter[:, :], 0.0)
                        nc.vector.bn_aggr(mv[:, w, :], stats[:, w, :]).then_inc(stats_ready, 1)
                    elif kind in ("N", "N2"):
                        w = 2 * (kind == "N2") + side(i)
                        dve.wait_ge(rstd_ready, b * len(norm) + norm[("W" + kind[1:], i, 0)] + 1)
                        if kind == "N2":
                            dve.wait_ge(st_x2[side(i)], (b * (NT // 2) + (ORDER.index(i) // 2 + 1)) * 16)
                        nc.vector.tensor_scalar((x2 if kind == "N2" else x1)[:, side(i), :], y[:, w, :], mv[:, w, 0:1],
                                                rstd[:, w:w + 1], ALU.subtract, ALU.mult).then_inc(
                                                    x2_ready if kind == "N2" else x1_ready, 1)
                        if kind == "N":
                            dve.wait_ge(x1_ready, b * NT + ORDER.index(i) + 1)
                    elif kind == "PV2":
                        m.wait(dve, it, m.full(key))
                        src = full[:, 0:H2 * (HD2 + 1)].rearrange("p (h e) -> p h e", h=H2)
                        linked(nc.vector.reciprocal(rden2[:, side(i), :], src[:, :, HD2]))
                        nc.vector.tensor_tensor(c2[:, side(i), :].rearrange("p (h d) -> p h d", h=H2), src[:, :, 0:HD2],
                                                spread(rden2[:, side(i), :], 2, [P, H2, HD2]), ALU.mult).then_inc(done, 1)
                    elif kind == "G":
                        m.wait(dve, it, m.full(key))
                        at = logits[:, bass.ds(b * NT + i, 1), :].rearrange("p a e -> p (a e)")
                        nc.vector.tensor_copy(at, full[:, 0:NE]).then_inc(done, 1)
                    elif kind in ("C", "X", "C2", "X2"):
                        if not on_scalar(key):
                            m.wait(dve, it, m.full(key))
                            dst = {"C": c1T, "X": x1T, "C2": c2T, "X2": x2T}[kind]
                            nc.vector.tensor_copy(dst[:, side(i)], blocks(full)).then_inc(done, 1)
                    elif kind in ("T", "T2"):
                        for n3, (j, n) in enumerate(transpose_groups(kind, i)):
                            key = s + (n3,)
                            if on_scalar(key):
                                continue
                            m.wait(dve, it, m.full(key))
                            full, done = bank(m, key), banks.ring_emptied[m.stage.ring[key][0]]
                            if kind == "T":
                                nc.vector.tensor_copy(probsT[:, unit[(i, h)] % 2, j:j + n, :], blocks(full, n)).then_inc(done, 1)
                            else:
                                rows = TAIL if j else P
                                nc.vector.tensor_copy(p2T[0:rows, side(i), h, j:j + n, :], blocks(full, n)[0:rows]).then_inc(done, 1)
                assert own == m.stage.links_rise, (own, m.stage.links_rise)

            over_stages(dve, walk)

        @block.tensor
        def _(pe):
            pe.wait_ge(ld_rel, 32)
            pe.wait_ge(rel_ready, 1)
            nc.tensor.matmul(psO[0:H2, 0:HANKEL], reld[:, :], onehot[:, :], start=True, stop=True).then_inc(vec_full, 1)
            pe.wait_ge(w_ready, 4)

            def walk(m, it, b, nb):
                for s in m.stage.steps:
                    kind, i, h = s
                    key = s + (0,)
                    need = []
                    if key in m.stage.ring and kind not in ("T", "T2"):
                        need = [m.claim(key)]
                        full, done = bank(m, key), banks.ring_full[m.stage.ring[key][0]]
                    q = slice(i * P, (i + 1) * P)
                    if kind == "QK":
                        m.wait(pe, it, *need)
                        pe.wait_ge(x_split, nb * 2 + h + 1)
                        w, cols = slice(i * P, (i + 1) * P), slice(h * 512, (h + 1) * 512)
                        accumulate(pe, full[:, :], exact_products(
                            [((w_hi[:, k, w], w_lo[:, k, w]), (x_hi[:, k, cols], x_lo[:, k, cols])) for k in range(KD)]
                        )).then_inc(done, 1)
                    elif kind == "V":
                        m.wait(pe, it, *need)
                        w = slice(2 * D, 3 * D)
                        for n in range(2):
                            t = slice((2 * i + n) * P, (2 * i + n + 1) * P)
                            mm = accumulate(pe, full[:, n * D:(n + 1) * D], exact_products(
                                [((x_hi[:, k, t], x_lo[:, k, t]), (w_hi[:, k, w], w_lo[:, k, w])) for k in range(KD)]))
                        mm.then_inc(done, 1)
                    elif kind == "K2":
                        m.wait(pe, it, *need)
                        for n in range(2):
                            mm = accumulate(pe, full[:, n * KP:(n + 1) * KP], [
                                (wk2[:, k, n * P:(n + 1) * P], ctxT[:, k, 0:KP]) for k in range(KD)])
                        mm.then_inc(done, 1)
                    elif kind == "V2":
                        m.wait(pe, it, *need)
                        if b is None:
                            pe.wait_ge(ld_c, 16 * LOADS_C)
                        pe.wait_ge(ld_ctx, (nb + 1) * 16)
                        for n in range(2):
                            for c in range(NCH):
                                rows, at = min(P, GK - c * P), (n * NCH + c) * 3 * HD2
                                w = (n * GH + CHUNK_HEAD[c]) * HD2
                                mm = accumulate(pe, full[0:rows, at:at + 3 * HD2], [
                                    (ctxT[:, k, c * P:c * P + rows], wv2[:, k, w:w + 3 * HD2]) for k in range(KD)])
                        mm.then_inc(done, 1)
                    elif kind == "S":
                        if unit[(i, h)] == 0:
                            need = m.before()
                        m.wait(pe, it, m.claim_scores(s), *need)
                        r, t, nk = slice(h % 2 * HD1, h % 2 * HD1 + HD1), h // 2, (i + 1) * P
                        for c in range(0, nk, 512):
                            cols = slice(c, min(c + 512, nk))
                            last = cols.stop == nk
                            products = exact_products([((qk_hi[r, t, q], qk_lo[r, t, q]),
                                                        (qk_hi[r, 2 + t, cols], qk_lo[r, 2 + t, cols]))])
                            for n, (lhs, rhs) in enumerate(products):
                                mm = pe.matmul(scores(m, s)[:, cols], lhs, rhs, start=(n == 0),
                                               stop=(n == len(products) - 1 and not last))
                        pe.matmul(scores(m, s)[:, i * P:nk], identb[:, :], causal[:, :], start=False,
                                  stop=True).then_inc(banks.scores_full[m.stage.slot[s][0]], 1)
                    elif kind == "T":
                        m.wait(pe, it, m.scores_read(("S", i, h)))
                        u = unit[(i, h)]
                        for n3, (j, n) in enumerate(transpose_groups(kind, i)):
                            m.wait(pe, it, m.claim(s + (n3,)))
                            for jj in range(j, j + n):
                                mm = pe.transpose(bank(m, s + (n3,))[:, (jj - j) * P:(jj - j + 1) * P],
                                                  probs[:, u % 2, jj * P:(jj + 1) * P], identf[:, :])
                            mm.then_inc(banks.ring_full[m.stage.ring[s + (n3,)][0]], 1)
                    elif kind == "PV":
                        u = unit[(i, h)]
                        if h == 0 and ORDER.index(i) >= 2:
                            pe.wait_ge(c1_ready, b * NT + ORDER.index(i) - 1)
                        m.wait(pe, it, *[m.emptied(("T", i, h, n3)) for n3 in range(len(transpose_groups("T", i)))])
                        w = side(i) * D
                        d = slice(h * HD1, (h + 1) * HD1)
                        accumulate(pe, psO[:, w + h * HD1:w + (h + 1) * HD1], [(probsT[:, u % 2, j, :], V[:, j, d]) for j in range(i + 1)]).then_inc(pv_done, 1)
                    elif kind == "AM":
                        m.wait(pe, it, *need)
                        if i == ORDER[0]:
                            pe.wait_ge(sigma_done, (b + 1) * 4)
                        for n in range(2):
                            w = 2 * (HD1 + 1)
                            mm = pe.matmul(full[:, n * w:(n + 1) * w], sq[:, n, q], memz[:, n, :, :], start=True, stop=True)
                        mm.then_inc(done, 1)
                    elif kind in ("C", "X", "C2", "X2"):
                        src, ready = {"C": (c1, c1_ready), "X": (x1, x1_ready), "C2": (c2, None), "X2": (x2, x2_ready)}[kind]
                        if ready is None:
                            need.append(m.emptied(("PV2", i, 0, 0)))
                        m.wait(pe, it, *need)
                        if ready is not None:
                            pe.wait_ge(ready, b * NT + ORDER.index(i) + 1)
                        for k in range(KD):
                            mm = pe.transpose(full[:, k * P:(k + 1) * P], src[:, side(i), k * P:(k + 1) * P], identf[:, :])
                        mm.then_inc(done, 1)
                    elif kind in ("W", "W2", "G"):
                        before, lhs, rhs = {"W": ("C", c1T, wo1), "W2": ("C2", c2T, wo2), "G": ("X2", x2T, gw)}[kind]
                        m.wait(pe, it, *need, m.emptied((before, i, 0, 0)))
                        products = [(lhs[:, side(i), k, :], rhs[:, k, :]) for k in range(KD)]
                        accumulate(pe, full[:, 0:NE if kind == "G" else D], products).then_inc(done, 1)
                    elif kind == "Q2":
                        m.wait(pe, it, *need, m.emptied(("X", i, 0, 0)))
                        for n in range(2):
                            mm = accumulate(pe, full[:, n * P:(n + 1) * P], [
                                (wq2[:, k, n * P:(n + 1) * P], x1T[:, side(i), k, :]) for k in range(KD)])
                        mm.then_inc(done, 1)
                    elif kind == "S2":
                        if s2_at[(i, h)] == 0:
                            pe.wait_ge(k2_ready, (b + 1) * 2)
                            pe.wait_ge(k2_lo_ready, (b + 1) * 2)
                            pe.wait_ge(mrow_ready, b + 1)
                        m.wait(pe, it, m.emptied(("Q2", i, 0, 0)), m.claim_scores(s))
                        if i < BIAS_TILES:
                            pe.wait_ge(bias_masked, (b + 1) * BIAS_TILES)
                        for n in range(2):
                            h4 = slice(4 * n, 4 * n + 4)
                            products = exact_products([((q2_hi[:, side(i), h, :], q2_lo[:, side(i), h, :]),
                                                        (k2_hi[:, h, h4, :], k2_lo[:, h, h4, :]))])
                            if i < BIAS_TILES:
                                products.append((identf[:, :], bias[:, i, h * GH + 4 * n:h * GH + 4 * n + 4, :]))
                            products.append((ones2[:, :], spread(mrow[:, :], 1, [64, 4, KP])))
                            mm = accumulate(pe, psS[:, m.stage.slot[s][0], n, 0:4 * KP], products)
                        mm.then_inc(banks.scores_full[m.stage.slot[s][0]], 1)
                    elif kind == "R":
                        m.wait(pe, it, *need)
                        routing.ranking(nc, pe, i, full, done)
                    elif kind == "T2":
                        pe.wait_ge(p2_ready, b * len(s2_at) + s2_at[(i, h)] + 1)
                        for n3, (j, n) in enumerate(transpose_groups(kind, i)):
                            m.wait(pe, it, m.claim(s + (n3,)))
                            for c in range(j, j + n):
                                rows = min(P, GK - c * P)
                                mm = pe.transpose(bank(m, s + (n3,))[0:rows, (c - j) * P:(c - j + 1) * P],
                                                  p2[:, side(i), h, c * P:c * P + rows], identf[:, :])
                            mm.then_inc(banks.ring_full[m.stage.ring[s + (n3,)][0]], 1)
                    elif kind == "PV2":
                        m.wait(pe, it, *need, *[m.emptied(("T2", i, n, n3)) for n in range(2) for n3 in range(2)])
                        for n in range(2):
                            for c in range(NCH):
                                rows, at = min(P, GK - c * P), (n * GH + CHUNK_HEAD[c]) * (HD2 + 1)
                                mm = pe.matmul(full[:, at:at + 3 * (HD2 + 1)], p2T[0:rows, side(i), n, c, :],
                                               v2[0:rows, n, 3 * c:3 * c + 3, :], start=(n == 0 and c == 0),
                                               stop=(n == 1 and c == NCH - 1), skip_group_check=True)
                        mm.then_inc(done, 1)

            over_stages(pe, walk, lambda: pe.wait_ge(consts_ready, 1))


def mixture(nc, a, routing, x2r):
    with ExitStack() as ctx:
        def sem(name):
            return ctx.enter_context(nc.semaphore(name))

        def sb(name, shape, dt=F32):
            return ctx.enter_context(nc.sbuf_tensor(name, list(shape), dt))

        routing.work_in(sb("route_space", [P, 4 * NT * NE]))
        identf = sb("identf_e", [P, P])
        xe = sb("xe", [P, 2, 3, D])
        xe_hi, xe_lo = sb("xe_hi", [P, KD, CAP], F32R), sb("xe_lo", [P, KD, CAP], F32R)
        w1s, w2s = sb("w1_in", [P, 2, KD, DFF]), sb("w2_in", [P, FC, D])
        w1h, w1l = sb("w1_hi", [P, 2, KD, DFF], F32R), sb("w1_lo", [P, 2, KD, DFF], F32R)
        w2h, w2l = sb("w2_hi", [P, 2, FC, D], F32R), sb("w2_lo", [P, 2, FC, D], F32R)
        hid = sb("hid", [P, FC, CAP])
        hid_hi, hid_lo = sb("hid_hi", [P, 2, FC, CAP], F32R), sb("hid_lo", [P, 2, FC, CAP], F32R)
        ye = sb("ye", [P, 3, D])
        psX = ctx.enter_context(nc.psum_tensor("rows_banks", [P, 2, 512], F32))
        psH = ctx.enter_context(nc.psum_tensor("hidden_banks", [P, 3, 512], F32))
        psY = ctx.enter_context(nc.psum_tensor("out_banks", [P, 2, 512], F32))
        psR = ctx.enter_context(nc.psum_tensor("rank_bank", [P, 512], F32))
        HB = 3
        ld_ident, ld_w2, ranked, bank_read = (sem(n) for n in ("e_ld_ident", "ld_w2", "ranked", "rank_bank_read"))
        ld_w1, ld_xe = [sem(f"ld_w1_{u}") for u in range(2)], [sem(f"ld_xe_{u}") for u in range(2)]
        w1_hi_done, w1_split, w2_hi_done, w2_split = (sem(n) for n in ("w1_hi_done", "w1_split", "w2_hi_done", "w2_split"))
        rows_full, rows_hi, rows_split = sem("rows_full"), sem("rows_hi"), sem("rows_split")
        hidden_full, gelu_done, hidden_hi, hidden_split = (sem(n) for n in ("hidden_full", "gelu_done", "hidden_hi", "hidden_split"))
        out_full, out_copied, st_ye = (sem(n) for n in ("out_full", "out_copied", "st_ye"))
        ld_x2 = [sem(f"r_ld_x2_{b}") for b in range(B)]
        block = ctx.enter_context(nc.Block())

        def over_experts(eng, body):
            body(0, 0, 0)
            with eng.Fori(0, NE // 2 - 1) as j:
                body(j * 2 + 1, 1, j)
                body(j * 2 + 2, 0, j + 1)
            body(NE - 1, 1, NE // 2 - 1)

        def is_expert(e, n):
            return isinstance(e, int) and e == n

        @block.sync
        def _(sp):
            def load_w1(e, u):
                sp.dma_start(w1s[:, u], a["w1"][e].rearrange("(k p) f -> p k f", p=P)).then_inc(ld_w1[u], 16)

            def load_w2(e):
                sp.dma_start(w2s[:, :, :], a["w2"][e].rearrange("(f p) d -> p f d", p=P)).then_inc(ld_w2, 16)

            def load_rows(e, u):
                sp.dma_start(xe[:, u, 0:2, :], a["xde"][e][0:2 * P].rearrange("(t p) d -> p t d", p=P)).then_inc(ld_xe[u], 16)
                sp.dma_start(xe[0:CAP - 2 * P, u, 2, :], a["xde"][e][2 * P:CAP]).then_inc(ld_xe[u], 16)

            def load_x2(b):
                sp.dma_start(x2r[:, b * NT:(b + 1) * NT, :],
                             a["x2d"][b].rearrange("(t p) d -> p t d", p=P)).then_inc(ld_x2[b], 16)

            load_x2(B - 1)
            sp.dma_start(identf[:, :], a["identf"]).then_inc(ld_ident, 16)
            load_w1(0, 0)
            sp.wait_ge(routing.sent, 16 * TT)
            load_rows(0, 0)
            load_w1(1, 1)
            load_w2(0)
            load_rows(1, 1)
            for b in range(B - 1):
                load_x2(b)
            with sp.Fori(0, NE // 2 - 1) as j:
                for u in range(2):
                    e = j * 2 + u
                    sp.wait_ge(w1_split, (e + 1) * KD)
                    load_w1(e + 2, u)
                    sp.wait_ge(rows_full, (e + 1) * 2)
                    load_rows(e + 2, u)
                    sp.wait_ge(w2_split, (e + 1) * 2)
                    load_w2(e + 1)
            sp.wait_ge(w2_split, (NE - 1) * 2)
            load_w2(NE - 1)

        @block.scalar
        def _(act):
            def w1_hi(e, u, half):
                act.wait_ge(ld_w1[u], (half + 1) * 16)
                for k in range(KD):
                    nc.scalar.copy(w1h[:, u, k, :], w1s[:, u, k, :]).then_inc(w1_hi_done, 1)

            def w2_hi(e, u):
                act.wait_ge(ld_w2, (e + 1) * 16)
                for n in range(2):
                    f = slice(n * FC // 2, (n + 1) * FC // 2)
                    nc.scalar.copy(w2h[:, u, f, :], w2s[:, f, :]).then_inc(w2_hi_done, 1)

            def xe_high(e):
                for k in range(KD):
                    act.wait_ge(rows_full, e * 2 + k + 1)
                    nc.scalar.copy(xe_hi[:, k, :], psX[:, k, 0:CAP]).then_inc(rows_hi, 1)

            def body(e, u, half):
                for f in range(FC):
                    act.wait_ge(hidden_full, e * FC + f + 1)
                    if not is_expert(e, 0):
                        act.wait_ge(hidden_split, (e - 1) * FC + f + 1)
                    nc.scalar.activation(hid[:, f, :], psH[:, f % HB, 0:CAP], ACT.Gelu_apprx_tanh).then_inc(gelu_done, 1)
                if not is_expert(e, NE - 1):
                    xe_high(e + 1)
                    w1_hi(e + 1, 1 - u, half + u)
                w2_hi(e, u)

            routing.exponentials(nc, act, B - 1)
            w1_hi(0, 0, 0)
            xe_high(0)
            over_experts(act, body)

        @block.vector
        def _(dve):
            def w1_lo(e, u, k):
                dve.wait_ge(w1_hi_done, e * KD + k + 1)
                nc.vector.tensor_tensor(w1l[:, u, k, :], w1s[:, u, k, :], w1h[:, u, k, :].bitcast(F32),
                                        ALU.subtract).then_inc(w1_split, 1)

            def w2_lo(e, u, n):
                f = slice(n * FC // 2, (n + 1) * FC // 2)
                dve.wait_ge(w2_hi_done, e * 2 + n + 1)
                nc.vector.tensor_tensor(w2l[:, u, f, :], w2s[:, f, :], w2h[:, u, f, :].bitcast(F32),
                                        ALU.subtract).then_inc(w2_split, 1)

            def xe_low(e):
                for k in range(KD):
                    dve.wait_ge(rows_hi, e * 2 + k + 1)
                    nc.vector.tensor_tensor(xe_lo[:, k, :], psX[:, k, 0:CAP], xe_hi[:, k, :].bitcast(F32),
                                            ALU.subtract).then_inc(rows_split, 1)

            def copy_out(e, u, t):
                dve.wait_ge(out_full, e * 3 + t + 1)
                if t == 0 and not is_expert(e, 0):
                    dve.wait_ge(st_ye, e * 32)
                nc.vector.tensor_copy(ye[:, t, :], psY[:, (u + t) % 2, 0:D]).then_inc(out_copied, 1)

            def body(e, u, half):
                first, last = is_expert(e, 0), is_expert(e, NE - 1)
                for f in range(FC):
                    dve.wait_ge(gelu_done, e * FC + f + 1)
                    nc.vector.tensor_copy(hid_hi[:, u, f, :], hid[:, f, :]).then_inc(hidden_hi, 1)
                    dve.wait_ge(hidden_hi, e * FC + f + 1)
                    nc.vector.tensor_tensor(hid_lo[:, u, f, :], hid[:, f, :], hid_hi[:, u, f, :].bitcast(F32),
                                            ALU.subtract).then_inc(hidden_split, 1)
                if not last:
                    xe_low(e + 1)
                for n in range(3):
                    if n < KD and not last:
                        w1_lo(e + 1, 1 - u, n)
                    if n:
                        w2_lo(e, u, n - 1)
                    if not first:
                        copy_out(e - 1, 1 - u, n)

            routing.compare(nc, dve, B - 1)
            routing.choose(nc, dve)
            dve.wait_ge(ranked, 1)
            routing.rank_tokens(nc, dve, B - 1, psR, bank_read)
            routing.find_slots(nc, dve, B - 1)
            routing.weigh(nc, dve, B - 1)
            for k in range(KD):
                w1_lo(0, 0, k)
            xe_low(0)
            over_experts(dve, body)
            for t in range(3):
                copy_out(NE - 1, 1, t)

        @block.gpsimd
        def _(pool):
            pool.wait_ge(ld_x2[B - 1], 16)
            routing.send(nc, pool, B - 1, a["xd"], x2r[:, (B - 1) * NT:, :])
            with pool.Fori(0, NE) as e:
                pool.wait_ge(out_copied, (e + 1) * 3 + 2)
                pool.dma_start(a["yde"][e][0:2 * P].rearrange("(t p) d -> p t d", p=P), ye[:, 0:2, :]).then_inc(st_ye, 16)
                pool.dma_start(a["yde"][e][2 * P:CAP], ye[3 * P - CAP:P, 2, :]).then_inc(st_ye, 16)
            pool.wait_ge(st_ye, NE * 32)
            for b in range(B):
                pool.wait_ge(ld_x2[b], 16)

        @block.tensor
        def _(pe):
            def rows(e, u, half):
                pe.wait_ge(ld_xe[u], (half + 1) * 32)
                if not is_expert(e, 0):
                    pe.wait_ge(rows_split, e * 2)
                for k in range(KD):
                    for t, (at, n) in enumerate(TOK_TILES):
                        mm = pe.transpose(psX[:, k, at:at + n], xe[0:n, u, t, k * P:(k + 1) * P], identf[0:n, 0:n])
                    mm.then_inc(rows_full, 1)

            def second(e, u):
                pe.wait_ge(w2_split, (e + 1) * 2)
                pe.wait_ge(hidden_split, (e + 1) * FC)
                for t, at in enumerate((0, P, CAP - P)):
                    n = (u + t) % 2
                    pe.wait_ge(out_copied, e * 3 + t + 1)
                    accumulate(pe, psY[:, n, 0:D], exact_products(
                        [((hid_hi[:, u, f, at:at + P], hid_lo[:, u, f, at:at + P]), (w2h[:, u, f, :], w2l[:, u, f, :]))
                         for f in range(FC)])).then_inc(out_full, 1)

            def body(e, u, half):
                pe.wait_ge(w1_split, (e + 1) * KD)
                pe.wait_ge(rows_split, (e + 1) * 2)
                for f in range(FC):
                    w = slice(f * P, (f + 1) * P)
                    if not (is_expert(e, 0) and f < HB):
                        pe.wait_ge(gelu_done, e * FC + (f + 1 - HB if f >= HB else 0))
                    mm = accumulate(pe, psH[:, f % HB, 0:CAP], exact_products(
                        [((w1h[:, u, k, w], w1l[:, u, k, w]), (xe_hi[:, k, :], xe_lo[:, k, :])) for k in range(KD)]))
                    mm.then_inc(hidden_full, 1)
                if not is_expert(e, NE - 1):
                    rows(e + 1, 1 - u, half + u)
                if not is_expert(e, 0):
                    second(e - 1, 1 - u)

            routing.ranking(nc, pe, B - 1, psR, ranked)
            pe.sem_inc(out_copied, 2)
            pe.wait_ge(ld_ident, 16)
            rows(0, 0, 0)
            over_experts(pe, body)
            second(NE - 1, 1)


def combine(nc, a, routing, x2r):
    with ExitStack() as ctx:
        def sem(name):
            return ctx.enter_context(nc.semaphore(name))

        def sb(name, shape, dt=F32):
            return ctx.enter_context(nc.sbuf_tensor(name, list(shape), dt))

        ENDS, AHEAD = [8, 16, 24, 28, 32], 5
        assert ENDS[-1] == TT
        groups = [slice(a0, a1) for a0, a1 in zip([0] + ENDS, ENDS)]
        got = sb("got", [P, TT, D])
        mhalf = sb("minus_half_c", [P, 1])
        stats, mv = sb("stats_c", [P, TT, 6]), sb("mean_var_c", [P, TT, 2])
        less, vpe, rstd, shift = (sb(n, [P, TT]) for n in ("minus_mean", "var_eps_c", "rstd_c", "shift_c"))
        halves, summed, stats_done, stats_ready, less_done, var_ready, rstd_ready, shift_ready, normed, st_out = (sem(n) for n in (
            "half_set", "summed", "stats_done", "c_stats_ready", "less_done", "c_var_ready", "c_rstd_ready", "shift_ready", "normed", "st_out"))
        landed = [sem(f"landed{n}") for n in range(TT)]
        block = ctx.enter_context(nc.Block())

        @block.gpsimd
        def _(pool):
            nc.gpsimd.memset(mhalf[:, :], -0.5).then_inc(halves, 1)
            pool.wait_ge(halves, 1)
            for t in range(1, TT + AHEAD + 1):
                if t <= TT:
                    nc.gpsimd.indirect_dma_start(got[:, t - 1, :], None, a["yd"],
                                                 bass.IndirectOffsetOnAxis(ap=routing.slot_g[:, t - 1:t], axis=0),
                                                 ).then_inc(landed[t - 1], 16)
                if t - AHEAD in ENDS:
                    n = ENDS.index(t - AHEAD)
                    s = groups[n]
                    pool.wait_ge(less_done, n + 1)
                    pool.wait_ge(var_ready, n + 1)
                    nc.gpsimd.tensor_tensor(rstd[:, s], vpe[:, s], mhalf[:, :].broadcast_to([P, s.stop - s.start]),
                                            ALU.pow).then_inc(rstd_ready, 1)
                    pool.wait_ge(rstd_ready, n + 1)
                    nc.gpsimd.tensor_tensor(shift[:, s], less[:, s], rstd[:, s], ALU.mult).then_inc(shift_ready, 1)

        @block.vector
        def _(dve):
            for t in range(TT + 2):
                if t < TT:
                    dve.wait_ge(landed[t], 16)
                    nc.vector.scalar_tensor_tensor(out=x2r[:, t, :], in0=got[:, t, :], scalar=routing.weight[:, t:t + 1],
                                                   in1=x2r[:, t, :], op0=ALU.mult, op1=ALU.add).then_inc(summed, 1)
                if 1 <= t <= TT:
                    dve.wait_ge(summed, t)
                    nc.vector.bn_stats(stats[:, t - 1, :], x2r[:, t - 1, :]).then_inc(stats_done, 1)
                if 2 <= t <= TT + 1:
                    dve.wait_ge(stats_done, t - 1)
                    nc.vector.bn_aggr(mv[:, t - 2, :], stats[:, t - 2, :]).then_inc(stats_ready, 1)
                    if t - 1 in ENDS:
                        s = groups[ENDS.index(t - 1)]
                        dve.wait_ge(stats_ready, s.stop)
                        nc.vector.tensor_scalar(less[:, s], mv[:, s, 0], -1.0, None, ALU.mult).then_inc(less_done, 1)
                        nc.vector.tensor_scalar(vpe[:, s], mv[:, s, 1], EPS, None, ALU.add).then_inc(var_ready, 1)

        @block.scalar
        def _(act):
            for t in range(TT):
                act.wait_ge(shift_ready, sum(t >= end for end in ENDS) + 1)
                nc.scalar.activation(got[:, t, :], x2r[:, t, :], ACT.Identity, bias=shift[:, t:t + 1],
                                     scale=rstd[:, t:t + 1]).then_inc(normed, 1)

        @block.sync
        def _(sp):
            for t in range(0, TT, 4):
                sp.wait_ge(normed, t + 4)
                sp.dma_start(a["out"].rearrange("(t p) d -> p t d", p=P)[:, t:t + 4, :], got[:, t:t + 4, :]).then_inc(st_out, 16)
            sp.wait_ge(st_out, 4 * TT)


def decoder_layer(nc, a):
    xd = nc.dram_tensor("dispatched_rows", (NE * CAP, D), F32)
    yd = nc.dram_tensor("expert_rows", (NE * CAP, D), F32)
    a = dict(a, xd=xd.ap(), yd=yd.ap(), x2d=nc.dram_tensor("x2_rows", (B, S, D), F32).ap(),
             xde=xd.ap().rearrange("(e c) d -> e c d", e=NE), yde=yd.ap().rearrange("(e c) d -> e c d", e=NE))
    with ExitStack() as ctx:
        routing = Routing(ctx, nc)
        attention(nc, a, routing)
        x2r = ctx.enter_context(nc.sbuf_tensor("x2_tokens", [P, TT, D], F32))
        mixture(nc, a, routing, x2r)
        combine(nc, a, routing, x2r)


def bucket(distance):
    import numpy as np
    half, exact = BUCKETS // 2, BUCKETS // 4
    far = np.abs(distance)
    step = np.log(np.maximum(far, 1).astype(np.float32) / np.float32(exact)) / np.float32(np.log(MAX_DIST / exact))
    large = np.minimum(exact + (step * np.float32(half - exact)).astype(np.int32), half - 1)
    return (distance > 0) * half + np.where(far < exact, far, large)


def constants():
    import numpy as np
    i = np.arange(P)
    r = np.arange(NCH * P).reshape(NCH, P)
    mine = (r // KP)[:, :, None] == (np.array(CHUNK_HEAD)[:, None, None] + np.arange(3))
    pad = np.zeros((64, KP), np.float32)
    pad[:, 0:KP - SK] = -1e30
    return {
        "identf": np.eye(P, dtype=np.float32),
        "causal": ((i[None, :] > i[:, None]) * -1e30).astype(np.float32),
        "before": (i[:, None] < i[None, :]).astype(np.float32),
        "iota": np.tile(np.arange(NE, dtype=np.float32), (P, 1)),
        "onehot": (bucket(KP - 1 - np.arange(HANKEL))[None, :] == np.arange(BUCKETS)[:, None]).astype(np.float32),
        "padneg": pad,
        "blk_k": (i[:, None] // HD2 == np.arange(GH)).astype(np.float32),
        "blk_v": np.ascontiguousarray(mine.transpose(1, 0, 2).reshape(P, NCH * 3).astype(np.float32)),
    }


def kernel(**inputs):
    import concourse.bacc as bacc
    import numpy as np
    from concourse.bass_utils import run_bass_kernel_spmd

    v = {k: np.asarray(x) for k, x in inputs.items()}

    def T(name):
        return np.ascontiguousarray(v[name].T)

    ctxT = np.zeros((B, D, GH, KP), np.float32)
    ctxT[:, :, :, KP - SK:] = v["ctx_1024"][:, ::-1].transpose(0, 2, 1)[:, :, None, :]
    mask = np.zeros((P, B, KP), bool)
    mask[:, :, KP - SK:] = v["mask_Bx1x1xS2_bk0"][:, 0, 0, ::-1][None]
    memz = np.zeros((2, HD1, 2, 2, HD1 + 1), np.float32)
    for h in range(H1):
        memz[h % 2, :, h // 2, h % 2, 0:HD1] = v["L0_attn_mem"][h]
        memz[h % 2, :, h // 2, h % 2, HD1:] = v["L0_attn_z"][h]
    rel = v["L0_xattn_rel_bias"].T
    arrays = {
        "x": v["x"], "xT": np.ascontiguousarray(v["x"].transpose(0, 2, 1)), "ctxT": ctxT.reshape(B, D, GK), "mask": mask,
        "WqT": T("L0_attn_Wq"), "WkT": T("L0_attn_Wk"), "WvT": T("L0_attn_Wv"), "Wo1T": T("L0_attn_Wo"),
        "bo": np.tile(v["L0_attn_bo"], (P, 1)), "betas": np.tile(v["L0_attn_betas"].reshape(1, H1), (P, 1)),
        "memz": memz.reshape(P, 2, 2, HD1 + 1),
        "Wq2T": T("L0_xattn_Wq"), "Wk2T": T("L0_xattn_Wk"), "Wv2T": T("L0_xattn_Wv"), "Wo2T": T("L0_xattn_Wo"),
        "rel": np.ascontiguousarray(np.stack([rel, np.tile(rel[BUCKETS // 2 - 1], (BUCKETS, 1))], axis=1)),
        "gateT": T("L0_ffn_gate_w"), "w1": v["L0_ffn_w1"], "w2": v["L0_ffn_w2"], **constants(),
    }
    nc = bacc.Bacc("TRN2", target_bir_lowering=False, num_devices=1)
    aps = {k: nc.dram_tensor(f"in_{k}", x.shape, mybir.dt.from_np(x.dtype), kind="ExternalInput").ap() for k, x in arrays.items()}
    aps["out"] = nc.dram_tensor("out_0", (NTOK, D), F32, kind="ExternalOutput").ap()
    decoder_layer(nc, aps)
    r = run_bass_kernel_spmd(nc, [{f"in_{k}": x for k, x in arrays.items()}], core_ids=[0])
    return r.results[0]["out_0"].reshape(B, S, D)
```
